# Optimizing a Trainium2 kernel written in Bass

```python
import numpy as np
import jax
import jax.numpy as jnp

def _softmax(x, axis=-1):
    return jax.nn.softmax(x, axis=axis)

def _gelu(x):
    return jax.nn.gelu(x, approximate=True)

def _silu(x):
    return jax.nn.silu(x)

def _sigmoid(x):
    return jax.nn.sigmoid(x)

def _layernorm(x, axis=-1, eps=1e-05):
    m = jnp.mean(x, axis=axis, keepdims=True)
    v = jnp.var(x, axis=axis, keepdims=True)
    return (x - m) / jnp.sqrt(v + eps)

def _scatter_add(tgt, idx, src, axis=0):
    return tgt.at[idx].add(src)

def _segment_sum(src, seg, n):
    return jax.ops.segment_sum(src, seg, n)
kernel_name = 'mk_early_fusion_d2_tok_img1024_r4_ce752b'

def setup_inputs(seed: int=0):
    np.random.seed(seed)
    _w = jnp.asarray

    def _rec_inputs():
        import jax
        import jax.numpy as jnp
        _rk = jax.random.key(seed)
        x = -0.000348323 + 0.999952 * jax.random.normal(jax.random.fold_in(_rk, 1), (8, 3, 96, 96), jnp.float32)
        txt = -0.000563189 + 0.999639 * jax.random.normal(jax.random.fold_in(_rk, 2), (8, 128, 256), jnp.float32)
        return (x, txt)
    x, txt = _rec_inputs()

    def _L0_tok_setup():
        import jax, jax.numpy as jnp
        import numpy as np
        from jax import lax
        PATCH = 16
        key = jax.random.key(seed)
        k1, k2 = jax.random.split(key)
        B, C, IMG, HID = (32, 3, 96, 256)
        inputs = jax.random.normal(k1, (B, C, IMG, IMG), dtype=jnp.float32)
        flat = C * PATCH * PATCH
        W = jax.random.normal(k2, (flat, HID), dtype=jnp.float32) / np.sqrt(flat)
        return {'inputs': inputs, 'W': W}
    _L0_tok_all = _L0_tok_setup()
    _L0_tok_in = {k: v for k, v in _L0_tok_all.items() if k in ('W',)}
    del _L0_tok_all

    def _L0_attn_setup():
        import jax, jax.numpy as jnp
        import numpy as np
        B, T, D, H = (4, 512, 256, 16)
        E = D // H
        DH = D // 4
        key = jax.random.key(seed)
        ks = jax.random.split(key, 9)
        s = D ** (-0.5)
        return {'x': jax.random.normal(ks[0], (B, T, D), jnp.float32), 'q_w': jax.random.normal(ks[1], (D, D), jnp.float32) * s, 'k_w': jax.random.normal(ks[2], (D, D), jnp.float32) * s, 'v_w': jax.random.normal(ks[3], (D, D), jnp.float32) * s, 'o_w': jax.random.normal(ks[4], (D, D), jnp.float32) * s, 'cs_w1': jax.random.normal(ks[5], (DH, D), jnp.float32) * s, 'cs_b1': jnp.zeros((DH,), jnp.float32), 'cs_w2': jax.random.normal(ks[6], (H, DH), jnp.float32) * DH ** (-0.5), 'cs_b2': jnp.zeros((H,), jnp.float32), 'decay_params': jax.random.normal(ks[7], (H, E), jnp.float32) + 3.0}
    _L0_attn_all = _L0_attn_setup()
    _L0_attn_in = {k: v for k, v in _L0_attn_all.items() if k in ('q_w', 'k_w', 'v_w', 'o_w', 'cs_w1', 'cs_b1', 'cs_w2', 'cs_b2', 'decay_params')}
    del _L0_attn_all

    def _L0_ffn_setup():
        import jax, jax.numpy as jnp
        import numpy as np
        B, T, D = (4, 1024, 256)
        E = 8
        TOP_K = 2
        FFN = 768
        HALF = FFN // 2

        def _kaiming_uniform(key, shape, fan_in):
            bound = 1.0 / np.sqrt(fan_in)
            return jax.random.uniform(key, shape, jnp.float32, -bound, bound)
        key = jax.random.key(seed)
        ks = jax.random.split(key, 7)
        x = jax.random.normal(ks[0], (B, T, D), jnp.float32)
        gate_w = _kaiming_uniform(ks[1], (E, D), D) * 0.01
        w_up = _kaiming_uniform(ks[2], (E, FFN, D), D)
        w_down = _kaiming_uniform(ks[3], (E, D, HALF), HALF)
        sg_gate = _kaiming_uniform(ks[4], (HALF, D), D)
        sg_up = _kaiming_uniform(ks[5], (HALF, D), D)
        sg_down = _kaiming_uniform(ks[6], (D, HALF), HALF)
        return {'x': x, 'gate_w': gate_w, 'w_up': w_up, 'w_down': w_down, 'sg_gate': sg_gate, 'sg_up': sg_up, 'sg_down': sg_down}
    _L0_ffn_all = _L0_ffn_setup()
    _L0_ffn_in = {k: v for k, v in _L0_ffn_all.items() if k in ('gate_w', 'w_up', 'w_down', 'sg_gate', 'sg_up', 'sg_down')}
    del _L0_ffn_all

    def _L1_attn_setup():
        import jax, jax.numpy as jnp
        import numpy as np
        D_MODEL = 256
        NHEAD = 16
        HEAD_DIM = D_MODEL // NHEAD
        SCALE = float(np.sqrt(HEAD_DIM))
        key = jax.random.key(seed)
        ks = jax.random.split(key, 6)
        B, T = (2, 512)
        x = jax.random.normal(ks[0], (B, T, D_MODEL), dtype=jnp.float32)
        s = 1.0 / np.sqrt(D_MODEL)
        qkv_w = jax.random.uniform(ks[1], (3 * D_MODEL, D_MODEL), jnp.float32, -s, s)
        qkv_b = jax.random.uniform(ks[2], (3 * D_MODEL,), jnp.float32, -s, s)
        out_w = jax.random.uniform(ks[3], (D_MODEL, D_MODEL), jnp.float32, -s, s)
        out_b = jax.random.uniform(ks[4], (D_MODEL,), jnp.float32, -s, s)
        decay_alpha = jnp.full((NHEAD,), 0.1, dtype=jnp.float32)
        return {'x': x, 'qkv_w': qkv_w, 'qkv_b': qkv_b, 'out_w': out_w, 'out_b': out_b, 'decay_alpha': decay_alpha}
    _L1_attn_all = _L1_attn_setup()
    _L1_attn_in = {k: v for k, v in _L1_attn_all.items() if k in ('qkv_w', 'qkv_b', 'out_w', 'out_b', 'decay_alpha')}
    del _L1_attn_all

    def _L1_ffn_setup():
        import jax, jax.numpy as jnp
        import numpy as np
        NUM_EXPERTS = 8
        TOP_K = 2
        key = jax.random.key(seed)
        ks = jax.random.split(key, 4)
        B, S, H, F = (4, 1024, 256, 1024)
        x = jax.random.normal(ks[0], (B, S, H), dtype=jnp.float32)
        router_w = jax.random.normal(ks[1], (H, NUM_EXPERTS), dtype=jnp.float32) * 0.02
        w1 = jax.random.normal(ks[2], (H, F), dtype=jnp.float32) * 0.02
        b1 = jnp.zeros((F,), dtype=jnp.float32)
        w2 = jax.random.normal(ks[3], (F, H), dtype=jnp.float32) * 0.02
        b2 = jnp.zeros((H,), dtype=jnp.float32)
        return {'x': x, 'router_w': router_w, 'w1': w1, 'b1': b1, 'w2': w2, 'b2': b2}
    _L1_ffn_all = _L1_ffn_setup()
    _L1_ffn_in = {k: v for k, v in _L1_ffn_all.items() if k in ('router_w', 'w1', 'b1', 'w2', 'b2')}
    del _L1_ffn_all
    return {'x': x, 'txt': txt, 'L0_tok_W': _L0_tok_in['W'], 'L0_attn_q_w': _L0_attn_in['q_w'], 'L0_attn_k_w': _L0_attn_in['k_w'], 'L0_attn_v_w': _L0_attn_in['v_w'], 'L0_attn_o_w': _L0_attn_in['o_w'], 'L0_attn_cs_w1': _L0_attn_in['cs_w1'], 'L0_attn_cs_b1': _L0_attn_in['cs_b1'], 'L0_attn_cs_w2': _L0_attn_in['cs_w2'], 'L0_attn_cs_b2': _L0_attn_in['cs_b2'], 'L0_attn_decay_params': _L0_attn_in['decay_params'], 'L0_ffn_gate_w': _L0_ffn_in['gate_w'], 'L0_ffn_w_up': _L0_ffn_in['w_up'], 'L0_ffn_w_down': _L0_ffn_in['w_down'], 'L0_ffn_sg_gate': _L0_ffn_in['sg_gate'], 'L0_ffn_sg_up': _L0_ffn_in['sg_up'], 'L0_ffn_sg_down': _L0_ffn_in['sg_down'], 'L1_attn_qkv_w': _L1_attn_in['qkv_w'], 'L1_attn_qkv_b': _L1_attn_in['qkv_b'], 'L1_attn_out_w': _L1_attn_in['out_w'], 'L1_attn_out_b': _L1_attn_in['out_b'], 'L1_attn_decay_alpha': _L1_attn_in['decay_alpha'], 'L1_ffn_router_w': _L1_ffn_in['router_w'], 'L1_ffn_w1': _L1_ffn_in['w1'], 'L1_ffn_b1': _L1_ffn_in['b1'], 'L1_ffn_w2': _L1_ffn_in['w2'], 'L1_ffn_b2': _L1_ffn_in['b2']}

def reference(x, txt, L0_tok_W, L0_attn_q_w, L0_attn_k_w, L0_attn_v_w, L0_attn_o_w, L0_attn_cs_w1, L0_attn_cs_b1, L0_attn_cs_w2, L0_attn_cs_b2, L0_attn_decay_params, L0_ffn_gate_w, L0_ffn_w_up, L0_ffn_w_down, L0_ffn_sg_gate, L0_ffn_sg_up, L0_ffn_sg_down, L1_attn_qkv_w, L1_attn_qkv_b, L1_attn_out_w, L1_attn_out_b, L1_attn_decay_alpha, L1_ffn_router_w, L1_ffn_w1, L1_ffn_b1, L1_ffn_w2, L1_ffn_b2):
    import jax
    import jax.numpy as jnp

    def _L0_tok_ref(inputs, W):
        import jax, jax.numpy as jnp
        import numpy as np
        from jax import lax
        PATCH = 16
        B, C, H, Wimg = inputs.shape
        patches = lax.conv_general_dilated_patches(inputs, filter_shape=[PATCH, PATCH], window_strides=[PATCH, PATCH], padding='VALID', dimension_numbers=('NCHW', 'HWIO', 'NCHW'))
        patches = patches.reshape(B, -1, C * PATCH * PATCH)
        return jnp.einsum('bnf,fh->bnh', patches, W)

    def _L0_attn_ref(x, q_w, k_w, v_w, o_w, cs_w1, cs_b1, cs_w2, cs_b2, decay_params):
        import jax, jax.numpy as jnp
        import numpy as np
        B, T, D, H = (4, 512, 256, 16)
        E = D // H
        DH = D // 4
        Bx, Tx, Dx = x.shape
        q = (x @ q_w.T).reshape(Bx, Tx, H, E)
        k = (x @ k_w.T).reshape(Bx, Tx, H, E)
        v = (x @ v_w.T).reshape(Bx, Tx, H, E)
        lc = jax.nn.sigmoid(jnp.tanh(x @ cs_w1.T + cs_b1) @ cs_w2.T + cs_b2)
        base = jax.nn.sigmoid(decay_params)[None, None]
        lam = jnp.clip(base * (1.0 + 0.2 * lc[..., None]), 0.0, 0.9995)

        def step(state, inp):
            qt, kt, vt, dt = inp
            state = state * dt[..., None] + kt[..., None] * vt[:, :, None, :]
            out_t = jnp.einsum('bhe,bhef->bhf', qt, state)
            return (state, out_t)
        init = jnp.zeros((Bx, H, E, E), x.dtype)
        xs = (jnp.swapaxes(q, 0, 1), jnp.swapaxes(k, 0, 1), jnp.swapaxes(v, 0, 1), jnp.swapaxes(lam, 0, 1))
        _, ys = jax.lax.scan(step, init, xs)
        y = jnp.swapaxes(ys, 0, 1).reshape(Bx, Tx, Dx)
        return y @ o_w.T

    def _L0_ffn_ref(x, gate_w, w_up, w_down, sg_gate, sg_up, sg_down):
        import jax, jax.numpy as jnp
        import numpy as np
        B, T, D = (4, 1024, 256)
        E = 8
        TOP_K = 2
        FFN = 768
        HALF = FFN // 2

        def _kaiming_uniform(key, shape, fan_in):
            bound = 1.0 / np.sqrt(fan_in)
            return jax.random.uniform(key, shape, jnp.float32, -bound, bound)
        b, t, d = x.shape
        xf = x.reshape(b * t, d)
        N = xf.shape[0]
        logits = xf @ gate_w.T
        topk_logits, topk_idx = jax.lax.top_k(logits, TOP_K)
        topk_w = jax.nn.softmax(topk_logits.astype(jnp.float32), axis=-1).astype(x.dtype)
        comb = jnp.zeros((N, E), x.dtype).at[jnp.arange(N)[:, None], topk_idx].add(topk_w)
        wg = w_up[:, :HALF, :]
        wu = w_up[:, HALF:, :]
        out = jnp.zeros_like(xf)
        for e in range(E):
            g = xf @ wg[e].T
            u = xf @ wu[e].T
            y = jax.nn.silu(g) * u @ w_down[e].T
            out = out + comb[:, e:e + 1] * y
        shared = jax.nn.silu(xf @ sg_gate.T) * (xf @ sg_up.T) @ sg_down.T
        return (shared + out).reshape(b, t, d)

    def _L1_attn_ref(x, qkv_w, qkv_b, out_w, out_b, decay_alpha):
        import jax, jax.numpy as jnp
        import numpy as np
        D_MODEL = 256
        NHEAD = 16
        HEAD_DIM = D_MODEL // NHEAD
        SCALE = float(np.sqrt(HEAD_DIM))
        B, T, D = x.shape
        qkv = x @ qkv_w.T + qkv_b
        qkv = qkv.reshape(B, T, 3, NHEAD, HEAD_DIM).transpose(2, 0, 3, 1, 4)
        q, k, v = (qkv[0], qkv[1], qkv[2])
        logits = jnp.einsum('bhqd,bhkd->bhqk', q, k) / SCALE
        pos = jnp.arange(T, dtype=jnp.float32)
        dist = jnp.abs(pos[None, :] - pos[:, None])
        alpha = jax.nn.softplus(decay_alpha)
        logits = logits - alpha[:, None, None] * dist[None]
        attn = jax.nn.softmax(logits, axis=-1)
        out = jnp.einsum('bhqk,bhkd->bhqd', attn, v)
        out = out.transpose(0, 2, 1, 3).reshape(B, T, D)
        out = out @ out_w.T + out_b
        return out

    def _L1_ffn_ref(x, router_w, w1, b1, w2, b2):
        import jax, jax.numpy as jnp
        import numpy as np
        NUM_EXPERTS = 8
        TOP_K = 2
        B, S, H = x.shape
        xt = x.reshape(-1, H)
        router_logits = jnp.matmul(xt, router_w)
        router_probs = jax.nn.softmax(router_logits, axis=-1)
        top_k_probs, top_k_indices = jax.lax.top_k(router_probs, TOP_K)
        top_k_probs = top_k_probs / jnp.sum(top_k_probs, axis=-1, keepdims=True)
        one_hot = jax.nn.one_hot(top_k_indices, NUM_EXPERTS, dtype=xt.dtype)
        combine = jnp.einsum('tk,tke->te', top_k_probs, one_hot)
        expert_out = jnp.matmul(jax.nn.gelu(jnp.matmul(xt, w1) + b1), w2) + b2
        out = expert_out * jnp.sum(combine, axis=-1, keepdims=True)
        return out.reshape(B, S, H)
    h = _L0_tok_ref(x, L0_tok_W)
    h = jnp.concatenate([h, txt], axis=1)
    h = h + _L0_attn_ref(_layernorm(h, axis=-1), L0_attn_q_w, L0_attn_k_w, L0_attn_v_w, L0_attn_o_w, L0_attn_cs_w1, L0_attn_cs_b1, L0_attn_cs_w2, L0_attn_cs_b2, L0_attn_decay_params)
    h = h + _L0_ffn_ref(_layernorm(h, axis=-1), L0_ffn_gate_w, L0_ffn_w_up, L0_ffn_w_down, L0_ffn_sg_gate, L0_ffn_sg_up, L0_ffn_sg_down)
    h = h + _L1_attn_ref(_layernorm(h, axis=-1), L1_attn_qkv_w, L1_attn_qkv_b, L1_attn_out_w, L1_attn_out_b, L1_attn_decay_alpha)
    h = h + _L1_ffn_ref(_layernorm(h, axis=-1), L1_ffn_router_w, L1_ffn_w1, L1_ffn_b1, L1_ffn_w2, L1_ffn_b2)
    return h

_drawn_inputs = setup_inputs


def setup_inputs(seed=0):
    import zlib

    import numpy as np

    out = dict(_drawn_inputs(seed))
    spreads = {'L0_attn_cs_b1': (0.0, 0.539),
     'L0_attn_cs_b2': (0.0, 0.1),
     'L1_attn_decay_alpha': (0.10000000149011612, 0.6),
     'L1_ffn_b1': (0.0, 0.8),
     'L1_ffn_b2': (0.0, 2.0)}
    factors = {'L0_ffn_gate_w': 8.0,
     'L0_ffn_w_up': 8.0,
     'L0_ffn_w_down': 8.0,
     'L0_ffn_sg_gate': 8.0,
     'L0_ffn_sg_up': 8.0,
     'L0_ffn_sg_down': 8.0,
     'L1_attn_qkv_w': 8.0,
     'L1_attn_qkv_b': 8.0,
     'L1_attn_out_w': 8.0,
     'L1_attn_out_b': 64.0,
     'L1_ffn_router_w': 64.0,
     'L1_ffn_w1': 8.0,
     'L1_ffn_w2': 8.0}
    for name, (base, spread) in spreads.items():
        noise = np.random.default_rng([zlib.crc32(name.encode()), seed]).standard_normal(out[name].shape)
        drawn = base * np.exp(spread * noise) if base else spread * noise
        out[name] = jnp.asarray(drawn.astype(out[name].dtype))
    for name, factor in factors.items():
        out[name] = (out[name] * factor).astype(out[name].dtype)
    return out
```

```python
import concourse.bass as bass
from concourse import mybir
from contextlib import ExitStack

B, T, D = 8, 164, 256
IMG, TXT = 36, 128
P = 128
KC = D // P
NT = 2
TT = T // NT
HEADS, HD = 16, 16
HH = HEADS // KC
PC = 6
CH = 41
NCH = T // CH
COFF = [CH * r * (r + 1) // 2 for r in range(NCH + 1)]
KW = COFF[NCH]
MIDC = CH // 2
BT = B * NT
LAM_MIN, LAM_MAX = 0.02, 0.9995
NE, TOPK, HALF = 8, 2, 384
FC = HALF // P
FF = 1024
FFC = FF // P
GR = 4
GN = B * T // GR
SLOTS = P
RT = (TOPK * B * T + NE * (SLOTS - 1)) // SLOTS
SCALE = 4.0
EPS = 1e-5


class Chain:

    def __init__(self, eng, sem, base=0):
        self.eng, self.sem, self.base, self.n = eng, sem, base, 0

    def add(self, ins):
        ins.then_inc(self.sem, 1)
        self.n += 1

    def wait(self):
        self.eng.wait_ge(self.sem, self.base + self.n)

    def __call__(self, ins):
        self.add(ins)
        self.wait()

    def step(self, n):
        assert self.n == n, (self.n, n)


def early_fusion_kernel(nc, a, out):
    f32, i32, u32 = mybir.dt.float32, mybir.dt.int32, mybir.dt.uint32
    ALU = mybir.AluOpType
    ACT = mybir.ActivationFunctionType

    ctx = ExitStack()
    with ctx:
        def sb(name, shape, dt=f32):
            return ctx.enter_context(nc.sbuf_tensor(name, shape, dt))

        def sem(name):
            return ctx.enter_context(nc.semaphore(name))

        bank = [ctx.enter_context(nc.psum_tensor(f"bank{i}", [P, 512], f32)) for i in range(8)]

        h = sb("h", [TT, B * NT * D])
        h4 = h[:, :].rearrange("p (b t d) -> p b t d", b=B, t=NT)
        ident = sb("ident", [P, P])
        hmask = sb("hmask", [P, HH])
        cmask = sb("cmask", [TT, 2, CH], i32)
        ones = sb("ones", [P, T])
        EPSC = sb("eps_column", [P, 1])
        tok = sb("tok", [3 * IMG, 3, D])
        wq = sb("wq", [P, KC, D])
        wk = sb("wk", [P, KC, D])
        wv = sb("wv", [P, KC, D])
        wo = sb("wo", [P, KC, D])
        cw1 = sb("cw1", [P, KC, 64])
        cb1 = sb("cb1", [64, 1])
        cw2 = sb("cw2", [64, D])
        cb2 = sb("cb2", [P, KC])
        dec = sb("dec", [P, KC])
        base = sb("base", [P, KC])
        base02 = sb("base02", [P, KC])
        eup = sb("eup", [P, KC, NE * 2 * HALF])
        flat = eup[:, :, :].rearrange("p c n -> p (c n)")
        used = [0]

        def carve(*shape):
            n = 1
            for x in shape:
                n *= x
            v = flat[:, used[0]:used[0] + n]
            used[0] += n
            assert used[0] <= KC * NE * 2 * HALF
            if len(shape) == 2:
                v = v.rearrange("p (a b) -> p a b", a=shape[0])
            elif len(shape) == 3:
                v = v.rearrange("p (a b c) -> p a b c", a=shape[0], b=shape[1])
            return v

        st = sb("st", [TT, NT * 6])
        mv = sb("mv", [TT, NT, 2])
        lnv = sb("lnv", [TT, NT])
        rstd = sb("rstd", [TT, NT])
        xn = sb("xn", [TT, NT, D])
        xnT = sb("xnT", [P, KC, T])
        th = sb("th", [64, T])
        lc = carve(KC, T)
        lam = carve(KC, T)
        lnlam = carve(KC, T)
        G = carve(KC, T)
        dq = carve(KC * T)
        dk = carve(KC, KW)
        eq = carve(KC * T)
        ek = carve(KC, KW)
        ksb = carve(KC, T)
        qe = carve(KC, T)
        kr = [carve(KC, KW) for i in range(2)]
        qb = [sb(f"qb{i}", [P, KC, HH, T]) for i in range(2)]
        spare = [qb[i][:, :, :, :].rearrange("p c h t -> p (c h t)") for i in range(2)]
        xp = spare[0][:, 0:PC * B * IMG].rearrange("p (c n) -> p c n", c=PC)
        tokw = spare[1][:, 0:PC * D].rearrange("p (c n) -> p c n", c=PC)
        sgate = spare[0][:, 0:FC * GN].rearrange("p (j n) -> p j n", j=FC)
        shid = [spare[i][:, FC * GN:2 * FC * GN].rearrange("p (j n) -> p j n", j=FC) for i in range(2)]
        vz = [[sb(f"vz{i}_{par}", [P, NT, HEADS // 2, 2, HD]) for par in range(2)] for i in range(2)]
        asb = [carve(NT, HH, T) for i in range(2)]
        yT = sb("yT", [P, KC, T])

        shared_w = sb("shared_w", [P, KC * 2 * HALF + FC * D])
        sup = shared_w[:, 0:KC * 2 * HALF].rearrange("p (c n) -> p c n", c=KC)
        sdn = shared_w[:, KC * 2 * HALF:].rearrange("p (j n) -> p j n", j=FC)
        edn = sb("edn", [P, FC, NE * D])
        gw = sb("gw", [P, KC, NE])
        st2 = sb("st2", [TT, NT * 6])
        mv2 = sb("mv2", [TT, NT, 2])
        lnv2 = sb("lnv2", [TT, NT])
        rstd2 = sb("rstd2", [TT, NT])
        x2s = sb("x2s", [TT, NT, D])
        x2Ts = sb("x2Ts", [P, KC, T])
        x2w = sb("x2w", [P, BT * D])
        x2 = x2w[0:TT, :]
        w1 = x2w[:, 0:KC * FF].rearrange("p (c n) -> p c n", c=KC)
        w2 = x2w[:, KC * FF:KC * FF + FFC * D].rearrange("p (j n) -> p j n", j=FFC)
        x2T = sb("x2T", [P, KC, B * T])
        tri = sb("tri", [TT, TT])
        rc = sb("rc", [TT, BT * NE + BT * NE + RT * NE + NE])
        desc = rc[:, 0:BT * NE].rearrange("p (i e) -> p i e", e=NE)
        fresh = rc[:, BT * NE:2 * BT * NE]
        tileno = rc[:, 2 * BT * NE:2 * BT * NE + RT * NE].rearrange("p (j e) -> p j e", e=NE)
        lg = sb("lg", [TT, BT * NE])
        rb = sb("rb", [TT, 12, BT * NE])
        rs = sb("rs", [TT, 8, BT])
        r8 = sb("r8", [TT, 6, NE])
        r8i = sb("r8i", [TT, 2, NE], i32)
        slotf = sb("slotf", [TT, TOPK, BT])
        slot = sb("slot", [TT, TOPK, BT], u32)
        gatew = sb("gatew", [TT, TOPK, BT])
        texp = sb("texp", [TT, RT * NE])
        texpf = sb("texpf", [TT, RT])
        texpi = sb("texpi", [TT, RT], i32)
        zero = x2T[:, :, :].rearrange("p c n -> p (c n)")[:, 0:1024]
        xg = [sb(f"xg{i}", [P, D]) for i in range(2)]
        xgT = [sb(f"xgT{i}", [P, KC, P]) for i in range(2)]
        rg = sb("rg", [P, HALF])
        rh = [sb(f"rh{i}", [P, HALF]) for i in range(2)]
        rhT = sb("rhT", [P, FC, P])
        ry = [sb(f"ry{i}", [P, D]) for i in range(2)]
        yg = [shared_w[0:TT, i * NT * TOPK * D:(i + 1) * NT * TOPK * D].rearrange("p (t k d) -> p t k d", t=NT, k=TOPK) for i in range(2)]
        used[0] = 0
        pT = [carve(NT, HH, T) for i in range(2)]
        ring = [carve(3, T) for i in range(4)]
        q1 = [carve(KC, T) for i in range(2)]
        ksb1 = carve(KC, T)
        rbs = carve(KC, T)
        rspread = carve(NT, D)
        hid = [carve(FFC, GN)]
        ednf = edn[:, :, :].rearrange("p j n -> p (j n)")
        kb = [ednf[:, i * KC * HH * T:(i + 1) * KC * HH * T].rearrange("p (c h t) -> p c h t", c=KC, h=HH) for i in range(2)]
        hid.append(ednf[:, 0:FFC * GN].rearrange("p (j n) -> p j n", j=FFC))
        fade = [spare[i][0:TT, :].rearrange("p (h t) -> p h t", h=HEADS) for i in range(2)]
        dist = sb("dist", [TT, NT, T])
        arow = sb("arow", [TT, HEADS])
        aabs = sb("aabs", [TT, 2, HEADS])
        alpha = sb("alpha", [TT, HEADS])
        rows1 = sb("rows1", [TT, 3, D])
        qkb = sb("qkb", [P, 2, KC])
        nqb = sb("nqb", [P, KC])
        b1c = sb("b1c", [P, FFC])
        rw = sb("rw", [P, KC, NE])
        mn = sb("mn", [TT, NT * HEADS])
        rsum = sb("rsum", [TT, NT * HEADS])
        rinv = sb("rinv", [TT, NT, HEADS])
        ftmp = sb("ftmp", [TT, NT * D])
        cs = sb("cs", [TT, BT])

        s_l1c, s_w1in, s_wff = sem("l1_const_in"), sem("l1_weights_in"), sem("ff_weights_in")
        s_al, s_alpha, s_fade, s_nqb, s_pz = sem("alpha_parts"), sem("alpha"), sem("fade"), sem("nqb"), sem("pT_zeroed")
        v1ch, a1ch, g1ch, v4ch, a4ch, cch2, v1chx = [sem(n) for n in ("dve_chain_l1", "act_chain_l1", "pool_chain_l1", "dve_chain_n4", "act_chain_n4", "router_chain", "values1_chain")]
        s_mv1, s_rstd1, s_xn1, s_xT1ps, s_xT1 = [sem(n) for n in ("mv1", "rstd1", "xn1", "xT1_ps", "xT1_sb")]
        s_q1ps, s_k1ps, s_v1ps, s_q1, s_k1, s_v1, s_kb, s_hb = [sem(n) for n in ("q1_ps", "k1_ps", "v1_ps", "q1_sb", "k1_sb", "v1_sb", "k1_masked", "h_biased")]
        s_sps, s_min, s_p, s_ptps, s_pt, s_pv1 = [sem(n) for n in ("logits1_ps", "logits1_sb", "probs", "probsT_ps", "probsT_sb", "pv1_ps")]
        s_rspread = sem("rinv_spread")
        s_rinv, s_rbps, s_rbs, s_y1, s_o1ps, s_h3 = [sem(n) for n in ("rinv", "rb_ps", "rb_sb", "y1_sb", "o1_ps", "h_attn1")]
        s_mv4, s_rstd4, s_x4, s_x4Tps, s_x4T, s_lg4ps, s_lg4, s_x4Tall = [sem(n) for n in ("mv4", "rstd4", "x4", "x4T_ps", "x4T_sb", "router_ps", "router_sb", "x4T_all")]
        s_fups, s_hid, s_fdps, s_ft, s_h4, s_rexp, s_rx = [sem(n) for n in ("ff_up_ps", "ff_hidden", "ff_down_ps", "ff_biased", "h_final", "router_exp", "router_shifted")]

        xs_dram = nc.dram_tensor("routed_in", (RT * SLOTS, D), f32, kind="Internal").ap()
        ys_dram = nc.dram_tensor("routed_out", (RT * SLOTS, D), f32, kind="Internal").ap()

        s_rc, s_wf, s_zset, s_zdone = sem("routing_const_in"), sem("wf_in"), sem("zero_set"), sem("slots_zeroed")
        s_mv2, s_rstd2, s_x2 = sem("mv2_ready"), sem("rstd2_ready"), sem("x2_ready")
        s_x2Tps, s_x2T, s_lgps, s_lg = sem("x2T_ps"), sem("x2T_sb"), sem("logits_ps"), sem("logits_sb")
        s_x2all, s_x2Tall = sem("x2_all"), sem("x2T_all")
        vch2, ach2, rch = sem("dve_chain2"), sem("act_chain2"), sem("routing_chain")
        s_gap, s_gw, s_m12, s_rps = sem("logit_gap"), sem("tanh_gap"), sem("choices"), sem("prefix_ps")
        s_slot, s_texp, s_eup = sem("slots_known"), sem("tile_experts"), sem("eup_in")
        s_scat, s_xg = sem("scattered"), [sem(f"xg_in{i}") for i in range(2)]
        s_sups, s_sg, s_shid, s_sdps, s_hsh = sem("shared_up_ps"), sem("shared_gate_sb"), sem("shared_hidden"), sem("shared_down_ps"), sem("h_shared")
        s_xgTps, s_xgT, s_rups, s_rg, s_rh = sem("xgT_ps"), sem("xgT_sb"), sem("routed_up_ps"), sem("routed_gate_sb"), sem("routed_hidden")
        s_rhTps, s_rhT, s_rdps, s_ry, s_yst = sem("rhT_ps"), sem("rhT_sb"), sem("routed_down_ps"), sem("routed_y_sb"), [sem(f"routed_stored{i}") for i in range(2)]
        s_yg = [sem(f"gathered{i}") for i in range(2)]
        s_comb, cch = sem("combined"), sem("combine_chain")

        s_const, s_tokin, s_txt, s_w0 = sem("const_in"), sem("tok_in"), sem("txt_in"), sem("w0_in")
        s_ones = sem("ones_set")
        s_zero = sem("zeros_set")
        s_tokps, s_toksb, s_tokh = sem("tok_ps"), sem("tok_sb"), sem("tok_in_h")
        s_base = sem("base_ready")
        vch, ach, gch = sem("dve_chain"), sem("act_chain"), sem("pool_chain")
        s_mv, s_rstd, s_xn = sem("mv_ready"), sem("rstd_ready"), sem("xn_ready")
        s_xTps, s_xT = sem("xT_ps"), sem("xT_sb")
        s_z1, s_q, s_k, s_v = sem("z1_ps"), sem("q_ps"), sem("k_ps"), sem("v_ps")
        s_th, s_z2, s_lc = sem("tanh_sb"), sem("z2_ps"), sem("lc_sb")
        s_lam, s_lnlam, s_G = sem("lam_sb"), sem("lnlam_sb"), sem("G_sb")
        s_dq, s_dk, s_eq, s_ek = sem("dq_sb"), sem("dk_sb"), sem("eq_sb"), sem("ek_sb")
        s_ksb, s_vsb, s_qe, s_kr = sem("k_sb"), sem("v_sb"), sem("qe_sb"), sem("kr_sb")
        s_qb0, s_qb1 = sem("qb_half0"), sem("qb_half1")
        s_aps, s_adve, s_aact, s_pv = sem("scores_ps"), sem("scores_dve"), sem("scores_act"), sem("pv_ps")
        s_ysb, s_ops, s_h1 = sem("y_sb"), sem("o_ps"), sem("h_attn0")
        s_settled = sem("dve_waits_met")
        s_out = sem("out_done")

        UNITS = [(0, 0), (1, 0), (2, 0), (2, 1), (3, 0), (3, 1)]
        MASKED = [0, 1, 3, 5]
        PLAIN = [2, 4]
        UNITS1 = [(half, t, n, min(3, HH - n)) for half in range(KC) for t in range(NT) for n in range(0, HH, 3)]
        NU1 = len(UNITS1)

        def since(eng, s, v):
            if not isinstance(v, int) or v > 0:
                eng.wait_ge(s, v)

        def htile(b):
            return h[:, bass.ds(b * (NT * D), NT * D)].rearrange("p (t d) -> p t d", t=NT)

        block = ctx.enter_context(nc.Block())

        @block.sync
        def _(sp):
            sp.dma_start(xp[:, :, :], a["patches"]).then_inc(s_tokin, 16)
            sp.dma_start(tokw[:, :, :], a["tok_w"]).then_inc(s_tokin, 16)
            sp.dma_start(h4[IMG:TT, :, 0, :], a["txt"][:, 0:TT - IMG, :].rearrange("b p d -> p b d")).then_inc(s_txt, 16)
            sp.dma_start(h4[:, :, 1, :], a["txt"][:, TT - IMG:TXT, :].rearrange("b p d -> p b d")).then_inc(s_txt, 16)
            for dst, src in ((ident, "ident"), (hmask, "hmask")):
                sp.dma_start(dst[:, :], a[src]).then_inc(s_const, 16)
            sp.dma_start(cmask[:, :, :], a["cmask"]).then_inc(s_const, 16)
            for dst, src in ((wq, "wq"), (wk, "wk"), (wv, "wv"), (wo, "wo"), (cw1, "cw1"), (gw, "gw")):
                sp.dma_start(dst[:, :, :], a[src]).then_inc(s_w0, 16)
            for dst, src in ((cb1, "cb1"), (cw2, "cw2"), (cb2, "cb2"), (dec, "dec")):
                sp.dma_start(dst[:, :], a[src]).then_inc(s_w0, 16)
            for dst, src in ((arow, "alpha"), (b1c, "b1")):
                sp.dma_start(dst[:, :], a[src]).then_inc(s_l1c, 16)
            for dst, src in ((dist, "dist"), (rows1, "rows1"), (qkb, "qkb"), (rw, "rw")):
                sp.dma_start(dst[:, :, :], a[src]).then_inc(s_l1c, 16)
            for b in range(B):
                i, j = divmod(b, 3)
                sp.wait_ge(s_toksb, i + 1)
                sp.dma_start(h4[0:IMG, b, 0, :], tok[IMG * j:IMG * j + IMG, i, :]).then_inc(s_tokh, 16)
            for dst, src in ((tri, "tri"), (rc, "rc")):
                sp.dma_start(dst[:, :], a[src]).then_inc(s_rc, 16)
            for dst, src in ((sup, "sup"), (sdn, "sdn"), (edn[:, :, :], "edn")):
                sp.dma_start(dst, a[src]).then_inc(s_wf, 16)
            sp.wait_ge(s_zset, 1)
            for n in range(RT // 4):
                sp.dma_start(xs_dram[4 * n * SLOTS:4 * (n + 1) * SLOTS, :].rearrange("(p k) d -> p (k d)", p=P),
                             zero[:, :]).then_inc(s_zdone, 16)
            sp.wait_ge(s_zdone, 16 * (RT // 4))
            with sp.Fori(0, B) as b:
                sp.wait_ge(s_x2, b + 1)
                sp.dma_start(x2[:, bass.ds(b * (NT * D), NT * D)],
                             x2s[:, :, :].rearrange("p t d -> p (t d)")).then_inc(s_x2all, 16)
                sp.wait_ge(s_x2T, b + 1)
                sp.dma_start(x2T[:, :, bass.ds(b * T, T)], x2Ts[:, :, :]).then_inc(s_x2Tall, 16)

            sp.wait_ge(s_h1, B)
            sp.dma_start(eup[:, :, :], a["eup"]).then_inc(s_eup, 16)
            for dst, src in ((wq, "wq1"), (wk, "wk1"), (wv, "wv1"), (wo, "wo1")):
                sp.dma_start(dst[:, :, :], a[src]).then_inc(s_w1in, 16)
            sp.wait_ge(s_scat, 16 * TOPK * BT)
            sp.dma_start(w1, a["w1"]).then_inc(s_wff, 16)
            sp.dma_start(w2, a["w2"]).then_inc(s_wff, 16)

            def load(j, p):
                since(sp, s_xgTps, j - 1)
                sp.dma_start(xg[p][:, :], xs_dram[bass.ds(j * SLOTS, SLOTS), :]).then_inc(s_xg[p], 16)

            def store(j, p):
                sp.wait_ge(s_ry, j + 1)
                sp.dma_start(ys_dram[bass.ds(j * SLOTS, SLOTS), :], ry[p][:, :]).then_inc(s_yst[p], 16)

            load(0, 0)
            load(1, 1)
            with sp.Fori(0, RT // 2 - 1) as i:
                load(2 * i + 2, 0)
                store(2 * i, 0)
                load(2 * i + 3, 1)
                store(2 * i + 1, 1)
            store(RT - 2, 0)
            store(RT - 1, 1)
            with sp.Fori(0, B) as b:
                sp.wait_ge(s_x4T, b + 1)
                sp.dma_start(x2T[:, :, bass.ds(b * T, T)], x2Ts[:, :, :]).then_inc(s_x4Tall, 16)
            for b in range(B):
                sp.wait_ge(s_h4, b + 1)
                sp.dma_start(out[b].rearrange("(t p) d -> p t d", t=NT), h4[:, b, :, :]).then_inc(s_out, 16)
            sp.wait_ge(s_out, 16 * B)

        @block.tensor
        def _(pe):
            mm = nc.tensor.matmul
            pe.wait_ge(s_tokin, 32)
            for i in range(3):
                n = IMG * min(3, B - 3 * i)
                for c in range(PC):
                    last = mm(bank[i][0:n, 0:D], xp[:, c, 3 * IMG * i:3 * IMG * i + n], tokw[:, c, :],
                              start=(c == 0), stop=(c == PC - 1))
                last.then_inc(s_tokps, 1)
            pe.wait_ge(s_w0, 16 * 10)
            pe.wait_ge(s_const, 16 * 3)
            pe.wait_ge(s_toksb, 3)

            def project(b):
                pe.wait_ge(s_xn, b + 1)
                since(pe, s_lc, 2 * b)
                for t in range(NT):
                    for c in range(KC):
                        last = nc.tensor.transpose(bank[0][:, c * T + t * TT:c * T + (t + 1) * TT],
                                                   xn[:, t, c * P:(c + 1) * P], ident[0:TT, 0:TT])
                last.then_inc(s_xTps, 1)
                pe.wait_ge(s_xT, b + 1)
                for c in range(KC):
                    last = mm(bank[0][0:64, 0:T], cw1[:, c, :], xnT[:, c, :], start=(c == 0), stop=(c == KC - 1))
                last.then_inc(s_z1, 1)
                since(pe, s_qe, b)
                for o in range(KC):
                    for c in range(KC):
                        last = mm(bank[1][:, o * T:(o + 1) * T], wq[:, c, o * P:(o + 1) * P], xnT[:, c, :],
                                  start=(c == 0), stop=(c == KC - 1))
                last.then_inc(s_q, 1)
                since(pe, s_ksb, b)
                for o in range(KC):
                    for c in range(KC):
                        last = mm(bank[2][:, o * T:(o + 1) * T], wk[:, c, o * P:(o + 1) * P], xnT[:, c, :],
                                  start=(c == 0), stop=(c == KC - 1))
                last.then_inc(s_k, 1)
                since(pe, s_vsb, b)
                for t in range(NT):
                    for c in range(KC):
                        last = mm(bank[3][0:TT, t * D:(t + 1) * D], xnT[:, c, t * TT:(t + 1) * TT], wv[:, c, :],
                                  start=(c == 0), stop=(c == KC - 1))
                last.then_inc(s_v, 1)

            def gate(b):
                pe.wait_ge(s_th, b + 1)
                for o in range(KC):
                    last = mm(bank[0][:, o * T:(o + 1) * T], cw2[:, o * P:(o + 1) * P], th[:, :], start=True, stop=True)
                last.then_inc(s_z2, 1)

            def scores(b, p, half):
                pe.wait_ge(s_kr, b + 1)
                pe.wait_ge(s_qb0 if half == 0 else s_qb1, b + 1)
                for u, (r, t) in enumerate(UNITS):
                    if u == 0:
                        since(pe, s_aact, 4 * b + 2 * half)
                    elif u == 4:
                        pe.wait_ge(s_aact, 4 * b + 2 * half + 1)
                    else:
                        since(pe, s_adve, 8 * b + 4 * half + [None, 0, 1, 2, None, 3][u])
                    m = min(TT, CH * (r + 1) - TT * t)
                    mm(bank[4 + u % 2][0:m, 0:HH * CH],
                       kr[p][:, half, COFF[r] + TT * t:COFF[r] + TT * t + m],
                       qb[p][:, half, :, CH * r:CH * (r + 1)], start=True, stop=True).then_inc(s_aps, 1)

            def mix(b, p, half):
                pe.wait_ge(s_adve, 8 * b + 4 * half + 4)
                pe.wait_ge(s_aact, 4 * b + 2 * half + 2)
                if half == 0:
                    pe.wait_ge(s_vsb, b + 1)
                    since(pe, s_ysb, b)
                for t in range(NT):
                    for par in range(2):
                        for i in range(4):
                            last = mm(bank[6][32 * i:32 * i + 32, half * T + t * TT:(half + 1) * T],
                                      vz[p][par][:, t, 4 * half + i, :, :],
                                      asb[half][:, t, 2 * i + par, t * TT:T],
                                      start=(t == 0 and par == 0), stop=(t == 1 and par == 1),
                                      skip_group_check=True, tile_position=(0, 32 * i))
                last.then_inc(s_pv, 1)

            def project_out(b):
                pe.wait_ge(s_ysb, b + 1)
                since(pe, s_lg, b)
                for t in range(NT):
                    for c in range(KC):
                        last = mm(bank[7][0:TT, t * D:(t + 1) * D], yT[:, c, t * TT:(t + 1) * TT], wo[:, c, :],
                                  start=(c == 0), stop=(c == KC - 1))
                last.then_inc(s_ops, 1)

            def turn2(b):
                pe.wait_ge(s_x2, b + 1)
                pe.wait_ge(s_ysb, b + 1)
                for t in range(NT):
                    for c in range(KC):
                        last = nc.tensor.transpose(bank[6][:, c * T + t * TT:c * T + (t + 1) * TT],
                                                   x2s[:, t, c * P:(c + 1) * P], ident[0:TT, 0:TT])
                last.then_inc(s_x2Tps, 1)

            def route(b):
                pe.wait_ge(s_x2T, b + 1)
                pe.wait_ge(s_h1, b + 1)
                for t in range(NT):
                    for c in range(KC):
                        last = mm(bank[7][0:TT, t * NE:(t + 1) * NE], x2Ts[:, c, t * TT:(t + 1) * TT], gw[:, c, :],
                                  start=(c == 0), stop=(c == KC - 1))
                last.then_inc(s_lgps, 1)

            def step(b, p, first=False):
                project(b + 1)
                scores(b, p, 0)
                if not first:
                    turn2(b - 1)
                gate(b + 1)
                scores(b, p, 1)
                if not first:
                    route(b - 1)
                    pe.wait_ge(s_x2T, b)
                mix(b, p, 0)
                mix(b, p, 1)
                project_out(b)

            project(0)
            gate(0)
            step(0, 0, first=True)
            with pe.Fori(0, B // 2 - 1) as i:
                step(2 * i + 1, 1)
                step(2 * i + 2, 0)
            scores(B - 1, 1, 0)
            turn2(B - 2)
            scores(B - 1, 1, 1)
            route(B - 2)
            pe.wait_ge(s_x2T, B - 1)
            mix(B - 1, 1, 0)
            mix(B - 1, 1, 1)
            project_out(B - 1)
            turn2(B - 1)
            route(B - 1)

            def shared_up(g, j):
                if g == 0:
                    pe.wait_ge(s_lg, B)
                else:
                    pe.wait_ge(s_shid, FC * (g - 1) + j + 1)
                for half in range(2):
                    for c in range(KC):
                        last = mm(bank[2 * j + half][:, 0:GN], sup[:, c, half * HALF + j * P:half * HALF + (j + 1) * P],
                                  x2T[:, c, g * GN:(g + 1) * GN], start=(c == 0), stop=(c == KC - 1))
                last.then_inc(s_sups, 1)

            def shared_down(g):
                pe.wait_ge(s_shid, FC * (g + 1))
                for q in range(2):
                    since(pe, s_hsh, 2 * g + q - 1)
                    for t in range(NT):
                        for j in range(FC):
                            last = mm(bank[6 + q][0:TT, t * D:(t + 1) * D],
                                      shid[g % 2][:, j, q * T + t * TT:q * T + (t + 1) * TT], sdn[:, j, :],
                                      start=(j == 0), stop=(j == FC - 1))
                    last.then_inc(s_sdps, 1)

            pe.wait_ge(s_wf, 16 * 3)
            pe.wait_ge(s_x2Tall, 16 * B)
            shared_up(0, 0)
            shared_up(0, 1)
            pe.wait_ge(s_m12, 1)
            pe.wait_ge(s_rc, 32)
            m12 = rb[:, 6, :]
            mm(bank[7][0:TT, 0:BT * NE], tri[:, :], m12, start=True, stop=True)
            mm(bank[7][0:TT, 256:256 + BT * NE], ones[0:TT, 0:TT], m12, start=True, stop=True).then_inc(s_rps, 1)
            shared_up(0, 2)
            for g in range(1, GR):
                for j in range(FC):
                    shared_up(g, j)
                if g == 1:
                    pe.wait_ge(s_slot, 1)
                shared_down(g - 1)
            shared_down(GR - 1)

            pe.wait_ge(s_texp, 1)
            pe.wait_ge(s_eup, 16)

            def turn_x(j, p):
                pe.wait_ge(s_xg[p], 8 * j + 16 - 8 * p)
                since(pe, s_xgT, j)
                for c in range(KC):
                    last = nc.tensor.transpose(bank[0][:, c * P:(c + 1) * P], xg[p][:, c * P:(c + 1) * P], ident[:, :])
                last.then_inc(s_xgTps, 1)

            def up(j, p):
                e = pe.value_load(texpi[0:1, bass.ds(j, 1)], min_val=0, max_val=NE - 1)
                pe.wait_ge(s_xgT, j + 1)
                since(pe, s_rh, j - 1)
                for half in range(2):
                    for c in range(KC):
                        last = mm(bank[1 + 2 * p + half][:, 0:HALF], xgT[p][:, c, :],
                                  eup[:, c, bass.ds(e * (2 * HALF) + half * HALF, HALF)],
                                  start=(c == 0), stop=(c == KC - 1))
                last.then_inc(s_rups, 1)

            def turn_hidden(j, p):
                pe.wait_ge(s_rh, j + 1)
                since(pe, s_rhT, j)
                for k in range(FC):
                    last = nc.tensor.transpose(bank[5][:, k * P:(k + 1) * P], rh[p][:, k * P:(k + 1) * P], ident[:, :])
                last.then_inc(s_rhTps, 1)

            def down(j):
                e = pe.value_load(texpi[0:1, bass.ds(j, 1)], min_val=0, max_val=NE - 1)
                pe.wait_ge(s_rhT, j + 1)
                since(pe, s_ry, j)
                for k in range(FC):
                    last = mm(bank[6][:, 0:D], rhT[:, k, :], edn[:, k, bass.ds(e * D, D)],
                              start=(k == 0), stop=(k == FC - 1))
                last.then_inc(s_rdps, 1)

            def tile_step(j, p):
                turn_hidden(j - 1, 1 - p)
                turn_x(j + 1, 1 - p)
                up(j, p)
                down(j - 1)

            turn_x(0, 0)
            turn_x(1, 1)
            up(0, 0)
            tile_step(1, 1)
            tile_step(2, 0)
            with pe.Fori(1, RT // 2 - 1) as i:
                tile_step(2 * i + 1, 1)
                tile_step(2 * i + 2, 0)
            turn_hidden(RT - 2, 0)
            up(RT - 1, 1)
            down(RT - 2)
            turn_hidden(RT - 1, 1)
            down(RT - 1)

            pe.wait_ge(s_w1in, 64)
            pe.wait_ge(s_l1c, 16 * 6)

            def project1(b):
                pe.wait_ge(s_xn1, b + 1)
                since(pe, s_lg4, b - 1)
                for t in range(NT):
                    for c in range(KC):
                        last = nc.tensor.transpose(bank[0][:, c * T + t * TT:c * T + (t + 1) * TT],
                                                   xn[:, t, c * P:(c + 1) * P], ident[0:TT, 0:TT])
                last.then_inc(s_xT1ps, 1)
                pe.wait_ge(s_xT1, b + 1)
                since(pe, s_y1, b - 1)
                for o in range(KC):
                    for c in range(KC):
                        last = mm(bank[1][:, o * T:(o + 1) * T], wq[:, c, o * P:(o + 1) * P], xnT[:, c, :],
                                  start=(c == 0), stop=(c == KC - 1))
                last.then_inc(s_q1ps, 1)
                since(pe, s_rbs, b - 1)
                for o in range(KC):
                    for c in range(KC):
                        last = mm(bank[2][:, o * T:(o + 1) * T], wk[:, c, o * P:(o + 1) * P], xnT[:, c, :],
                                  start=(c == 0), stop=(c == KC - 1))
                last.then_inc(s_k1ps, 1)
                since(pe, s_h3, b - 1)
                for t in range(NT):
                    for c in range(KC):
                        last = mm(bank[3][0:TT, t * D:(t + 1) * D], xnT[:, c, t * TT:(t + 1) * TT], wv[:, c, :],
                                  start=(c == 0), stop=(c == KC - 1))
                last.then_inc(s_v1ps, 1)

            def logits1(b, p, u):
                half, t, n, w = UNITS1[u]
                if u == 0:
                    pe.wait_ge(s_q1, 2 * b + 2)
                if u % (NU1 // 2) == 0:
                    pe.wait_ge(s_kb, 2 * b + half + 1)
                since(pe, s_min, NU1 * b + u - 1)
                mm(bank[4 + u % 2][0:TT, 0:w * T], q1[p][:, half, t * TT:(t + 1) * TT], kb[p][:, half, n:n + w, :],
                   start=True, stop=True).then_inc(s_sps, 1)

            def turn_probs(b, u):
                half, t, n, w = UNITS1[u]
                pe.wait_ge(s_p, NU1 * b + u + 1)
                since(pe, s_pt, NU1 * b + u - 1)
                for kt in range(NT):
                    for i in range(w):
                        last = nc.tensor.transpose(bank[6 + u % 2][0:TT, (kt * w + i) * TT:(kt * w + i + 1) * TT],
                                                   ring[u % 4][0:TT, i, kt * TT:(kt + 1) * TT], ident[0:TT, 0:TT])
                last.then_inc(s_ptps, 1)

            def turn4(b):
                pe.wait_ge(s_x4, b + 1)
                for t in range(NT):
                    for c in range(KC):
                        last = nc.tensor.transpose(bank[0][:, c * T + t * TT:c * T + (t + 1) * TT],
                                                   x2s[:, t, c * P:(c + 1) * P], ident[0:TT, 0:TT])
                last.then_inc(s_x4Tps, 1)

            def router(b):
                pe.wait_ge(s_x4T, b + 1)
                for t in range(NT):
                    for c in range(KC):
                        last = mm(bank[0][0:TT, t * NE:(t + 1) * NE], x2Ts[:, c, t * TT:(t + 1) * TT], rw[:, c, :],
                                  start=(c == 0), stop=(c == KC - 1))
                last.then_inc(s_lg4ps, 1)

            def mix1(b, p, half):
                pe.wait_ge(s_pt, NU1 * b + (half + 1) * NU1 // 2)
                for t in range(NT):
                    for par in range(2):
                        for i in range(4):
                            last = mm(bank[1][32 * i:32 * i + 32, half * T:(half + 1) * T],
                                      vz[p][par][:, t, 4 * half + i, :, :], pT[half][:, t, 2 * i + par, :],
                                      start=(t == 0 and par == 0), stop=(t == 1 and par == 1),
                                      skip_group_check=True, tile_position=(0, 32 * i))
                last.then_inc(s_pv1, 1)

            def finish1(b):
                pe.wait_ge(s_rspread, b + 1)
                for half in range(KC):
                    for t in range(NT):
                        last = mm(bank[2][:, half * T + t * TT:half * T + (t + 1) * TT],
                                  rspread[0:TT, t, half * P:(half + 1) * P],
                                  ident[0:TT, 0:TT], start=True, stop=True)
                last.then_inc(s_rbps, 1)
                pe.wait_ge(s_y1, b + 1)
                for t in range(NT):
                    for c in range(KC):
                        last = mm(bank[3][0:TT, t * D:(t + 1) * D], yT[:, c, t * TT:(t + 1) * TT], wo[:, c, :],
                                  start=(c == 0), stop=(c == KC - 1))
                last.then_inc(s_o1ps, 1)

            def step1(b, p, first=False, final=False):
                for u in range(NU1):
                    logits1(b, p, u)
                    if u == 1 and not first:
                        turn4(b - 1)
                    if u >= 2:
                        turn_probs(b, u - 2)
                if not first:
                    router(b - 1)
                if not final:
                    project1(b + 1)
                turn_probs(b, NU1 - 2)
                turn_probs(b, NU1 - 1)
                if not final:
                    pe.wait_ge(s_q1, 2 * b + 4)
                    pe.wait_ge(s_v1, b + 2)
                    pe.wait_ge(s_k1, b + 2)
                else:
                    pe.wait_ge(s_v1, b + 1)
                if first:
                    pe.wait_ge(s_pz, 1)
                mix1(b, p, 0)
                mix1(b, p, 1)
                finish1(b)

            project1(0)
            step1(0, 0, first=True)
            with pe.Fori(0, B // 2 - 1) as i:
                step1(2 * i + 1, 1)
                step1(2 * i + 2, 0)
            step1(B - 1, 1, final=True)
            turn4(B - 1)
            router(B - 1)

            def ff_up(g):
                for j in range(FFC):
                    n = FFC * g + j
                    since(pe, s_hid, n - 5)
                    for c in range(KC):
                        last = mm(bank[n % 6][:, 0:GN], w1[:, c, j * P:(j + 1) * P], x2T[:, c, g * GN:(g + 1) * GN],
                                  start=(c == 0), stop=(c == KC - 1))
                    last.then_inc(s_fups, 1)

            def ff_down(g):
                pe.wait_ge(s_hid, FFC * (g + 1))
                for q in range(2):
                    since(pe, s_ft, 2 * g + q - 1)
                    for t in range(NT):
                        for j in range(FFC):
                            last = mm(bank[6 + q][0:TT, t * D:(t + 1) * D],
                                      hid[g % 2][:, j, q * T + t * TT:q * T + (t + 1) * TT], w2[:, j, :],
                                      start=(j == 0), stop=(j == FFC - 1))
                    last.then_inc(s_fdps, 1)

            pe.wait_ge(s_wff, 32)
            pe.wait_ge(s_x4Tall, 16 * B)
            pe.wait_ge(s_lg4, B)
            ff_up(0)
            for g in range(1, GR):
                ff_up(g)
                ff_down(g - 1)
            ff_down(GR - 1)

        @block.scalar
        def _(act):
            acte = nc.scalar.activation
            for i in range(3):
                n = IMG * min(3, B - 3 * i)
                act.wait_ge(s_tokps, i + 1)
                nc.scalar.copy(tok[0:n, i, :], bank[i][0:n, 0:D]).then_inc(s_toksb, 1)
            act.wait_ge(s_w0, 16 * 10)
            nc.scalar.preload_act_table_set("sigmoid_and_others")
            acte(base[:, :], dec[:, :], ACT.Sigmoid).then_inc(s_base, 1)
            act.wait_ge(s_zero, 1)
            nc.scalar.preload_act_table_set("natural_log_exp_and_others")
            act.wait_ge(s_al, 1)
            acte(aabs[:, 1, :], aabs[:, 0, :], ACT.Exp, scale=-1.0).then_inc(a1ch, 1)
            act.wait_ge(a1ch, 1)
            acte(aabs[:, 0, :], aabs[:, 1, :], ACT.Ln, bias=1.0).then_inc(s_al, 1)

            def norm_scale(b):
                nc.scalar.preload_act_table_set("natural_log_exp_and_others")
                act.wait_ge(s_mv, b + 1)
                acte(lnv[:, :], mv[:, :, 1], ACT.Ln, bias=EPSC[0:TT, 0:1]).then_inc(ach, 1)
                act.wait_ge(ach, b + 1)
                acte(rstd[:, :], lnv[:, :], ACT.Exp, scale=-0.5).then_inc(s_rstd, 1)

            def front(b, p):
                norm_scale(b)
                act.wait_ge(s_xTps, b + 1)
                since(act, s_v, b)
                nc.scalar.copy(xnT[:, :, :].rearrange("p c t -> p (c t)"), bank[0][:, 0:KC * T]).then_inc(s_xT, 1)
                nc.scalar.preload_act_table_set("sigmoid_and_others")
                act.wait_ge(s_z1, b + 1)
                since(act, s_z2, b)
                acte(th[:, :], bank[0][0:64, 0:T], ACT.Tanh, bias=cb1[:, 0:1]).then_inc(s_th, 1)
                act.wait_ge(s_k, b + 1)
                since(act, s_kr, b)
                nc.scalar.copy(ksb[:, :, :].rearrange("p c t -> p (c t)"), bank[2][:, 0:KC * T]).then_inc(s_ksb, 1)
                act.wait_ge(s_v, b + 1)
                since(act, s_pv, 2 * b - 2)
                for par in range(2):
                    src = bank[3][0:TT, :].rearrange("p (t i j d) -> p (t i) j d", t=NT, i=HEADS // 2, j=2)
                    dst = vz[p][par][0:TT, :, :, :, :].rearrange("p t i j d -> p (t i) j d")
                    ins = nc.scalar.copy(dst[:, :, par, :], src[:, :, par, :])
                ins.then_inc(s_vsb, 1)

            def decays(b):
                act.wait_ge(s_z2, b + 1)
                since(act, s_lam, b)
                for o in range(KC):
                    acte(lc[:, o, :], bank[0][:, o * T:(o + 1) * T], ACT.Sigmoid, bias=cb2[:, o:o + 1]).then_inc(s_lc, 1)
                nc.scalar.preload_act_table_set("natural_log_exp_and_others")
                act.wait_ge(s_lam, b + 1)
                since(act, s_G, b)
                acte(lnlam[:, :, :], lam[:, :, :], ACT.Ln).then_inc(s_lnlam, 1)
                act.wait_ge(s_dq, b + 1)
                since(act, s_qe, b)
                acte(eq[:, :], dq[:, :], ACT.Exp).then_inc(s_eq, 1)
                act.wait_ge(s_dk, b + 1)
                since(act, s_kr, b)
                acte(ek[:, :, :], dk[:, :, :], ACT.Exp).then_inc(s_ek, 1)

            def plain(b, half):
                for n, u in enumerate(PLAIN):
                    r, t = UNITS[u]
                    act.wait_ge(s_aps, 12 * b + 6 * half + u + 1)
                    if n == 0:
                        since(act, s_pv, 2 * b + half - 1)
                    nc.scalar.copy(asb[half][0:TT, t, :, CH * r:CH * (r + 1)],
                                   bank[4 + u % 2][0:TT, 0:HH * CH].rearrange("p (h c) -> p h c", c=CH)).then_inc(s_aact, 1)

            def mixed(b):
                act.wait_ge(s_pv, 2 * b + 2)
                since(act, s_ops, b)
                nc.scalar.copy(yT[:, :, :].rearrange("p c t -> p (c t)"), bank[6][:, 0:KC * T]).then_inc(s_ysb, 1)

            def norm2(b):
                act.wait_ge(s_mv2, b + 1)
                acte(lnv2[:, :], mv2[:, :, 1], ACT.Ln, bias=EPSC[0:TT, 0:1]).then_inc(ach2, 1)
                act.wait_ge(ach2, b + 1)
                acte(rstd2[:, :], lnv2[:, :], ACT.Exp, scale=-0.5).then_inc(s_rstd2, 1)

            def turned2(b):
                act.wait_ge(s_x2Tps, b + 1)
                since(act, s_x2Tall, 16 * b)
                since(act, s_lgps, b)
                nc.scalar.copy(x2Ts[:, :, :].rearrange("p c t -> p (c t)"), bank[6][:, 0:KC * T]).then_inc(s_x2T, 1)

            def step(b, p, first=False):
                front(b + 1, 1 - p)
                plain(b, 0)
                if not first:
                    turned2(b - 1)
                decays(b + 1)
                plain(b, 1)
                mixed(b)
                norm2(b)

            front(0, 0)
            decays(0)
            step(0, 0, first=True)
            with act.Fori(0, B // 2 - 1) as i:
                step(2 * i + 1, 1)
                step(2 * i + 2, 0)
            plain(B - 1, 0)
            turned2(B - 2)
            plain(B - 1, 1)
            mixed(B - 1)
            norm2(B - 1)
            turned2(B - 1)

            nc.scalar.preload_act_table_set("silu_and_others")
            act.wait_ge(s_gap, 1)
            acte(rs[:, 5, :], rs[:, 4, :], ACT.Tanh, scale=0.5).then_inc(s_gw, 1)
            for g in range(GR):
                for j in range(FC):
                    act.wait_ge(s_sups, FC * g + j + 1)
                    since(act, s_shid, FC * (g - 1) + j + 1)
                    acte(sgate[:, j, :], bank[2 * j][:, 0:GN], ACT.Silu).then_inc(s_sg, 1)

            def silu(j, p):
                act.wait_ge(s_rups, j + 1)
                since(act, s_rh, j)
                acte(rg[:, :], bank[1 + 2 * p][:, 0:HALF], ACT.Silu).then_inc(s_rg, 1)

            def hidden_turned(j):
                act.wait_ge(s_rhTps, j + 1)
                since(act, s_rdps, j)
                nc.scalar.copy(rhT[:, :, :].rearrange("p k n -> p (k n)"), bank[5][:, 0:FC * P]).then_inc(s_rhT, 1)

            silu(0, 0)
            hidden_turned(0)
            silu(1, 1)
            hidden_turned(1)
            silu(2, 0)
            with act.Fori(1, RT // 2 - 1) as i:
                hidden_turned(2 * i)
                silu(2 * i + 1, 1)
                hidden_turned(2 * i + 1)
                silu(2 * i + 2, 0)
            hidden_turned(RT - 2)
            silu(RT - 1, 1)
            hidden_turned(RT - 1)

            nc.scalar.preload_act_table_set("natural_log_exp_and_others")

            def norm1(b):
                act.wait_ge(s_mv1, b + 1)
                acte(lnv[:, :], mv[:, :, 1], ACT.Ln, bias=EPSC[0:TT, 0:1]).then_inc(a1ch, 1)
                act.wait_ge(a1ch, b + 2)
                acte(rstd[:, :], lnv[:, :], ACT.Exp, scale=-0.5).then_inc(s_rstd1, 1)

            def norm4(b):
                act.wait_ge(s_mv4, b + 1)
                acte(lnv2[:, :], mv2[:, :, 1], ACT.Ln, bias=EPSC[0:TT, 0:1]).then_inc(a4ch, 1)
                act.wait_ge(a4ch, b + 1)
                acte(rstd2[:, :], lnv2[:, :], ACT.Exp, scale=-0.5).then_inc(s_rstd4, 1)

            def projected1(b, p):
                act.wait_ge(s_xT1ps, b + 1)
                since(act, s_v1ps, b)
                nc.scalar.copy(xnT[:, :, :].rearrange("p c t -> p (c t)"), bank[0][:, 0:KC * T]).then_inc(s_xT1, 1)
                act.wait_ge(s_q1ps, b + 1)
                since(act, s_sps, NU1 * (b - 1))
                for o in range(KC):
                    acte(q1[p][:, o, :], bank[1][:, o * T:(o + 1) * T], ACT.Identity, bias=nqb[:, o:o + 1],
                         scale=-1.0 / SCALE).then_inc(s_q1, 1)
                act.wait_ge(s_k1ps, b + 1)
                since(act, s_kb, 2 * b)
                for o in range(KC):
                    ins = acte(ksb1[:, o, :], bank[2][:, o * T:(o + 1) * T], ACT.Identity, bias=qkb[:, 1, o:o + 1])
                ins.then_inc(s_k1, 1)

            def probs(b, u):
                half, t, n, w = UNITS1[u]
                act.wait_ge(s_min, NU1 * b + u + 1)
                for i in range(w):
                    col = t * HEADS + half * HH + n + i
                    ins = acte(ring[u % 4][0:TT, i, :], ring[u % 4][0:TT, i, :], ACT.Exp, scale=-1.0,
                               bias=mn[:, col:col + 1], accum_out=rsum[:, col:col + 1])
                ins.then_inc(s_p, 1)

            def step1(b, p, first=False, final=False):
                for u in range(NU1):
                    probs(b, u)
                    if u == 2 and not final:
                        norm1(b + 1)
                    if u == 3 and not first:
                        turned4(b - 1)
                if not final:
                    projected1(b + 1, 1 - p)
                act.wait_ge(s_rbps, b + 1)
                since(act, s_y1, b)
                nc.scalar.copy(rbs[:, :, :].rearrange("p c t -> p (c t)"), bank[2][:, 0:KC * T]).then_inc(s_rbs, 1)
                norm4(b)

            def turned4(b):
                act.wait_ge(s_x4Tps, b + 1)
                since(act, s_x4Tall, 16 * b)
                since(act, s_lg4ps, b)
                nc.scalar.copy(x2Ts[:, :, :].rearrange("p c t -> p (c t)"), bank[0][:, 0:KC * T]).then_inc(s_x4T, 1)

            act.wait_ge(s_nqb, 1)
            act.wait_ge(s_l1c, 16 * 6)
            norm1(0)
            projected1(0, 0)
            step1(0, 0, first=True)
            with act.Fori(0, B // 2 - 1) as i:
                step1(2 * i + 1, 1)
                step1(2 * i + 2, 0)
            step1(B - 1, 1, final=True)
            turned4(B - 1)
            act.wait_ge(s_rx, 1)
            acte(rb[:, 1, :], rb[:, 0, :], ACT.Exp).then_inc(s_rexp, 1)
            nc.scalar.preload_act_table_set("gelu_apprx_tanh_and_others")
            for g in range(GR):
                for j in range(FFC):
                    n = FFC * g + j
                    act.wait_ge(s_fups, n + 1)
                    if j == 0:
                        since(act, s_fdps, 2 * (g - 1))
                    acte(hid[g % 2][:, j, :], bank[n % 6][:, 0:GN], ACT.Gelu_apprx_tanh, bias=b1c[:, j:j + 1]).then_inc(s_hid, 1)

        @block.vector
        def _(dve):
            v = nc.vector

            def settle():
                dve.sem_inc(s_settled, 1)

            v.memset(ones[:, :], 1.0).then_inc(vch, 1)
            dve.wait_ge(s_base, 1)
            v.tensor_scalar(base02[:, :], base[:, :], 0.2, None, ALU.mult).then_inc(vch, 1)
            dve.wait_ge(s_txt, 32)
            dve.wait_ge(s_tokh, 16 * B)
            dve.wait_ge(s_const, 48)
            dve.wait_ge(vch, 2)
            dve.wait_ge(s_l1c, 16 * 6)
            v.tensor_scalar(nqb[:, :], qkb[:, 0, :], -1.0 / SCALE, None, ALU.mult).then_inc(s_nqb, 1)
            v.scalar_tensor_tensor(aabs[:, 0, :], arow[:, :], -1.0, arow[:, :], ALU.mult, ALU.max).then_inc(s_al, 1)
            dve.wait_ge(s_al, 2)
            v.scalar_tensor_tensor(alpha[:, :], arow[:, :], 0.0, aabs[:, 0, :], ALU.max, ALU.add).then_inc(s_alpha, 1)

            def front(b):
                c = Chain(dve, vch, 2 + 7 * b)
                ht = htile(b)
                for t in range(NT):
                    c.add(v.bn_stats(st[:, 6 * t:6 * t + 6], ht[:, t, :]))
                c.wait()
                since(dve, s_rstd, b)
                settle()
                v.bn_aggr(mv[:, 0, :], st[:, 0:6]).then_inc(vch, 1)
                v.bn_aggr(mv[:, 1, :], st[:, 6:12]).then_inc(s_mv, 1)
                c.n += 1
                dve.wait_ge(s_rstd, b + 1)
                since(dve, s_xTps, b)
                c.add(v.tensor_scalar(xn[:, 0, :], ht[:, 0, :], mv[:, 0, 0:1], rstd[:, 0:1], ALU.subtract, ALU.mult))
                v.tensor_scalar(xn[:, 1, :], ht[:, 1, :], mv[:, 1, 0:1], rstd[:, 1:2], ALU.subtract, ALU.mult).then_inc(s_xn, 1)
                c.step(4)

            def decays(b, p):
                c = Chain(dve, vch, 2 + 7 * b + 4)
                dve.wait_ge(s_lc, 2 * b + 2)
                since(dve, s_lnlam, b)
                for o in range(KC):
                    c.add(v.tensor_scalar(lam[:, o, :], lc[:, o, :], base02[:, o:o + 1], base[:, o:o + 1], ALU.mult, ALU.add))
                c.wait()
                v.tensor_scalar(lam[:, :, :], lam[:, :, :], LAM_MAX, LAM_MIN, ALU.min, ALU.max).then_inc(s_lam, 1)
                dve.wait_ge(s_lnlam, b + 1)
                since(dve, s_dk, b)
                c.add(v.tensor_tensor_scan(G[:, 0, :], ones[:, :], lnlam[:, 0, :], 0.0, ALU.mult, ALU.add))
                v.tensor_tensor_scan(G[:, 1, :], ones[:, :], lnlam[:, 1, :], 0.0, ALU.mult, ALU.add).then_inc(s_G, 1)
                c.wait()
                dve.wait_ge(s_G, b + 1)
                since(dve, s_eq, b)
                Gc = G[:, :, :].rearrange("p c (n t) -> p (c n) t", t=CH)
                v.tensor_tensor(dq[:, :].rearrange("p (n t) -> p n t", t=CH), Gc,
                                Gc[:, :, MIDC:MIDC + 1].to_broadcast([P, KC * NCH, CH]), ALU.subtract).then_inc(s_dq, 1)
                c.step(3)

            def queries(b, p):
                dve.wait_ge(s_eq, b + 1)
                dve.wait_ge(s_q, b + 1)
                since(dve, s_qb1, b)
                v.tensor_tensor(qe[:, :, :].rearrange("p c t -> p (c t)"), bank[1][:, 0:KC * T], eq[:, :], ALU.mult).then_inc(s_qe, 1)
                dve.wait_ge(s_qe, b + 1)
                since(dve, s_aps, 12 * (b - 1))
                v.tensor_tensor(qb[p][:, 0, :, :], qe[:, 0:1, :].to_broadcast([P, HH, T]),
                                hmask[:, :].unsqueeze(2).to_broadcast([P, HH, T]), ALU.mult).then_inc(s_qb0, 1)

            def masked(b, half):
                for n, u in enumerate(MASKED):
                    r, t = UNITS[u]
                    m = min(TT, CH * (r + 1) - TT * t)
                    dve.wait_ge(s_aps, 12 * b + 6 * half + u + 1)
                    if n == 0:
                        since(dve, s_pv, 2 * b + half - 1)
                    settle()
                    v.copy_predicated(asb[half][0:m, t, :, CH * r:CH * (r + 1)],
                                      cmask[0:m, r % 2, :].unsqueeze(1).to_broadcast([m, HH, CH]),
                                      bank[4 + u % 2][0:m, 0:HH * CH].rearrange("p (h c) -> p h c", c=CH)).then_inc(s_adve, 1)

            def residual(b):
                dve.wait_ge(s_ops, b + 1)
                hb = h[:, bass.ds(b * (NT * D), NT * D)]
                v.tensor_tensor(hb, hb, bank[7][0:TT, :], ALU.add).then_inc(s_h1, 1)

            def norm2(b):
                c = Chain(dve, vch2, 4 * b)
                ht = htile(b)
                dve.wait_ge(s_h1, b + 1)
                settle()
                for t in range(NT):
                    c.add(v.bn_stats(st2[:, 6 * t:6 * t + 6], ht[:, t, :]))
                c.wait()
                settle()
                c.add(v.bn_aggr(mv2[:, 0, :], st2[:, 0:6]))
                v.bn_aggr(mv2[:, 1, :], st2[:, 6:12]).then_inc(s_mv2, 1)
                dve.wait_ge(s_rstd2, b + 1)
                since(dve, s_x2Tps, b)
                since(dve, s_x2all, 16 * b)
                c.add(v.tensor_scalar(x2s[:, 0, :], ht[:, 0, :], mv2[:, 0, 0:1], rstd2[:, 0:1], ALU.subtract, ALU.mult))
                v.tensor_scalar(x2s[:, 1, :], ht[:, 1, :], mv2[:, 1, 0:1], rstd2[:, 1:2], ALU.subtract, ALU.mult).then_inc(s_x2, 1)
                c.step(4)

            def logits(b):
                dve.wait_ge(s_lgps, b + 1)
                v.tensor_scalar(lg[:, bass.ds(b * (NT * NE), NT * NE)], bank[7][0:TT, 0:NT * NE], 1.0, None, ALU.mult).then_inc(s_lg, 1)

            def step(b, p, first=False):
                front(b + 1)
                masked(b, 0)
                decays(b + 1, 1 - p)
                masked(b, 1)
                if not first:
                    logits(b - 1)
                queries(b + 1, 1 - p)
                residual(b)
                norm2(b)

            front(0)
            decays(0, 0)
            queries(0, 0)
            step(0, 0, first=True)
            with dve.Fori(0, B // 2 - 1) as i:
                step(2 * i + 1, 1)
                step(2 * i + 2, 0)
            masked(B - 1, 0)
            masked(B - 1, 1)
            logits(B - 2)
            residual(B - 1)
            norm2(B - 1)
            logits(B - 1)

            dve.wait_ge(s_lg, B)
            dve.wait_ge(s_rc, 32)
            c = Chain(dve, rch)
            AX = mybir.AxisListType.X

            def grid(x):
                return x.rearrange("p (i e) -> p i e", e=NE)

            def over(x):
                return x.unsqueeze(2).to_broadcast([TT, BT, NE])

            logit, same, rank, first, rest, second = lg[:, :], rb[:, 0, :], rb[:, 1, :], rb[:, 2, :], rb[:, 3, :], rb[:, 4, :]
            best, bestrank, next_, nextrank = rs[:, 0, :], rs[:, 1, :], rs[:, 2, :], rs[:, 3, :]

            def choose(x, top, toprank, pick):
                c(v.tensor_reduce(top, grid(x), AX, ALU.max))
                c(v.tensor_tensor(grid(same), grid(x), over(top), ALU.is_equal))
                c(v.tensor_tensor(grid(rank), grid(same), desc, ALU.mult))
                c(v.tensor_reduce(toprank, grid(rank), AX, ALU.max))
                c(v.tensor_tensor(grid(pick), desc, over(toprank), ALU.is_equal))

            choose(logit, best, bestrank, first)
            c(v.scalar_tensor_tensor(rest, first, -1e30, logit, ALU.mult, ALU.add))
            choose(rest, next_, nextrank, second)
            v.tensor_tensor(rs[:, 4, :], best, next_, ALU.subtract).then_inc(s_gap, 1)
            v.tensor_tensor(rb[:, 6, :], first, second, ALU.add).then_inc(s_m12, 1)

            def shared_hidden(g, j):
                dve.wait_ge(s_sg, FC * g + j + 1)
                since(dve, s_sdps, 2 * (g - 1))
                v.tensor_tensor(shid[g % 2][:, j, :], sgate[:, j, :], bank[2 * j + 1][:, 0:GN], ALU.mult).then_inc(s_shid, 1)

            shared_hidden(0, 0)
            dve.wait_ge(s_rps, 1)
            tot, cum, before, pos, pick = rb[:, 7, :], rb[:, 8, :], rb[:, 9, :], rb[:, 10, :], rb[:, 11, :]
            eg = lambda x: x.rearrange("p (e i) -> p e i", e=NE)
            flip = lambda x: x.rearrange("p (e i) -> p i e", e=NE)
            c(v.tensor_copy(eg(tot), bank[7][0:TT, 256:256 + BT * NE].rearrange("p (i e) -> p e i", e=NE)))
            c(v.tensor_tensor_scan(cum, fresh, tot, 0.0, ALU.mult, ALU.add))
            c(v.tensor_tensor(before, cum, tot, ALU.subtract))
            c(v.tensor_scalar(r8i[:, 0, :], eg(cum)[:, :, BT - 1], float(SLOTS - 1), None, ALU.add))
            c(v.tensor_scalar(r8i[:, 1, :], r8i[:, 0, :], 7, None, ALU.arith_shift_right))
            c(v.tensor_copy(r8[:, 0, :], r8i[:, 1, :]))
            c(v.tensor_tensor_scan(r8[:, 1, :], ones[0:TT, 0:NE], r8[:, 0, :], 0.0, ALU.mult, ALU.add))
            c(v.tensor_tensor(r8[:, 2, :], r8[:, 1, :], r8[:, 0, :], ALU.subtract))
            c(v.tensor_scalar(r8[:, 3, :], r8[:, 2, :], float(SLOTS), None, ALU.mult))
            c(v.tensor_tensor(eg(before), eg(before), r8[:, 3, :].unsqueeze(2).to_broadcast([TT, NE, BT]), ALU.add))
            c(v.tensor_tensor(grid(pos), grid(bank[7][0:TT, 0:BT * NE]), flip(before), ALU.add))
            for k, choice in enumerate((first, second)):
                c(v.tensor_tensor(pick, choice, pos, ALU.mult))
                c(v.tensor_reduce(slotf[:, k, :], grid(pick), AX, ALU.add))
            v.tensor_copy(slot[:, :, :], slotf[:, :, :]).then_inc(s_slot, 1)
            shared_hidden(0, 1)
            c(v.tensor_tensor(texp[:, :].rearrange("p (j e) -> p j e", e=NE), tileno,
                              r8[:, 1:2, :].to_broadcast([TT, RT, NE]), ALU.is_ge))
            c(v.tensor_reduce(texpf[:, :], texp[:, :].rearrange("p (j e) -> p j e", e=NE), AX, ALU.add))
            v.tensor_scalar(texpi[:, :], texpf[:, :], float(NE - 1), None, ALU.min).then_inc(s_texp, 1)
            shared_hidden(0, 2)
            dve.wait_ge(s_gw, 1)
            c.add(v.tensor_scalar(gatew[:, 0, :], rs[:, 5, :], 0.5, 0.5, ALU.mult, ALU.add))
            c(v.tensor_scalar(gatew[:, 1, :], rs[:, 5, :], -0.5, 0.5, ALU.mult, ALU.add))

            def shared_add(g):
                for q in range(2):
                    dve.wait_ge(s_sdps, 2 * g + q + 1)
                    hb = h[:, (2 * g + q) * NT * D:(2 * g + q + 1) * NT * D]
                    v.tensor_tensor(hb, hb, bank[6 + q][0:TT, :], ALU.add).then_inc(s_hsh, 1)

            for g in range(1, GR):
                for j in range(FC):
                    shared_hidden(g, j)
                shared_add(g - 1)
            shared_add(GR - 1)

            def x_turned(j, p):
                dve.wait_ge(s_xgTps, j + 1)
                since(dve, s_rups, j - 1)
                v.tensor_copy(xgT[p][:, :, :].rearrange("p c n -> p (c n)"), bank[0][:, 0:D]).then_inc(s_xgT, 1)

            def hidden(j, p):
                dve.wait_ge(s_rg, j + 1)
                since(dve, s_rhTps, j - 1)
                v.tensor_tensor(rh[p][:, :], rg[:, :], bank[2 + 2 * p][:, 0:HALF], ALU.mult).then_inc(s_rh, 1)

            def lowered(j, p):
                dve.wait_ge(s_rdps, j + 1)
                since(dve, s_yst[p], 8 * (j - p))
                v.tensor_copy(ry[p][:, :], bank[6][:, 0:D]).then_inc(s_ry, 1)

            x_turned(0, 0)
            x_turned(1, 1)
            hidden(0, 0)
            x_turned(2, 0)
            hidden(1, 1)
            lowered(0, 0)
            for n in range(2):
                x_turned(3 + n, 1 - n)
                hidden(2 + n, n)
                lowered(1 + n, 1 - n)
            with dve.Fori(2, RT // 2 - 1) as i:
                for n in range(2):
                    x_turned(2 * i + n + 1, 1 - n)
                    hidden(2 * i + n, n)
                    lowered(2 * i + n - 1, 1 - n)
            x_turned(RT - 1, 1)
            hidden(RT - 2, 0)
            lowered(RT - 3, 1)
            hidden(RT - 1, 1)
            lowered(RT - 2, 0)
            lowered(RT - 1, 1)

            def combine(b, p):
                c = Chain(dve, cch, 3 * b)
                dve.wait_ge(s_yg[p], 32 * (b - p) + 64)
                for k in range(TOPK):
                    for t in range(NT):
                        hb = h[:, bass.ds(b * (NT * D) + t * D, D)]
                        ins = v.scalar_tensor_tensor(hb, yg[p][:, t, k, :], gatew[:, k, bass.ds(b * NT + t, 1)], hb,
                                                     ALU.mult, ALU.add)
                        if k == 0 or t == 0:
                            c.add(ins)
                    if k == 0:
                        c.wait()
                ins.then_inc(s_comb, 1)
                c.step(3)

            def stats(b, chain, done, st_, mv_, src):
                c = Chain(dve, chain, 4 * b)
                ht = htile(b)
                dve.wait_ge(src, b + 1)
                settle()
                for t in range(NT):
                    c.add(v.bn_stats(st_[:, 6 * t:6 * t + 6], ht[:, t, :]))
                c.wait()
                settle()
                c.add(v.bn_aggr(mv_[:, 0, :], st_[:, 0:6]))
                v.bn_aggr(mv_[:, 1, :], st_[:, 6:12]).then_inc(done, 1)
                c.step(3)

            def normed(b, chain, done, mv_, rstd_, dst):
                c = Chain(dve, chain, 4 * b + 3)
                ht = htile(b)
                c.add(v.tensor_scalar(dst[:, 0, :], ht[:, 0, :], mv_[:, 0, 0:1], rstd_[:, 0:1], ALU.subtract, ALU.mult))
                v.tensor_scalar(dst[:, 1, :], ht[:, 1, :], mv_[:, 1, 0:1], rstd_[:, 1:2], ALU.subtract, ALU.mult).then_inc(done, 1)

            def values1(b, p):
                dve.wait_ge(s_v1ps, b + 1)
                since(dve, s_pv1, 2 * (b - 1))
                for par in range(2):
                    src = bank[3][0:TT, :].rearrange("p (i j d) -> p i j d", j=2, d=HD)
                    dst = vz[p][par][0:TT, :, :, :, :].rearrange("p t i j d -> p (t i) j d")
                    for t in range(NT):
                        ins = v.tensor_tensor(dst[:, 8 * t:8 * t + 8, par, :], src[:, 8 * t:8 * t + 8, par, :],
                                              rows1[:, 0, :].rearrange("p (i j d) -> p i j d", j=2, d=HD)[:, :, par, :], ALU.add)
                        if par == 0 or t == 0:
                            ins.then_inc(v1chx, 1)
                ins.then_inc(s_v1, 1)

            def least(b, u):
                half, t, n, w = UNITS1[u]
                dve.wait_ge(s_sps, NU1 * b + u + 1)
                since(dve, s_ptps, NU1 * b + u - 3)
                settle()
                for i in range(w):
                    col = t * HEADS + half * HH + n + i
                    ins = v.tensor_tensor_reduce(out=ring[u % 4][0:TT, i, :], in0=bank[4 + u % 2][0:TT, i * T:(i + 1) * T],
                                                 in1=fade[t][:, half * HH + n + i, :], scale=1.0, scalar=3e38,
                                                 op0=ALU.add, op1=ALU.min, accum_out=mn[:, col:col + 1])
                ins.then_inc(s_min, 1)

            def probs_turned(b, u):
                half, t, n, w = UNITS1[u]
                dve.wait_ge(s_ptps, NU1 * b + u + 1)
                if u % (NU1 // 2) == 0:
                    since(dve, s_pv1, 2 * b + half - 1)
                v.tensor_copy(pT[half][0:TT, :, n:n + w, t * TT:(t + 1) * TT],
                              bank[6 + u % 2][0:TT, 0:NT * w * TT].rearrange("p (k h q) -> p k h q", k=NT, h=w)).then_inc(s_pt, 1)

            def routed4(b):
                dve.wait_ge(s_lg4ps, b + 1)
                v.tensor_scalar(lg[:, bass.ds(b * (NT * NE), NT * NE)], bank[0][0:TT, 0:NT * NE], 1.0, None, ALU.mult).then_inc(s_lg4, 1)

            def step1(b, p, first=False, final=False):
                for u in range(NU1):
                    least(b, u)
                    if u == 1 and not final:
                        combine(b + 1, 1 - p)
                        stats(b + 1, v1ch, s_mv1, st, mv, s_comb)
                    if u == 4 and not final:
                        dve.wait_ge(s_rstd1, b + 2)
                        since(dve, s_xT1ps, b + 1)
                        normed(b + 1, v1ch, s_xn1, mv, rstd, xn)
                    if u >= 3:
                        probs_turned(b, u - 3)
                if not first:
                    routed4(b - 1)
                probs_turned(b, NU1 - 3)
                if not final:
                    values1(b + 1, 1 - p)
                probs_turned(b, NU1 - 2)
                probs_turned(b, NU1 - 1)
                dve.wait_ge(s_p, NU1 * (b + 1))
                v.reciprocal(rinv[:, :, :].rearrange("p t h -> p (t h)"), rsum[:, :]).then_inc(s_rinv, 1)
                dve.wait_ge(s_rinv, b + 1)
                since(dve, s_rbps, b)
                v.tensor_copy(rspread[0:TT, :, :].rearrange("p t (h d) -> p (t h) d", d=HD),
                              rinv[:, :, :].rearrange("p t h -> p (t h)").unsqueeze(2).to_broadcast([TT, NT * HEADS, HD])).then_inc(s_rspread, 1)
                dve.wait_ge(s_rbs, b + 1)
                dve.wait_ge(s_pv1, 2 * b + 2)
                since(dve, s_o1ps, b)
                v.tensor_tensor(yT[:, :, :].rearrange("p c t -> p (c t)"), bank[1][:, 0:KC * T],
                                rbs[:, :, :].rearrange("p c t -> p (c t)"), ALU.mult).then_inc(s_y1, 1)
                dve.wait_ge(s_o1ps, b + 1)
                dve.wait_ge(s_hb, b + 1)
                hb = h[:, bass.ds(b * (NT * D), NT * D)]
                v.tensor_tensor(hb, hb, bank[3][0:TT, :], ALU.add).then_inc(s_h3, 1)
                stats(b, v4ch, s_mv4, st2, mv2, s_h3)
                dve.wait_ge(s_rstd4, b + 1)
                since(dve, s_x4Tps, b)
                normed(b, v4ch, s_x4, mv2, rstd2, x2s)

            dve.wait_ge(s_fade, 2)
            combine(0, 0)
            stats(0, v1ch, s_mv1, st, mv, s_comb)
            dve.wait_ge(s_rstd1, 1)
            normed(0, v1ch, s_xn1, mv, rstd, xn)
            values1(0, 0)
            step1(0, 0, first=True)
            with dve.Fori(0, B // 2 - 1) as i:
                step1(2 * i + 1, 1)
                step1(2 * i + 2, 0)
            step1(B - 1, 1, final=True)
            routed4(B - 1)

            dve.wait_ge(s_lg4, B)
            c = Chain(dve, cch2)
            x, e1, pr = rb[:, 0, :], rb[:, 1, :], rb[:, 5, :]
            c(v.tensor_reduce(rs[:, 0, :], grid(lg[:, :]), AX, ALU.max))
            v.tensor_tensor(grid(x), grid(lg[:, :]), over(rs[:, 0, :]), ALU.subtract).then_inc(s_rx, 1)
            dve.wait_ge(s_rexp, 1)
            c(v.tensor_reduce(rs[:, 1, :], grid(e1), AX, ALU.add))
            c(v.reciprocal(rs[:, 2, :], rs[:, 1, :]))
            c(v.tensor_tensor(grid(pr), grid(e1), over(rs[:, 2, :]), ALU.mult))
            top1, top2 = rs[:, 4, :], rs[:, 6, :]
            choose(pr, top1, rs[:, 3, :], rb[:, 2, :])
            c(v.scalar_tensor_tensor(rb[:, 3, :], rb[:, 2, :], -1e30, pr, ALU.mult, ALU.add))
            c(v.tensor_reduce(top2, grid(rb[:, 3, :]), AX, ALU.max))
            c(v.tensor_tensor(rs[:, 1, :], top1, top2, ALU.add))
            c(v.reciprocal(rs[:, 2, :], rs[:, 1, :]))
            c(v.tensor_tensor(rs[:, 0, :], top1, rs[:, 2, :], ALU.mult))
            c(v.tensor_tensor(rs[:, 3, :], top2, rs[:, 2, :], ALU.mult))
            c(v.tensor_tensor(cs[:, :], rs[:, 0, :], rs[:, 3, :], ALU.add))

            for g in range(GR):
                for q in range(2):
                    b = 2 * g + q
                    dve.wait_ge(s_fdps, b + 1)
                    v.tensor_tensor(ftmp[:, :].rearrange("p (t d) -> p t d", t=NT),
                                    bank[6 + q][0:TT, :].rearrange("p (t d) -> p t d", t=NT),
                                    rows1[:, 2:3, :].to_broadcast([TT, NT, D]), ALU.add).then_inc(s_ft, 1)
                    dve.wait_ge(s_ft, b + 1)
                    for t in range(NT):
                        i = NT * b + t
                        hb = h[:, i * D:(i + 1) * D]
                        ins = v.scalar_tensor_tensor(hb, ftmp[:, t * D:(t + 1) * D], cs[:, i:i + 1], hb, ALU.mult, ALU.add)
                        if t == 0:
                            c.add(ins)
                        else:
                            ins.then_inc(s_h4, 1)
                    dve.wait_ge(s_h4, b + 1)
                    c.wait()

        @block.gpsimd
        def _(pool):
            g = nc.gpsimd
            g.memset(EPSC[:, :], EPS).then_inc(gch, 1)
            for i in range(2):
                g.memset(asb[i][:, :, :, :], 0.0).then_inc(gch, 1)
                for par in range(2):
                    g.memset(vz[i][par][:, :, :, :, :], 0.0).then_inc(gch, 1)
            pool.wait_ge(gch, 7)
            pool.sem_inc(s_zero, 1)
            g.memset(zero[:, :], 0.0).then_inc(s_zset, 1)
            pool.wait_ge(s_const, 48)

            def keys(b, p):
                c = Chain(pool, gch, 7 + 6 * b)
                pool.wait_ge(s_G, b + 1)
                since(pool, s_ek, b)
                for r in range(NCH):
                    n = CH * (r + 1)
                    m = CH * r + MIDC
                    ins = g.tensor_tensor(dk[:, :, COFF[r]:COFF[r] + n], G[:, :, m:m + 1].to_broadcast([P, KC, n]),
                                          G[:, :, 0:n], ALU.subtract)
                    if r < NCH - 1:
                        c.add(ins)
                ins.then_inc(s_dk, 1)
                pool.wait_ge(s_ek, b + 1)
                pool.wait_ge(s_ksb, b + 1)
                since(pool, s_aps, 12 * (b - 1))
                for r in range(NCH):
                    n = CH * (r + 1)
                    ins = g.tensor_tensor(kr[p][:, :, COFF[r]:COFF[r] + n], ek[:, :, COFF[r]:COFF[r] + n],
                                          ksb[:, :, 0:n], ALU.mult)
                    if r < NCH - 1:
                        c.add(ins)
                ins.then_inc(s_kr, 1)
                pool.wait_ge(s_qe, b + 1)
                g.tensor_tensor(qb[p][:, 1, :, :], qe[:, 1:2, :].to_broadcast([P, HH, T]),
                                hmask[:, :].unsqueeze(2).to_broadcast([P, HH, T]), ALU.mult).then_inc(s_qb1, 1)
                c.step(6)

            keys(0, 0)
            keys(1, 1)
            with pool.Fori(1, B // 2) as i:
                keys(2 * i, 0)
                keys(2 * i + 1, 1)

            pool.wait_ge(s_zdone, 16 * (RT // 4))
            pool.wait_ge(s_x2all, 16 * B)
            pool.wait_ge(s_slot, 1)
            for i in range(BT):
                for k in range(TOPK):
                    g.indirect_dma_start(xs_dram, bass.IndirectOffsetOnAxis(ap=slot[:, k, i:i + 1], axis=0),
                                         x2[:, i * D:(i + 1) * D], None).then_inc(s_scat, 16)
            pool.wait_ge(s_hsh, 2 * GR)
            pool.wait_ge(s_alpha, 1)
            pool.wait_ge(s_l1c, 16 * 6)
            for t in range(NT):
                g.tensor_tensor(fade[t], dist[:, t:t + 1, :].to_broadcast([TT, HEADS, T]),
                                alpha[:, :].unsqueeze(2).to_broadcast([TT, HEADS, T]), ALU.mult).then_inc(s_fade, 1)

            def gather(b):
                since(pool, s_comb, b - 1)
                for t in range(NT):
                    for k in range(TOPK):
                        g.indirect_dma_start(yg[b % 2][:, t, k, :], None, ys_dram,
                                             bass.IndirectOffsetOnAxis(ap=slot[:, k, NT * b + t:NT * b + t + 1], axis=0)
                                             ).then_inc(s_yg[b % 2], 16)

            for p in range(2):
                pool.wait_ge(s_yst[p], 16 * (RT // 2))
            gather(0)
            gather(1)
            pool.wait_ge(s_fade, 2)
            for half in range(2):
                g.memset(pT[half][64:P, :, :, :], 0.0).then_inc(g1ch, 1)
            pool.wait_ge(g1ch, 2)
            pool.sem_inc(s_pz, 1)
            for b in range(B):
                p = b % 2
                pool.wait_ge(s_k1, b + 1)
                since(pool, s_sps, NU1 * (b - 1))
                for half in range(KC):
                    g.tensor_tensor(kb[p][:, half, :, :], ksb1[:, half:half + 1, :].to_broadcast([P, HH, T]),
                                    hmask[:, :].unsqueeze(2).to_broadcast([P, HH, T]), ALU.mult).then_inc(s_kb, 1)
                hb = h[:, b * NT * D:(b + 1) * NT * D].rearrange("p (t d) -> p t d", t=NT)
                pool.wait_ge(s_xn1, b + 1)
                g.tensor_tensor(hb, hb, rows1[:, 1:2, :].to_broadcast([TT, NT, D]), ALU.add).then_inc(s_hb, 1)
                if b + 2 < B:
                    gather(b + 2)


def laid_out(inputs):
    import numpy as np
    f = {k: np.asarray(v) for k, v in inputs.items()}

    def rows(w):
        return np.ascontiguousarray(w.reshape(-1, P, w.shape[-1]).transpose(1, 0, 2))

    def column(v, rep=1):
        return np.ascontiguousarray(np.repeat(v, rep).reshape(-1, P).T)

    o = {}
    x = f["x"].reshape(B, 3, 6, 16, 6, 16).transpose(0, 1, 3, 5, 2, 4).reshape(B * IMG, PC * P)
    o["patches"] = rows(x.T)
    o["tok_w"] = rows(f["L0_tok_W"])
    o["txt"] = f["txt"]
    o["ident"] = np.eye(P, dtype=np.float32)
    o["hmask"] = (np.arange(P)[:, None] // HD == np.arange(HH)[None]).astype(np.float32)
    k, q = np.arange(TT)[:, None, None], np.arange(CH)[None, None]
    o["cmask"] = (k <= q + CH * np.arange(2)[None, :, None]).astype(np.int32)
    for n, s in (("wq", "q_w"), ("wk", "k_w"), ("wv", "v_w"), ("wo", "o_w"), ("cw1", "cs_w1")):
        o[n] = rows(f["L0_attn_" + s].T)
    o["cb1"] = f["L0_attn_cs_b1"].reshape(64, 1)
    o["cw2"] = np.ascontiguousarray(np.repeat(f["L0_attn_cs_w2"].T, HD, axis=1))
    o["cb2"] = column(f["L0_attn_cs_b2"], HD)
    o["dec"] = column(f["L0_attn_decay_params"].reshape(-1))
    up = f["L0_ffn_w_up"].transpose(2, 0, 1)
    o["eup"] = rows(up.reshape(D, NE * 2 * HALF))
    o["edn"] = rows(f["L0_ffn_w_down"].transpose(2, 0, 1).reshape(HALF, NE * D))
    o["sup"] = rows(np.concatenate([f["L0_ffn_sg_gate"].T, f["L0_ffn_sg_up"].T], axis=1))
    o["sdn"] = rows(f["L0_ffn_sg_down"].T)
    o["gw"] = rows(f["L0_ffn_gate_w"].T)
    o["tri"] = np.triu(np.ones((TT, TT), np.float32), 1)
    o["rc"] = np.ascontiguousarray(np.broadcast_to(np.concatenate([
        np.tile(NE - np.arange(NE), BT), np.tile(np.arange(BT) > 0, NE),
        np.repeat(np.arange(RT), NE), np.arange(NE)]).astype(np.float32), (TT, 2 * BT * NE + RT * NE + NE)))
    qkv = f["L1_attn_qkv_w"].T
    for n, w in (("wq1", qkv[:, 0:D]), ("wk1", qkv[:, D:2 * D]), ("wv1", qkv[:, 2 * D:]), ("wo1", f["L1_attn_out_w"].T),
                 ("rw", f["L1_ffn_router_w"]), ("w1", f["L1_ffn_w1"]), ("w2", f["L1_ffn_w2"])):
        o[n] = rows(w)
    qkv_b = f["L1_attn_qkv_b"]
    o["qkb"] = np.ascontiguousarray(np.stack([column(qkv_b[0:D]), column(qkv_b[D:2 * D])], axis=1))
    o["b1"] = column(f["L1_ffn_b1"])
    o["rows1"] = np.ascontiguousarray(np.broadcast_to(
        np.stack([qkv_b[2 * D:], f["L1_attn_out_b"], f["L1_ffn_b2"]]), (TT, 3, D)))
    o["alpha"] = np.ascontiguousarray(np.broadcast_to(f["L1_attn_decay_alpha"], (TT, HEADS)))
    pos = np.arange(T, dtype=np.float32)
    o["dist"] = np.ascontiguousarray(np.abs(pos.reshape(NT, TT, 1) - pos).transpose(1, 0, 2))
    return o


OUT_SHAPE = (B, T, D)


def kernel(**inputs):
    import numpy as np
    import concourse.bacc as bacc
    from concourse.bass_utils import run_bass_kernel_spmd

    nc = bacc.Bacc("TRN2", target_bir_lowering=False, num_devices=1)
    arrays = laid_out(inputs)
    aps = {n: nc.dram_tensor("in_" + n, x.shape, mybir.dt.from_np(x.dtype), kind="ExternalInput").ap()
           for n, x in arrays.items()}
    out = nc.dram_tensor("out", OUT_SHAPE, mybir.dt.float32, kind="ExternalOutput").ap()
    early_fusion_kernel(nc, aps, out)
    r = run_bass_kernel_spmd(nc, [{"in_" + n: x for n, x in arrays.items()}], core_ids=[0])
    return r.results[0]["out"]
```

```python
import concourse.bass as bass
from concourse import mybir
from contextlib import ExitStack

B, T, D = 8, 164, 256
IMG, TXT = 36, 128
P = 128
KC = D // P
NT = 2
TT = T // NT
HEADS, HD = 16, 16
HH = HEADS // KC
PC = 6
CH = 41
NCH = T // CH
COFF = [CH * r * (r + 1) // 2 for r in range(NCH + 1)]
KW = COFF[NCH]
MIDC = CH // 2
BT = B * NT
LAM_MIN, LAM_MAX = 0.02, 0.9995
NE, TOPK, HALF = 8, 2, 384
FC = HALF // P
FF = 1024
FFC = FF // P
GR = 4
GN = B * T // GR
SLOTS = P
RT = (TOPK * B * T + NE * (SLOTS - 1)) // SLOTS
SCALE = 4.0
EPS = 1e-5


class Chain:

    def __init__(self, eng, sem, base=0):
        self.eng, self.sem, self.base, self.n = eng, sem, base, 0

    def add(self, ins):
        ins.then_inc(self.sem, 1)
        self.n += 1

    def wait(self):
        self.eng.wait_ge(self.sem, self.base + self.n)

    def __call__(self, ins):
        self.add(ins)
        self.wait()

    def step(self, n):
        assert self.n == n, (self.n, n)


def early_fusion_kernel(nc, a, out):
    f32, i32, u32 = mybir.dt.float32, mybir.dt.int32, mybir.dt.uint32
    ALU = mybir.AluOpType
    ACT = mybir.ActivationFunctionType

    ctx = ExitStack()
    with ctx:
        def sb(name, shape, dt=f32):
            return ctx.enter_context(nc.sbuf_tensor(name, shape, dt))

        def sem(name):
            return ctx.enter_context(nc.semaphore(name))

        bank = [ctx.enter_context(nc.psum_tensor(f"bank{i}", [P, 512], f32)) for i in range(8)]

        h = sb("h", [TT, B * NT * D])
        h4 = h[:, :].rearrange("p (b t d) -> p b t d", b=B, t=NT)
        ident = sb("ident", [P, P])
        hmask = sb("hmask", [P, HH])
        cmask = sb("cmask", [TT, 2, CH], i32)
        ones = sb("ones", [P, T])
        EPSC = sb("eps_column", [P, 1])
        tok = sb("tok", [3 * IMG, 3, D])
        wq = sb("wq", [P, KC, D])
        wk = sb("wk", [P, KC, D])
        wv = sb("wv", [P, KC, D])
        wo = sb("wo", [P, KC, D])
        cw1 = sb("cw1", [P, KC, 64])
        cb1 = sb("cb1", [64, 1])
        cw2 = sb("cw2", [64, D])
        cb2 = sb("cb2", [P, KC])
        dec = sb("dec", [P, KC])
        base = sb("base", [P, KC])
        base02 = sb("base02", [P, KC])
        eup = sb("eup", [P, KC, NE * 2 * HALF])
        flat = eup[:, :, :].rearrange("p c n -> p (c n)")
        used = [0]

        def carve(*shape):
            n = 1
            for x in shape:
                n *= x
            v = flat[:, used[0]:used[0] + n]
            used[0] += n
            assert used[0] <= KC * NE * 2 * HALF
            if len(shape) == 2:
                v = v.rearrange("p (a b) -> p a b", a=shape[0])
            elif len(shape) == 3:
                v = v.rearrange("p (a b c) -> p a b c", a=shape[0], b=shape[1])
            return v

        st = sb("st", [TT, NT * 6])
        mv = sb("mv", [TT, NT, 2])
        lnv = sb("lnv", [TT, NT])
        rstd = sb("rstd", [TT, NT])
        xn = sb("xn", [TT, NT, D])
        xnT = sb("xnT", [P, KC, T])
        th = sb("th", [64, T])
        lc = carve(KC, T)
        lam = carve(KC, T)
        lnlam = carve(KC, T)
        G = carve(KC, T)
        dq = carve(KC * T)
        dk = carve(KC, KW)
        eq = carve(KC * T)
        ek = carve(KC, KW)
        ksb = carve(KC, T)
        qe = carve(KC, T)
        kr = [carve(KC, KW) for i in range(2)]
        qb = [sb(f"qb{i}", [P, KC, HH, T]) for i in range(2)]
        spare = [qb[i][:, :, :, :].rearrange("p c h t -> p (c h t)") for i in range(2)]
        xp = spare[0][:, 0:PC * B * IMG].rearrange("p (c n) -> p c n", c=PC)
        tokw = spare[1][:, 0:PC * D].rearrange("p (c n) -> p c n", c=PC)
        sgate = spare[0][:, 0:FC * GN].rearrange("p (j n) -> p j n", j=FC)
        shid = [spare[i][:, FC * GN:2 * FC * GN].rearrange("p (j n) -> p j n", j=FC) for i in range(2)]
        vz = [[sb(f"vz{i}_{par}", [P, NT, HEADS // 2, 2, HD]) for par in range(2)] for i in range(2)]
        asb = [carve(NT, HH, T) for i in range(2)]
        yT = sb("yT", [P, KC, T])

        shared_w = sb("shared_w", [P, KC * 2 * HALF + FC * D])
        sup = shared_w[:, 0:KC * 2 * HALF].rearrange("p (c n) -> p c n", c=KC)
        sdn = shared_w[:, KC * 2 * HALF:].rearrange("p (j n) -> p j n", j=FC)
        edn = sb("edn", [P, FC, NE * D])
        gw = sb("gw", [P, KC, NE])
        st2 = sb("st2", [TT, NT * 6])
        mv2 = sb("mv2", [TT, NT, 2])
        lnv2 = sb("lnv2", [TT, NT])
        rstd2 = sb("rstd2", [TT, NT])
        x2s = sb("x2s", [TT, NT, D])
        x2Ts = sb("x2Ts", [P, KC, T])
        x2w = sb("x2w", [P, BT * D])
        x2 = x2w[0:TT, :]
        w1 = x2w[:, 0:KC * FF].rearrange("p (c n) -> p c n", c=KC)
        w2 = x2w[:, KC * FF:KC * FF + FFC * D].rearrange("p (j n) -> p j n", j=FFC)
        x2T = sb("x2T", [P, KC, B * T])
        tri = sb("tri", [TT, TT])
        rc = sb("rc", [TT, BT * NE + BT * NE + RT * NE + NE])
        desc = rc[:, 0:BT * NE].rearrange("p (i e) -> p i e", e=NE)
        fresh = rc[:, BT * NE:2 * BT * NE]
        tileno = rc[:, 2 * BT * NE:2 * BT * NE + RT * NE].rearrange("p (j e) -> p j e", e=NE)
        lg = sb("lg", [TT, BT * NE])
        rb = sb("rb", [TT, 12, BT * NE])
        rs = sb("rs", [TT, 8, BT])
        r8 = sb("r8", [TT, 6, NE])
        r8i = sb("r8i", [TT, 2, NE], i32)
        slotf = sb("slotf", [TT, TOPK, BT])
        slot = sb("slot", [TT, TOPK, BT], u32)
        gatew = sb("gatew", [TT, TOPK, BT])
        texp = sb("texp", [TT, RT * NE])
        texpf = sb("texpf", [TT, RT])
        texpi = sb("texpi", [TT, RT], i32)
        zero = x2T[:, :, :].rearrange("p c n -> p (c n)")[:, 0:1024]
        xg = [sb(f"xg{i}", [P, D]) for i in range(2)]
        xgT = [sb(f"xgT{i}", [P, KC, P]) for i in range(2)]
        rg = sb("rg", [P, HALF])
        rh = [sb(f"rh{i}", [P, HALF]) for i in range(2)]
        rhT = [sb("rhT0", [P, FC, P])]
        rhT.append(x2T[:, 0, 0:FC * P].rearrange("p (k n) -> p k n", k=FC))
        ry = [sb(f"ry{i}", [P, D]) for i in range(2)]
        yg = [shared_w[0:TT, i * NT * TOPK * D:(i + 1) * NT * TOPK * D].rearrange("p (t k d) -> p t k d", t=NT, k=TOPK) for i in range(2)]
        used[0] = 0
        pT = [carve(NT, HH, T) for i in range(2)]
        ring = [carve(3, T) for i in range(4)]
        q1 = [carve(KC, T) for i in range(2)]
        ksb1 = carve(KC, T)
        rbs = carve(KC, T)
        rspread = carve(NT, D)
        hid = [carve(FFC, GN)]
        ednf = edn[:, :, :].rearrange("p j n -> p (j n)")
        kb = [ednf[:, i * KC * HH * T:(i + 1) * KC * HH * T].rearrange("p (c h t) -> p c h t", c=KC, h=HH) for i in range(2)]
        hid.append(ednf[:, 0:FFC * GN].rearrange("p (j n) -> p j n", j=FFC))
        fade = [spare[i][0:TT, :].rearrange("p (h t) -> p h t", h=HEADS) for i in range(2)]
        dist = sb("dist", [TT, NT, T])
        arow = sb("arow", [TT, HEADS])
        aabs = sb("aabs", [TT, 2, HEADS])
        alpha = sb("alpha", [TT, HEADS])
        rows1 = sb("rows1", [TT, 3, D])
        qkb = sb("qkb", [P, 2, KC])
        nqb = sb("nqb", [P, KC])
        b1c = sb("b1c", [P, FFC])
        rw = sb("rw", [P, KC, NE])
        mn = sb("mn", [TT, NT * HEADS])
        rsum = [sb(f"rsum{i}", [TT, NT * HEADS]) for i in range(2)]
        rinv = sb("rinv", [TT, NT, HEADS])
        ftmp = sb("ftmp", [TT, NT * D])
        cs = sb("cs", [TT, BT])

        s_l1c, s_w1in, s_wff = sem("l1_const_in"), sem("l1_weights_in"), sem("ff_weights_in")
        s_al, s_alpha, s_fade, s_nqb, s_pz = sem("alpha_parts"), sem("alpha"), sem("fade"), sem("nqb"), sem("pT_zeroed")
        v1ch, a1ch, g1ch, v4ch, a4ch, cch2, v1chx = [sem(n) for n in ("dve_chain_l1", "act_chain_l1", "pool_chain_l1", "dve_chain_n4", "act_chain_n4", "router_chain", "values1_chain")]
        s_mv1, s_rstd1, s_xn1, s_xT1ps, s_xT1 = [sem(n) for n in ("mv1", "rstd1", "xn1", "xT1_ps", "xT1_sb")]
        s_q1ps, s_k1ps, s_v1ps, s_q1, s_k1, s_v1, s_kb, s_hb = [sem(n) for n in ("q1_ps", "k1_ps", "v1_ps", "q1_sb", "k1_sb", "v1_sb", "k1_masked", "h_biased")]
        s_sps, s_min, s_p, s_ptps, s_pv1 = [sem(n) for n in ("logits1_ps", "logits1_sb", "probs", "probsT_ps", "pv1_ps")]
        s_pt = [sem(f"probsT_sb{i}") for i in range(2)]
        s_rspread = sem("rinv_spread")
        s_rinv, s_rbps, s_rbs, s_y1, s_o1ps, s_h3 = [sem(n) for n in ("rinv", "rb_ps", "rb_sb", "y1_sb", "o1_ps", "h_attn1")]
        s_mv4, s_rstd4, s_x4, s_x4Tps, s_x4T, s_lg4ps, s_lg4, s_x4Tall = [sem(n) for n in ("mv4", "rstd4", "x4", "x4T_ps", "x4T_sb", "router_ps", "router_sb", "x4T_all")]
        s_fups, s_hid, s_fdps, s_ft, s_h4, s_rexp, s_rx = [sem(n) for n in ("ff_up_ps", "ff_hidden", "ff_down_ps", "ff_biased", "h_final", "router_exp", "router_shifted")]

        xs_dram = nc.dram_tensor("routed_in", (RT * SLOTS, D), f32, kind="Internal").ap()
        ys_dram = nc.dram_tensor("routed_out", (RT * SLOTS, D), f32, kind="Internal").ap()

        s_rc, s_wf, s_zset, s_zdone = sem("routing_const_in"), sem("wf_in"), sem("zero_set"), sem("slots_zeroed")
        s_mv2, s_rstd2, s_x2 = sem("mv2_ready"), sem("rstd2_ready"), sem("x2_ready")
        s_x2Tps, s_x2T, s_lgps, s_lg = sem("x2T_ps"), sem("x2T_sb"), sem("logits_ps"), sem("logits_sb")
        s_x2all, s_x2Tall = sem("x2_all"), sem("x2T_all")
        vch2, ach2, rch = sem("dve_chain2"), sem("act_chain2"), sem("routing_chain")
        s_gap, s_gw, s_m12, s_rps = sem("logit_gap"), sem("tanh_gap"), sem("choices"), sem("prefix_ps")
        s_slot, s_texp, s_eup = sem("slots_known"), sem("tile_experts"), sem("eup_in")
        s_scat, s_xg = sem("scattered"), [sem(f"xg_in{i}") for i in range(2)]
        s_sups, s_sg, s_shid, s_sdps, s_hsh = sem("shared_up_ps"), sem("shared_gate_sb"), sem("shared_hidden"), sem("shared_down_ps"), sem("h_shared")
        s_xgTps, s_xgT, s_rups, s_rg, s_rh = sem("xgT_ps"), sem("xgT_sb"), sem("routed_up_ps"), sem("routed_gate_sb"), sem("routed_hidden")
        s_rhTps, s_rhT, s_rdps, s_ry, s_yst = sem("rhT_ps"), sem("rhT_sb"), sem("routed_down_ps"), sem("routed_y_sb"), [sem(f"routed_stored{i}") for i in range(2)]
        s_yg = [sem(f"gathered{i}") for i in range(2)]
        s_comb, cch = sem("combined"), sem("combine_chain")

        s_const, s_tokin, s_txt, s_w0 = sem("const_in"), sem("tok_in"), sem("txt_in"), sem("w0_in")
        s_ones = sem("ones_set")
        s_zero = sem("zeros_set")
        s_tokps, s_toksb, s_tokh = sem("tok_ps"), sem("tok_sb"), sem("tok_in_h")
        s_base = sem("base_ready")
        vch, ach, gch = sem("dve_chain"), sem("act_chain"), sem("pool_chain")
        s_mv, s_rstd, s_xn = sem("mv_ready"), sem("rstd_ready"), sem("xn_ready")
        s_xTps, s_xT = sem("xT_ps"), sem("xT_sb")
        s_z1, s_q, s_k, s_v = sem("z1_ps"), sem("q_ps"), sem("k_ps"), sem("v_ps")
        s_th, s_z2, s_lc = sem("tanh_sb"), sem("z2_ps"), sem("lc_sb")
        s_lam, s_lnlam, s_G = sem("lam_sb"), sem("lnlam_sb"), sem("G_sb")
        s_dq, s_dk, s_eq, s_ek = sem("dq_sb"), sem("dk_sb"), sem("eq_sb"), sem("ek_sb")
        s_ksb, s_vsb, s_qe, s_kr = sem("k_sb"), sem("v_sb"), sem("qe_sb"), sem("kr_sb")
        s_qb0, s_qb1 = sem("qb_half0"), sem("qb_half1")
        s_aps, s_adve, s_aact, s_pv = sem("scores_ps"), sem("scores_dve"), sem("scores_act"), sem("pv_ps")
        s_ysb, s_ops, s_h1 = sem("y_sb"), sem("o_ps"), sem("h_attn0")
        s_settled = sem("dve_waits_met")
        s_out = sem("out_done")

        UNITS = [(0, 0), (1, 0), (2, 0), (2, 1), (3, 0), (3, 1)]
        MASKED = [0, 1, 3, 5]
        PLAIN = [2, 4]
        UNITS1 = [(half, t, n, min(3, HH - n)) for half in range(KC) for t in range(NT) for n in range(0, HH, 3)]
        NU1 = len(UNITS1)

        def since(eng, s, v):
            if not isinstance(v, int) or v > 0:
                eng.wait_ge(s, v)

        def htile(b):
            return h[:, bass.ds(b * (NT * D), NT * D)].rearrange("p (t d) -> p t d", t=NT)

        block = ctx.enter_context(nc.Block())

        @block.sync
        def _(sp):
            sp.dma_start(xp[:, :, :], a["patches"]).then_inc(s_tokin, 16)
            sp.dma_start(tokw[:, :, :], a["tok_w"]).then_inc(s_tokin, 16)
            sp.dma_start(h4[IMG:TT, :, 0, :], a["txt"][:, 0:TT - IMG, :].rearrange("b p d -> p b d")).then_inc(s_txt, 16)
            sp.dma_start(h4[:, :, 1, :], a["txt"][:, TT - IMG:TXT, :].rearrange("b p d -> p b d")).then_inc(s_txt, 16)
            for dst, src in ((ident, "ident"), (hmask, "hmask")):
                sp.dma_start(dst[:, :], a[src]).then_inc(s_const, 16)
            sp.dma_start(cmask[:, :, :], a["cmask"]).then_inc(s_const, 16)
            for dst, src in ((wq, "wq"), (wk, "wk"), (wv, "wv"), (wo, "wo"), (cw1, "cw1"), (gw, "gw")):
                sp.dma_start(dst[:, :, :], a[src]).then_inc(s_w0, 16)
            for dst, src in ((cb1, "cb1"), (cw2, "cw2"), (cb2, "cb2"), (dec, "dec")):
                sp.dma_start(dst[:, :], a[src]).then_inc(s_w0, 16)
            for dst, src in ((arow, "alpha"), (b1c, "b1")):
                sp.dma_start(dst[:, :], a[src]).then_inc(s_l1c, 16)
            for dst, src in ((dist, "dist"), (rows1, "rows1"), (qkb, "qkb"), (rw, "rw")):
                sp.dma_start(dst[:, :, :], a[src]).then_inc(s_l1c, 16)
            for b in range(B):
                i, j = divmod(b, 3)
                sp.wait_ge(s_toksb, i + 1)
                sp.dma_start(h4[0:IMG, b, 0, :], tok[IMG * j:IMG * j + IMG, i, :]).then_inc(s_tokh, 16)
            for dst, src in ((tri, "tri"), (rc, "rc")):
                sp.dma_start(dst[:, :], a[src]).then_inc(s_rc, 16)
            for dst, src in ((sup, "sup"), (sdn, "sdn"), (edn[:, :, :], "edn")):
                sp.dma_start(dst, a[src]).then_inc(s_wf, 16)
            sp.wait_ge(s_zset, 1)
            for n in range(RT // 4):
                sp.dma_start(xs_dram[4 * n * SLOTS:4 * (n + 1) * SLOTS, :].rearrange("(p k) d -> p (k d)", p=P),
                             zero[:, :]).then_inc(s_zdone, 16)
            sp.wait_ge(s_zdone, 16 * (RT // 4))
            with sp.Fori(0, B) as b:
                sp.wait_ge(s_x2, b + 1)
                sp.dma_start(x2[:, bass.ds(b * (NT * D), NT * D)],
                             x2s[:, :, :].rearrange("p t d -> p (t d)")).then_inc(s_x2all, 16)
                sp.wait_ge(s_x2T, b + 1)
                sp.dma_start(x2T[:, :, bass.ds(b * T, T)], x2Ts[:, :, :]).then_inc(s_x2Tall, 16)

            sp.wait_ge(s_h1, B)
            sp.dma_start(eup[:, :, :], a["eup"]).then_inc(s_eup, 16)
            for dst, src in ((wq, "wq1"), (wk, "wk1"), (wv, "wv1"), (wo, "wo1")):
                sp.dma_start(dst[:, :, :], a[src]).then_inc(s_w1in, 16)
            sp.wait_ge(s_scat, 16 * TOPK * BT)
            sp.dma_start(w1, a["w1"]).then_inc(s_wff, 16)
            sp.dma_start(w2, a["w2"]).then_inc(s_wff, 16)

            def load(j, p):
                since(sp, s_xgTps, j - 1)
                sp.dma_start(xg[p][:, :], xs_dram[bass.ds(j * SLOTS, SLOTS), :]).then_inc(s_xg[p], 16)

            def store(j, p):
                sp.wait_ge(s_ry, j + 1)
                sp.dma_start(ys_dram[bass.ds(j * SLOTS, SLOTS), :], ry[p][:, :]).then_inc(s_yst[p], 16)

            for j in range(4):
                load(j, j % 2)
            with sp.Fori(1, RT // 2 - 1) as i:
                load(2 * i + 2, 0)
                load(2 * i + 3, 1)
                store(2 * i - 2, 0)
                store(2 * i - 1, 1)
            for j in range(RT - 4, RT):
                store(j, j % 2)
            with sp.Fori(0, B) as b:
                sp.wait_ge(s_x4T, b + 1)
                sp.dma_start(x2T[:, :, bass.ds(b * T, T)], x2Ts[:, :, :]).then_inc(s_x4Tall, 16)
            for b in range(B):
                sp.wait_ge(s_h4, b + 1)
                sp.dma_start(out[b].rearrange("(t p) d -> p t d", t=NT), h4[:, b, :, :]).then_inc(s_out, 16)
            sp.wait_ge(s_out, 16 * B)

        @block.tensor
        def _(pe):
            mm = nc.tensor.matmul
            pe.wait_ge(s_tokin, 32)
            for i in range(3):
                n = IMG * min(3, B - 3 * i)
                for c in range(PC):
                    last = mm(bank[i][0:n, 0:D], xp[:, c, 3 * IMG * i:3 * IMG * i + n], tokw[:, c, :],
                              start=(c == 0), stop=(c == PC - 1))
                last.then_inc(s_tokps, 1)
            pe.wait_ge(s_w0, 16 * 10)
            pe.wait_ge(s_const, 16 * 3)
            pe.wait_ge(s_toksb, 3)

            def turn(b):
                pe.wait_ge(s_xn, b + 1)
                since(pe, s_x2T, b - 2)
                for t in range(NT):
                    for c in range(KC):
                        last = nc.tensor.transpose(bank[0][:, c * T + t * TT:c * T + (t + 1) * TT],
                                                   xn[:, t, c * P:(c + 1) * P], ident[0:TT, 0:TT])
                last.then_inc(s_xTps, 1)

            def gate_in(b):
                pe.wait_ge(s_xT, b + 1)
                for c in range(KC):
                    last = mm(bank[0][0:64, 0:T], cw1[:, c, :], xnT[:, c, :], start=(c == 0), stop=(c == KC - 1))
                last.then_inc(s_z1, 1)

            def gate_out(b):
                pe.wait_ge(s_th, b + 1)
                for o in range(KC):
                    last = mm(bank[0][:, o * T:(o + 1) * T], cw2[:, o * P:(o + 1) * P], th[:, :], start=True, stop=True)
                last.then_inc(s_z2, 1)

            def keys_queries(b):
                since(pe, s_ksb, b)
                for o in range(KC):
                    for c in range(KC):
                        last = mm(bank[2][:, o * T:(o + 1) * T], wk[:, c, o * P:(o + 1) * P], xnT[:, c, :],
                                  start=(c == 0), stop=(c == KC - 1))
                last.then_inc(s_k, 1)
                since(pe, s_qe, b)
                for o in range(KC):
                    for c in range(KC):
                        last = mm(bank[1][:, o * T:(o + 1) * T], wq[:, c, o * P:(o + 1) * P], xnT[:, c, :],
                                  start=(c == 0), stop=(c == KC - 1))
                last.then_inc(s_q, 1)

            def values(b):
                since(pe, s_vsb, b)
                for t in range(NT):
                    for c in range(KC):
                        last = mm(bank[3][0:TT, t * D:(t + 1) * D], xnT[:, c, t * TT:(t + 1) * TT], wv[:, c, :],
                                  start=(c == 0), stop=(c == KC - 1))
                last.then_inc(s_v, 1)

            def scores(b, p, half, pair):
                if pair == 0:
                    pe.wait_ge(s_kr, b + 1)
                    pe.wait_ge(s_qb0 if half == 0 else s_qb1, b + 1)
                for u in (2 * pair, 2 * pair + 1):
                    r, t = UNITS[u]
                    if u == 0:
                        since(pe, s_aact, 4 * b + 2 * half)
                    elif u == 4:
                        pe.wait_ge(s_aact, 4 * b + 2 * half + 1)
                    else:
                        since(pe, s_adve, 8 * b + 4 * half + [None, 0, 1, 2, None, 3][u])
                    m = min(TT, CH * (r + 1) - TT * t)
                    mm(bank[4 + u % 2][0:m, 0:HH * CH],
                       kr[p][:, half, COFF[r] + TT * t:COFF[r] + TT * t + m],
                       qb[p][:, half, :, CH * r:CH * (r + 1)], start=True, stop=True).then_inc(s_aps, 1)

            def mix(b, p, half):
                pe.wait_ge(s_adve, 8 * b + 4 * half + 4)
                pe.wait_ge(s_aact, 4 * b + 2 * half + 2)
                pe.wait_ge(s_vsb, b + 1)
                since(pe, s_ysb, b)
                for t in range(NT):
                    for par in range(2):
                        for i in range(4):
                            last = mm(bank[6][32 * i:32 * i + 32, half * T + t * TT:(half + 1) * T],
                                      vz[p][par][:, t, 4 * half + i, :, :],
                                      asb[half][:, t, 2 * i + par, t * TT:T],
                                      start=(t == 0 and par == 0), stop=(t == 1 and par == 1),
                                      skip_group_check=True, tile_position=(0, 32 * i))
                last.then_inc(s_pv, 1)

            def project_out(b):
                pe.wait_ge(s_ysb, b + 1)
                since(pe, s_lg, b)
                for t in range(NT):
                    for c in range(KC):
                        last = mm(bank[7][0:TT, t * D:(t + 1) * D], yT[:, c, t * TT:(t + 1) * TT], wo[:, c, :],
                                  start=(c == 0), stop=(c == KC - 1))
                last.then_inc(s_ops, 1)

            def turn2(b, final=False):
                pe.wait_ge(s_x2, b + 1)
                if final:
                    pe.wait_ge(s_x2T, b)
                else:
                    pe.wait_ge(s_lc, 2 * (b + 3))
                for t in range(NT):
                    for c in range(KC):
                        last = nc.tensor.transpose(bank[0][:, c * T + t * TT:c * T + (t + 1) * TT],
                                                   x2s[:, t, c * P:(c + 1) * P], ident[0:TT, 0:TT])
                last.then_inc(s_x2Tps, 1)

            def route(b):
                pe.wait_ge(s_x2T, b + 1)
                pe.wait_ge(s_h1, b + 1)
                for t in range(NT):
                    for c in range(KC):
                        last = mm(bank[7][0:TT, t * NE:(t + 1) * NE], x2Ts[:, c, t * TT:(t + 1) * TT], gw[:, c, :],
                                  start=(c == 0), stop=(c == KC - 1))
                last.then_inc(s_lgps, 1)

            def step(b, p, first=False, final=False):
                if not final:
                    turn(b + 1)
                scores(b, p, 0, 0)
                if not final:
                    gate_in(b + 1)
                if not first:
                    mix(b - 1, 1 - p, 1)
                if not final:
                    gate_out(b + 1)
                scores(b, p, 0, 1)
                if not final:
                    keys_queries(b + 1)
                if not first:
                    project_out(b - 1)
                scores(b, p, 0, 2)
                scores(b, p, 1, 0)
                if not final:
                    values(b + 1)
                scores(b, p, 1, 1)
                mix(b, p, 0)
                if not first:
                    if final:
                        pe.wait_ge(s_lc, 2 * B)
                    turn2(b - 1, final)
                scores(b, p, 1, 2)
                if not first:
                    route(b - 1)

            turn(0)
            gate_in(0)
            keys_queries(0)
            gate_out(0)
            values(0)
            step(0, 0, first=True)
            step(1, 1)
            with pe.Fori(1, B // 2 - 1) as i:
                step(2 * i, 0)
                step(2 * i + 1, 1)
            step(B - 2, 0)
            step(B - 1, 1, final=True)
            mix(B - 1, 1, 1)
            project_out(B - 1)
            turn2(B - 1, final=True)
            route(B - 1)

            def shared_up(g, j):
                if g == 0:
                    pe.wait_ge(s_lg, B)
                else:
                    pe.wait_ge(s_shid, FC * (g - 1) + j + 1)
                for half in range(2):
                    for c in range(KC):
                        last = mm(bank[2 * j + half][:, 0:GN], sup[:, c, half * HALF + j * P:half * HALF + (j + 1) * P],
                                  x2T[:, c, g * GN:(g + 1) * GN], start=(c == 0), stop=(c == KC - 1))
                last.then_inc(s_sups, 1)

            def shared_down(g):
                pe.wait_ge(s_shid, FC * (g + 1))
                for q in range(2):
                    since(pe, s_hsh, 2 * g + q - 1)
                    for t in range(NT):
                        for j in range(FC):
                            last = mm(bank[6 + q][0:TT, t * D:(t + 1) * D],
                                      shid[g % 2][:, j, q * T + t * TT:q * T + (t + 1) * TT], sdn[:, j, :],
                                      start=(j == 0), stop=(j == FC - 1))
                    last.then_inc(s_sdps, 1)

            pe.wait_ge(s_wf, 16 * 3)
            pe.wait_ge(s_x2Tall, 16 * B)
            shared_up(0, 0)
            shared_up(0, 1)
            pe.wait_ge(s_m12, 1)
            pe.wait_ge(s_rc, 32)
            m12 = rb[:, 6, :]
            mm(bank[7][0:TT, 0:BT * NE], tri[:, :], m12, start=True, stop=True)
            mm(bank[7][0:TT, 256:256 + BT * NE], ones[0:TT, 0:TT], m12, start=True, stop=True).then_inc(s_rps, 1)
            shared_up(0, 2)
            for g in range(1, GR):
                for j in range(FC):
                    shared_up(g, j)
                if g == 1:
                    pe.wait_ge(s_slot, 1)
                shared_down(g - 1)
            shared_down(GR - 1)

            pe.wait_ge(s_texp, 1)
            pe.wait_ge(s_eup, 16)

            def turn_x(j, p):
                pe.wait_ge(s_xg[p], 8 * j + 16 - 8 * p)
                since(pe, s_xgT, j)
                for c in range(KC):
                    last = nc.tensor.transpose(bank[0][:, c * P:(c + 1) * P], xg[p][:, c * P:(c + 1) * P], ident[:, :])
                last.then_inc(s_xgTps, 1)

            def up(j, p):
                e = pe.value_load(texpi[0:1, bass.ds(j, 1)], min_val=0, max_val=NE - 1)
                pe.wait_ge(s_xgT, j + 1)
                since(pe, s_rh, j - 1)
                for half in range(2):
                    for c in range(KC):
                        last = mm(bank[1 + 2 * p + half][:, 0:HALF], xgT[p][:, c, :],
                                  eup[:, c, bass.ds(e * (2 * HALF) + half * HALF, HALF)],
                                  start=(c == 0), stop=(c == KC - 1))
                last.then_inc(s_rups, 1)

            def turn_hidden(j, p):
                pe.wait_ge(s_rh, j + 1)
                since(pe, s_rhT, j)
                for k in range(FC):
                    last = nc.tensor.transpose(bank[5][:, k * P:(k + 1) * P], rh[p][:, k * P:(k + 1) * P], ident[:, :])
                last.then_inc(s_rhTps, 1)

            def down(j, p):
                e = pe.value_load(texpi[0:1, bass.ds(j, 1)], min_val=0, max_val=NE - 1)
                pe.wait_ge(s_rhT, j + 1)
                since(pe, s_ry, j)
                for k in range(FC):
                    last = mm(bank[6][:, 0:D], rhT[p][:, k, :], edn[:, k, bass.ds(e * D, D)],
                              start=(k == 0), stop=(k == FC - 1))
                last.then_inc(s_rdps, 1)

            def tile_step(j, p):
                turn_x(j + 1, 1 - p)
                up(j, p)
                turn_hidden(j - 1, 1 - p)
                down(j - 2, p)

            turn_x(0, 0)
            turn_x(1, 1)
            up(0, 0)
            turn_x(2, 0)
            up(1, 1)
            turn_hidden(0, 0)
            tile_step(2, 0)
            with pe.Fori(1, RT // 2 - 1) as i:
                tile_step(2 * i + 1, 1)
                tile_step(2 * i + 2, 0)
            up(RT - 1, 1)
            turn_hidden(RT - 2, 0)
            down(RT - 3, 1)
            turn_hidden(RT - 1, 1)
            down(RT - 2, 0)
            down(RT - 1, 1)

            pe.wait_ge(s_w1in, 64)
            pe.wait_ge(s_l1c, 16 * 6)

            def turn1(b):
                pe.wait_ge(s_xn1, b + 1)
                since(pe, s_lg4, b - 2)
                for t in range(NT):
                    for c in range(KC):
                        last = nc.tensor.transpose(bank[0][:, c * T + t * TT:c * T + (t + 1) * TT],
                                                   xn[:, t, c * P:(c + 1) * P], ident[0:TT, 0:TT])
                last.then_inc(s_xT1ps, 1)

            def keys1(b):
                pe.wait_ge(s_xT1, b + 1)
                for o in range(KC):
                    for c in range(KC):
                        last = mm(bank[0][:, o * T:(o + 1) * T], wk[:, c, o * P:(o + 1) * P], xnT[:, c, :],
                                  start=(c == 0), stop=(c == KC - 1))
                last.then_inc(s_k1ps, 1)

            def queries1(b):
                since(pe, s_rbs, b - 1)
                for o in range(KC):
                    for c in range(KC):
                        last = mm(bank[2][:, o * T:(o + 1) * T], wq[:, c, o * P:(o + 1) * P], xnT[:, c, :],
                                  start=(c == 0), stop=(c == KC - 1))
                last.then_inc(s_q1ps, 1)

            def values1(b, t):
                if t == 0:
                    since(pe, s_h3, b - 1)
                for c in range(KC):
                    last = mm(bank[3][0:TT, t * D:(t + 1) * D], xnT[:, c, t * TT:(t + 1) * TT], wv[:, c, :],
                              start=(c == 0), stop=(c == KC - 1))
                if t == 1:
                    last.then_inc(s_v1ps, 1)

            def logits1(b, p, u):
                half, t, n, w = UNITS1[u]
                if u == 0:
                    pe.wait_ge(s_q1, 2 * b + 2)
                if u % (NU1 // 2) == 0:
                    pe.wait_ge(s_kb, 2 * b + half + 1)
                since(pe, s_min, NU1 * b + u - 1)
                mm(bank[4 + u % 2][0:TT, 0:w * T], q1[p][:, half, t * TT:(t + 1) * TT], kb[p][:, half, n:n + w, :],
                   start=True, stop=True).then_inc(s_sps, 1)

            def turn_probs(b, u):
                half, t, n, w = UNITS1[u]
                pe.wait_ge(s_p, NU1 * b + u + 1)
                since(pe, s_pt[u % 2], NU1 // 2 * b + u // 2)
                for kt in range(NT):
                    for i in range(w):
                        last = nc.tensor.transpose(bank[6 + u % 2][0:TT, (kt * w + i) * TT:(kt * w + i + 1) * TT],
                                                   ring[u % 4][0:TT, i, kt * TT:(kt + 1) * TT], ident[0:TT, 0:TT])
                last.then_inc(s_ptps, 1)

            def turn4(b):
                pe.wait_ge(s_x4, b + 1)
                since(pe, s_lg4, b)
                for t in range(NT):
                    for c in range(KC):
                        last = nc.tensor.transpose(bank[0][:, c * T + t * TT:c * T + (t + 1) * TT],
                                                   x2s[:, t, c * P:(c + 1) * P], ident[0:TT, 0:TT])
                last.then_inc(s_x4Tps, 1)

            def router(b):
                pe.wait_ge(s_x4T, b + 1)
                for t in range(NT):
                    for c in range(KC):
                        last = mm(bank[0][0:TT, t * NE:(t + 1) * NE], x2Ts[:, c, t * TT:(t + 1) * TT], rw[:, c, :],
                                  start=(c == 0), stop=(c == KC - 1))
                last.then_inc(s_lg4ps, 1)

            def mix1(b, p, half):
                for par in range(2):
                    pe.wait_ge(s_pt[par], NU1 // 2 * b + (half + 1) * NU1 // 4)
                pe.wait_ge(s_v1, b + 1)
                since(pe, s_y1, b)
                for t in range(NT):
                    for par in range(2):
                        for i in range(4):
                            last = mm(bank[1][32 * i:32 * i + 32, half * T:(half + 1) * T],
                                      vz[p][par][:, t, 4 * half + i, :, :], pT[half][:, t, 2 * i + par, :],
                                      start=(t == 0 and par == 0), stop=(t == 1 and par == 1),
                                      skip_group_check=True, tile_position=(0, 32 * i))
                last.then_inc(s_pv1, 1)

            def sums1(b):
                pe.wait_ge(s_rspread, b + 1)
                for half in range(KC):
                    for t in range(NT):
                        last = mm(bank[2][:, half * T + t * TT:half * T + (t + 1) * TT],
                                  rspread[0:TT, t, half * P:(half + 1) * P],
                                  ident[0:TT, 0:TT], start=True, stop=True)
                last.then_inc(s_rbps, 1)

            def project_out1(b, t, final=False):
                if t == 0:
                    pe.wait_ge(s_y1, b + 1)
                    pe.wait_ge(s_v1, b + 1 if final else b + 2)
                for c in range(KC):
                    last = mm(bank[3][0:TT, t * D:(t + 1) * D], yT[:, c, t * TT:(t + 1) * TT], wo[:, c, :],
                              start=(c == 0), stop=(c == KC - 1))
                if t == 1:
                    last.then_inc(s_o1ps, 1)

            def step1(b, p, first=False, second=False, final=False):
                for u in range(NU1):
                    logits1(b, p, u)
                    if u >= 2:
                        turn_probs(b, u - 2)
                    elif not first:
                        turn_probs(b - 1, NU1 - 2 + u)
                    if not (first or second):
                        if u == 0:
                            turn4(b - 2)
                        elif u == 2:
                            router(b - 2)
                    if not first:
                        if u == 3:
                            mix1(b - 1, 1 - p, 1)
                        elif u == 5:
                            sums1(b - 1)
                        elif u == 7:
                            project_out1(b - 1, 0)
                        elif u == 8:
                            project_out1(b - 1, 1)
                    if not final:
                        if u == 4:
                            turn1(b + 1)
                        elif u == 6:
                            keys1(b + 1)
                        elif u == 9:
                            queries1(b + 1)
                        elif u == 11:
                            values1(b + 1, 0)
                            values1(b + 1, 1)
                    if u == 10:
                        if first:
                            pe.wait_ge(s_pz, 1)
                        mix1(b, p, 0)

            turn1(0)
            keys1(0)
            queries1(0)
            values1(0, 0)
            values1(0, 1)
            step1(0, 0, first=True)
            step1(1, 1, second=True)
            step1(2, 0)
            with pe.Fori(1, B // 2 - 1) as i:
                step1(2 * i + 1, 1)
                step1(2 * i + 2, 0)
            step1(B - 1, 1, final=True)
            turn_probs(B - 1, NU1 - 2)
            turn_probs(B - 1, NU1 - 1)
            turn4(B - 2)
            mix1(B - 1, 1, 1)
            sums1(B - 1)
            router(B - 2)
            project_out1(B - 1, 0, final=True)
            project_out1(B - 1, 1)
            turn4(B - 1)
            router(B - 1)

            def ff_up(g):
                for j in range(FFC):
                    n = FFC * g + j
                    since(pe, s_hid, n - 5)
                    for c in range(KC):
                        last = mm(bank[n % 6][:, 0:GN], w1[:, c, j * P:(j + 1) * P], x2T[:, c, g * GN:(g + 1) * GN],
                                  start=(c == 0), stop=(c == KC - 1))
                    last.then_inc(s_fups, 1)

            def ff_down(g):
                pe.wait_ge(s_hid, FFC * (g + 1))
                for q in range(2):
                    since(pe, s_ft, 2 * g + q - 1)
                    for t in range(NT):
                        for j in range(FFC):
                            last = mm(bank[6 + q][0:TT, t * D:(t + 1) * D],
                                      hid[g % 2][:, j, q * T + t * TT:q * T + (t + 1) * TT], w2[:, j, :],
                                      start=(j == 0), stop=(j == FFC - 1))
                    last.then_inc(s_fdps, 1)

            pe.wait_ge(s_wff, 32)
            pe.wait_ge(s_x4Tall, 16 * B)
            pe.wait_ge(s_lg4, B)
            ff_up(0)
            for g in range(1, GR):
                ff_up(g)
                ff_down(g - 1)
            ff_down(GR - 1)

        @block.scalar
        def _(act):
            acte = nc.scalar.activation
            for i in range(3):
                n = IMG * min(3, B - 3 * i)
                act.wait_ge(s_tokps, i + 1)
                nc.scalar.copy(tok[0:n, i, :], bank[i][0:n, 0:D]).then_inc(s_toksb, 1)
            act.wait_ge(s_w0, 16 * 10)
            nc.scalar.preload_act_table_set("sigmoid_and_others")
            acte(base[:, :], dec[:, :], ACT.Sigmoid).then_inc(s_base, 1)
            act.wait_ge(s_zero, 1)
            nc.scalar.preload_act_table_set("natural_log_exp_and_others")
            act.wait_ge(s_al, 1)
            acte(aabs[:, 1, :], aabs[:, 0, :], ACT.Exp, scale=-1.0).then_inc(a1ch, 1)
            act.wait_ge(a1ch, 1)
            acte(aabs[:, 0, :], aabs[:, 1, :], ACT.Ln, bias=1.0).then_inc(s_al, 1)

            def norm_scale(b):
                act.wait_ge(s_mv, b + 1)
                acte(lnv[:, :], mv[:, :, 1], ACT.Ln, bias=EPSC[0:TT, 0:1]).then_inc(ach, 1)
                act.wait_ge(ach, b + 1)
                acte(rstd[:, :], lnv[:, :], ACT.Exp, scale=-0.5).then_inc(s_rstd, 1)

            def turned(b):
                act.wait_ge(s_xTps, b + 1)
                since(act, s_v, b)
                nc.scalar.copy(xnT[:, :, :].rearrange("p c t -> p (c t)"), bank[0][:, 0:KC * T]).then_inc(s_xT, 1)
                nc.scalar.preload_act_table_set("sigmoid_and_others")

            def gate_in(b):
                act.wait_ge(s_z1, b + 1)
                since(act, s_z2, b)
                acte(th[:, :], bank[0][0:64, 0:T], ACT.Tanh, bias=cb1[:, 0:1]).then_inc(s_th, 1)

            def gate_out(b):
                act.wait_ge(s_z2, b + 1)
                since(act, s_lam, b)
                for o in range(KC):
                    acte(lc[:, o, :], bank[0][:, o * T:(o + 1) * T], ACT.Sigmoid, bias=cb2[:, o:o + 1]).then_inc(s_lc, 1)
                nc.scalar.preload_act_table_set("natural_log_exp_and_others")

            def logs(b):
                act.wait_ge(s_lam, b + 1)
                since(act, s_G, b)
                acte(lnlam[:, :, :], lam[:, :, :], ACT.Ln).then_inc(s_lnlam, 1)

            def keys_in(b):
                act.wait_ge(s_k, b + 1)
                since(act, s_kr, b)
                nc.scalar.copy(ksb[:, :, :].rearrange("p c t -> p (c t)"), bank[2][:, 0:KC * T]).then_inc(s_ksb, 1)

            def query_decay(b):
                act.wait_ge(s_dq, b + 1)
                since(act, s_qe, b)
                acte(eq[:, :], dq[:, :], ACT.Exp).then_inc(s_eq, 1)

            def key_decay(b):
                act.wait_ge(s_dk, b + 1)
                since(act, s_kr, b)
                acte(ek[:, :, :], dk[:, :, :], ACT.Exp).then_inc(s_ek, 1)

            def values(b, p):
                act.wait_ge(s_v, b + 1)
                since(act, s_pv, 2 * b - 2)
                for par in range(2):
                    src = bank[3][0:TT, :].rearrange("p (t i j d) -> p (t i) j d", t=NT, i=HEADS // 2, j=2)
                    dst = vz[p][par][0:TT, :, :, :, :].rearrange("p t i j d -> p (t i) j d")
                    ins = nc.scalar.copy(dst[:, :, par, :], src[:, :, par, :])
                ins.then_inc(s_vsb, 1)

            def plain(b, half, n):
                u = PLAIN[n]
                r, t = UNITS[u]
                act.wait_ge(s_aps, 12 * b + 6 * half + u + 1)
                if n == 0:
                    since(act, s_pv, 2 * b + half - 1)
                nc.scalar.copy(asb[half][0:TT, t, :, CH * r:CH * (r + 1)],
                               bank[4 + u % 2][0:TT, 0:HH * CH].rearrange("p (h c) -> p h c", c=CH)).then_inc(s_aact, 1)

            def mixed(b):
                act.wait_ge(s_pv, 2 * b + 2)
                since(act, s_ops, b)
                nc.scalar.copy(yT[:, :, :].rearrange("p c t -> p (c t)"), bank[6][:, 0:KC * T]).then_inc(s_ysb, 1)

            def norm2(b):
                act.wait_ge(s_mv2, b + 1)
                acte(lnv2[:, :], mv2[:, :, 1], ACT.Ln, bias=EPSC[0:TT, 0:1]).then_inc(ach2, 1)
                act.wait_ge(ach2, b + 1)
                acte(rstd2[:, :], lnv2[:, :], ACT.Exp, scale=-0.5).then_inc(s_rstd2, 1)

            def turned2(b):
                act.wait_ge(s_x2Tps, b + 1)
                since(act, s_x2Tall, 16 * b)
                since(act, s_lgps, b)
                nc.scalar.copy(x2Ts[:, :, :].rearrange("p c t -> p (c t)"), bank[0][:, 0:KC * T]).then_inc(s_x2T, 1)

            def step(b, p, first=False, last=False, final=False):
                if not final:
                    turned(b + 1)
                    gate_in(b + 1)
                if not first:
                    mixed(b - 1)
                if not final:
                    gate_out(b + 1)
                plain(b, 0, 0)
                if not final:
                    logs(b + 1)
                    keys_in(b + 1)
                    query_decay(b + 1)
                plain(b, 0, 1)
                if not final:
                    key_decay(b + 1)
                if not first:
                    norm2(b - 1)
                if not final:
                    values(b + 1, 1 - p)
                plain(b, 1, 0)
                if not first:
                    turned2(b - 1)
                plain(b, 1, 1)
                if not (last or final):
                    norm_scale(b + 2)

            norm_scale(0)
            turned(0)
            gate_in(0)
            keys_in(0)
            gate_out(0)
            logs(0)
            query_decay(0)
            key_decay(0)
            values(0, 0)
            norm_scale(1)
            step(0, 0, first=True)
            step(1, 1)
            with act.Fori(1, B // 2 - 1) as i:
                step(2 * i, 0)
                step(2 * i + 1, 1)
            step(B - 2, 0, last=True)
            step(B - 1, 1, final=True)
            mixed(B - 1)
            norm2(B - 1)
            turned2(B - 1)

            nc.scalar.preload_act_table_set("silu_and_others")
            act.wait_ge(s_gap, 1)
            acte(rs[:, 5, :], rs[:, 4, :], ACT.Tanh, scale=0.5).then_inc(s_gw, 1)
            for g in range(GR):
                for j in range(FC):
                    act.wait_ge(s_sups, FC * g + j + 1)
                    since(act, s_shid, FC * (g - 1) + j + 1)
                    acte(sgate[:, j, :], bank[2 * j][:, 0:GN], ACT.Silu).then_inc(s_sg, 1)

            def silu(j, p):
                act.wait_ge(s_rups, j + 1)
                since(act, s_rh, j)
                acte(rg[:, :], bank[1 + 2 * p][:, 0:HALF], ACT.Silu).then_inc(s_rg, 1)

            def hidden_turned(j, p):
                act.wait_ge(s_rhTps, j + 1)
                since(act, s_rdps, j - 1)
                nc.scalar.copy(rhT[p][:, :, :].rearrange("p k n -> p (k n)"), bank[5][:, 0:FC * P]).then_inc(s_rhT, 1)

            silu(0, 0)
            silu(1, 1)
            hidden_turned(0, 0)
            silu(2, 0)
            hidden_turned(1, 1)
            with act.Fori(1, RT // 2 - 1) as i:
                silu(2 * i + 1, 1)
                hidden_turned(2 * i, 0)
                silu(2 * i + 2, 0)
                hidden_turned(2 * i + 1, 1)
            silu(RT - 1, 1)
            hidden_turned(RT - 2, 0)
            hidden_turned(RT - 1, 1)

            nc.scalar.preload_act_table_set("natural_log_exp_and_others")

            def norm1(b):
                act.wait_ge(s_mv1, b + 1)
                acte(lnv[:, :], mv[:, :, 1], ACT.Ln, bias=EPSC[0:TT, 0:1]).then_inc(a1ch, 1)
                act.wait_ge(a1ch, b + 2)
                acte(rstd[:, :], lnv[:, :], ACT.Exp, scale=-0.5).then_inc(s_rstd1, 1)

            def norm4(b):
                act.wait_ge(s_mv4, b + 1)
                acte(lnv2[:, :], mv2[:, :, 1], ACT.Ln, bias=EPSC[0:TT, 0:1]).then_inc(a4ch, 1)
                act.wait_ge(a4ch, b + 1)
                acte(rstd2[:, :], lnv2[:, :], ACT.Exp, scale=-0.5).then_inc(s_rstd4, 1)

            def turned1(b):
                act.wait_ge(s_xT1ps, b + 1)
                since(act, s_v1ps, b)
                nc.scalar.copy(xnT[:, :, :].rearrange("p c t -> p (c t)"), bank[0][:, 0:KC * T]).then_inc(s_xT1, 1)

            def keys1(b):
                act.wait_ge(s_k1ps, b + 1)
                since(act, s_kb, 2 * b)
                for o in range(KC):
                    ins = acte(ksb1[:, o, :], bank[0][:, o * T:(o + 1) * T], ACT.Identity, bias=qkb[:, 1, o:o + 1])
                ins.then_inc(s_k1, 1)

            def queries1(b, p):
                act.wait_ge(s_q1ps, b + 1)
                since(act, s_sps, NU1 * (b - 1))
                for o in range(KC):
                    acte(q1[p][:, o, :], bank[2][:, o * T:(o + 1) * T], ACT.Identity, bias=nqb[:, o:o + 1],
                         scale=-1.0 / SCALE).then_inc(s_q1, 1)

            def probs(b, p, u):
                half, t, n, w = UNITS1[u]
                if u == 0:
                    since(act, s_rinv, b - 1)
                act.wait_ge(s_min, NU1 * b + u + 1)
                for i in range(w):
                    col = t * HEADS + half * HH + n + i
                    ins = acte(ring[u % 4][0:TT, i, :], ring[u % 4][0:TT, i, :], ACT.Exp, scale=-1.0,
                               bias=mn[:, col:col + 1], accum_out=rsum[p][:, col:col + 1])
                ins.then_inc(s_p, 1)

            def probs_turned(b, u):
                if u % 2 == 0:
                    return
                half, t, n, w = UNITS1[u]
                act.wait_ge(s_ptps, NU1 * b + u + 1)
                if u in (1, 7):
                    since(act, s_pv1, 2 * b + half - 1)
                nc.scalar.copy(pT[half][0:TT, :, n:n + w, t * TT:(t + 1) * TT],
                               bank[6 + u % 2][0:TT, 0:NT * w * TT].rearrange("p (k h q) -> p k h q", k=NT, h=w)).then_inc(s_pt[1], 1)

            def sums1(b):
                act.wait_ge(s_rbps, b + 1)
                since(act, s_y1, b)
                nc.scalar.copy(rbs[:, :, :].rearrange("p c t -> p (c t)"), bank[2][:, 0:KC * T]).then_inc(s_rbs, 1)

            def step1(b, p, first=False, second=False, final=False):
                for u in range(NU1):
                    if u >= 3:
                        probs_turned(b, u - 3)
                    elif not first:
                        probs_turned(b - 1, NU1 - 3 + u)
                    probs(b, p, u)
                    if not first:
                        if u == 5:
                            sums1(b - 1)
                        elif u == 10:
                            norm4(b - 1)
                    if u == 0 and not (first or second):
                        turned4(b - 2)
                    if not final:
                        if u == 2:
                            norm1(b + 1)
                        elif u == 4:
                            turned1(b + 1)
                        elif u == 6:
                            keys1(b + 1)
                        elif u == 9:
                            queries1(b + 1, 1 - p)

            def turned4(b):
                act.wait_ge(s_x4Tps, b + 1)
                since(act, s_x4Tall, 16 * b)
                since(act, s_lg4ps, b)
                nc.scalar.copy(x2Ts[:, :, :].rearrange("p c t -> p (c t)"), bank[0][:, 0:KC * T]).then_inc(s_x4T, 1)

            act.wait_ge(s_nqb, 1)
            act.wait_ge(s_l1c, 16 * 6)
            norm1(0)
            turned1(0)
            keys1(0)
            queries1(0, 0)
            step1(0, 0, first=True)
            step1(1, 1, second=True)
            step1(2, 0)
            with act.Fori(1, B // 2 - 1) as i:
                step1(2 * i + 1, 1)
                step1(2 * i + 2, 0)
            step1(B - 1, 1, final=True)
            probs_turned(B - 1, NU1 - 3)
            probs_turned(B - 1, NU1 - 1)
            turned4(B - 2)
            sums1(B - 1)
            norm4(B - 1)
            turned4(B - 1)
            act.wait_ge(s_rx, 1)
            acte(rb[:, 1, :], rb[:, 0, :], ACT.Exp).then_inc(s_rexp, 1)
            nc.scalar.preload_act_table_set("gelu_apprx_tanh_and_others")
            for g in range(GR):
                for j in range(FFC):
                    n = FFC * g + j
                    act.wait_ge(s_fups, n + 1)
                    if j == 0:
                        since(act, s_fdps, 2 * (g - 1))
                    acte(hid[g % 2][:, j, :], bank[n % 6][:, 0:GN], ACT.Gelu_apprx_tanh, bias=b1c[:, j:j + 1]).then_inc(s_hid, 1)

        @block.vector
        def _(dve):
            v = nc.vector

            def settle():
                dve.sem_inc(s_settled, 1)

            v.memset(ones[:, :], 1.0).then_inc(vch, 1)
            dve.wait_ge(s_base, 1)
            v.tensor_scalar(base02[:, :], base[:, :], 0.2, None, ALU.mult).then_inc(vch, 1)
            dve.wait_ge(s_txt, 32)
            dve.wait_ge(s_tokh, 16 * B)
            dve.wait_ge(s_const, 48)
            dve.wait_ge(vch, 2)
            dve.wait_ge(s_l1c, 16 * 6)
            v.tensor_scalar(nqb[:, :], qkb[:, 0, :], -1.0 / SCALE, None, ALU.mult).then_inc(s_nqb, 1)
            v.scalar_tensor_tensor(aabs[:, 0, :], arow[:, :], -1.0, arow[:, :], ALU.mult, ALU.max).then_inc(s_al, 1)
            dve.wait_ge(s_al, 2)
            v.scalar_tensor_tensor(alpha[:, :], arow[:, :], 0.0, aabs[:, 0, :], ALU.max, ALU.add).then_inc(s_alpha, 1)

            def stats0(b):
                c = Chain(dve, vch, 2 + 7 * b)
                ht = htile(b)
                for t in range(NT):
                    c.add(v.bn_stats(st[:, 6 * t:6 * t + 6], ht[:, t, :]))
                c.wait()
                since(dve, s_rstd, b)
                settle()
                c.add(v.bn_aggr(mv[:, 0, :], st[:, 0:6]))
                v.bn_aggr(mv[:, 1, :], st[:, 6:12]).then_inc(s_mv, 1)
                c.step(3)

            def normed0(b):
                c = Chain(dve, vch, 2 + 7 * b + 3)
                ht = htile(b)
                dve.wait_ge(s_rstd, b + 1)
                since(dve, s_xTps, b)
                c.add(v.tensor_scalar(xn[:, 0, :], ht[:, 0, :], mv[:, 0, 0:1], rstd[:, 0:1], ALU.subtract, ALU.mult))
                v.tensor_scalar(xn[:, 1, :], ht[:, 1, :], mv[:, 1, 0:1], rstd[:, 1:2], ALU.subtract, ALU.mult).then_inc(s_xn, 1)
                c.step(1)

            def decay(b):
                c = Chain(dve, vch, 2 + 7 * b + 4)
                dve.wait_ge(s_lc, 2 * b + 2)
                since(dve, s_lnlam, b)
                for o in range(KC):
                    c.add(v.tensor_scalar(lam[:, o, :], lc[:, o, :], base02[:, o:o + 1], base[:, o:o + 1], ALU.mult, ALU.add))
                c.wait()
                v.tensor_scalar(lam[:, :, :], lam[:, :, :], LAM_MAX, LAM_MIN, ALU.min, ALU.max).then_inc(s_lam, 1)
                c.step(2)

            def summed(b):
                c = Chain(dve, vch, 2 + 7 * b + 6)
                dve.wait_ge(s_lnlam, b + 1)
                since(dve, s_dk, b)
                c.add(v.tensor_tensor_scan(G[:, 0, :], ones[:, :], lnlam[:, 0, :], 0.0, ALU.mult, ALU.add))
                v.tensor_tensor_scan(G[:, 1, :], ones[:, :], lnlam[:, 1, :], 0.0, ALU.mult, ALU.add).then_inc(s_G, 1)
                c.wait()
                dve.wait_ge(s_G, b + 1)
                since(dve, s_eq, b)
                Gc = G[:, :, :].rearrange("p c (n t) -> p (c n) t", t=CH)
                v.tensor_tensor(dq[:, :].rearrange("p (n t) -> p n t", t=CH), Gc,
                                Gc[:, :, MIDC:MIDC + 1].to_broadcast([P, KC * NCH, CH]), ALU.subtract).then_inc(s_dq, 1)
                c.step(1)

            def queries(b, p):
                dve.wait_ge(s_eq, b + 1)
                dve.wait_ge(s_q, b + 1)
                since(dve, s_qb1, b)
                v.tensor_tensor(qe[:, :, :].rearrange("p c t -> p (c t)"), bank[1][:, 0:KC * T], eq[:, :], ALU.mult).then_inc(s_qe, 1)
                dve.wait_ge(s_qe, b + 1)
                since(dve, s_aps, 12 * (b - 1))
                v.tensor_tensor(qb[p][:, 0, :, :], qe[:, 0:1, :].to_broadcast([P, HH, T]),
                                hmask[:, :].unsqueeze(2).to_broadcast([P, HH, T]), ALU.mult).then_inc(s_qb0, 1)

            def masked(b, half, n):
                u = MASKED[n]
                r, t = UNITS[u]
                m = min(TT, CH * (r + 1) - TT * t)
                dve.wait_ge(s_aps, 12 * b + 6 * half + u + 1)
                if n == 0:
                    since(dve, s_pv, 2 * b + half - 1)
                settle()
                v.copy_predicated(asb[half][0:m, t, :, CH * r:CH * (r + 1)],
                                  cmask[0:m, r % 2, :].unsqueeze(1).to_broadcast([m, HH, CH]),
                                  bank[4 + u % 2][0:m, 0:HH * CH].rearrange("p (h c) -> p h c", c=CH)).then_inc(s_adve, 1)

            def residual(b):
                dve.wait_ge(s_ops, b + 1)
                hb = h[:, bass.ds(b * (NT * D), NT * D)]
                v.tensor_tensor(hb, hb, bank[7][0:TT, :], ALU.add).then_inc(s_h1, 1)
                c = Chain(dve, vch2, 4 * b)
                ht = htile(b)
                dve.wait_ge(s_h1, b + 1)
                settle()
                for t in range(NT):
                    c.add(v.bn_stats(st2[:, 6 * t:6 * t + 6], ht[:, t, :]))
                c.wait()
                settle()
                c.add(v.bn_aggr(mv2[:, 0, :], st2[:, 0:6]))
                v.bn_aggr(mv2[:, 1, :], st2[:, 6:12]).then_inc(s_mv2, 1)
                c.step(3)

            def normed2(b):
                c = Chain(dve, vch2, 4 * b + 3)
                ht = htile(b)
                dve.wait_ge(s_rstd2, b + 1)
                since(dve, s_x2Tps, b)
                since(dve, s_x2all, 16 * b)
                c.add(v.tensor_scalar(x2s[:, 0, :], ht[:, 0, :], mv2[:, 0, 0:1], rstd2[:, 0:1], ALU.subtract, ALU.mult))
                v.tensor_scalar(x2s[:, 1, :], ht[:, 1, :], mv2[:, 1, 0:1], rstd2[:, 1:2], ALU.subtract, ALU.mult).then_inc(s_x2, 1)
                c.step(1)

            def logits(b):
                dve.wait_ge(s_lgps, b + 1)
                v.tensor_scalar(lg[:, bass.ds(b * (NT * NE), NT * NE)], bank[7][0:TT, 0:NT * NE], 1.0, None, ALU.mult).then_inc(s_lg, 1)

            def step(b, p, first=False, last=False, final=False):
                masked(b, 0, 0)
                masked(b, 0, 1)
                if not final:
                    decay(b + 1)
                masked(b, 0, 2)
                if not final:
                    summed(b + 1)
                if not first:
                    residual(b - 1)
                masked(b, 0, 3)
                if not final:
                    queries(b + 1, 1 - p)
                masked(b, 1, 0)
                masked(b, 1, 1)
                if not first:
                    normed2(b - 1)
                masked(b, 1, 2)
                if not (last or final):
                    stats0(b + 2)
                masked(b, 1, 3)
                if not (last or final):
                    normed0(b + 2)
                if not first:
                    logits(b - 1)

            stats0(0)
            normed0(0)
            decay(0)
            summed(0)
            queries(0, 0)
            stats0(1)
            normed0(1)
            step(0, 0, first=True)
            step(1, 1)
            with dve.Fori(1, B // 2 - 1) as i:
                step(2 * i, 0)
                step(2 * i + 1, 1)
            step(B - 2, 0, last=True)
            step(B - 1, 1, final=True)
            residual(B - 1)
            normed2(B - 1)
            logits(B - 1)

            dve.wait_ge(s_lg, B)
            dve.wait_ge(s_rc, 32)
            c = Chain(dve, rch)
            AX = mybir.AxisListType.X

            def grid(x):
                return x.rearrange("p (i e) -> p i e", e=NE)

            def over(x):
                return x.unsqueeze(2).to_broadcast([TT, BT, NE])

            logit, same, rank, first, rest, second = lg[:, :], rb[:, 0, :], rb[:, 1, :], rb[:, 2, :], rb[:, 3, :], rb[:, 4, :]
            best, bestrank, next_, nextrank = rs[:, 0, :], rs[:, 1, :], rs[:, 2, :], rs[:, 3, :]

            def choose(x, top, toprank, pick):
                c(v.tensor_reduce(top, grid(x), AX, ALU.max))
                c(v.tensor_tensor(grid(same), grid(x), over(top), ALU.is_equal))
                c(v.tensor_tensor(grid(rank), grid(same), desc, ALU.mult))
                c(v.tensor_reduce(toprank, grid(rank), AX, ALU.max))
                c(v.tensor_tensor(grid(pick), desc, over(toprank), ALU.is_equal))

            choose(logit, best, bestrank, first)
            c(v.scalar_tensor_tensor(rest, first, -1e30, logit, ALU.mult, ALU.add))
            choose(rest, next_, nextrank, second)
            v.tensor_tensor(rs[:, 4, :], best, next_, ALU.subtract).then_inc(s_gap, 1)
            v.tensor_tensor(rb[:, 6, :], first, second, ALU.add).then_inc(s_m12, 1)

            def shared_hidden(g, j):
                dve.wait_ge(s_sg, FC * g + j + 1)
                since(dve, s_sdps, 2 * (g - 1))
                v.tensor_tensor(shid[g % 2][:, j, :], sgate[:, j, :], bank[2 * j + 1][:, 0:GN], ALU.mult).then_inc(s_shid, 1)

            shared_hidden(0, 0)
            dve.wait_ge(s_rps, 1)
            tot, cum, before, pos, pick = rb[:, 7, :], rb[:, 8, :], rb[:, 9, :], rb[:, 10, :], rb[:, 11, :]
            eg = lambda x: x.rearrange("p (e i) -> p e i", e=NE)
            flip = lambda x: x.rearrange("p (e i) -> p i e", e=NE)
            c(v.tensor_copy(eg(tot), bank[7][0:TT, 256:256 + BT * NE].rearrange("p (i e) -> p e i", e=NE)))
            c(v.tensor_tensor_scan(cum, fresh, tot, 0.0, ALU.mult, ALU.add))
            c(v.tensor_tensor(before, cum, tot, ALU.subtract))
            c(v.tensor_scalar(r8i[:, 0, :], eg(cum)[:, :, BT - 1], float(SLOTS - 1), None, ALU.add))
            c(v.tensor_scalar(r8i[:, 1, :], r8i[:, 0, :], 7, None, ALU.arith_shift_right))
            c(v.tensor_copy(r8[:, 0, :], r8i[:, 1, :]))
            c(v.tensor_tensor_scan(r8[:, 1, :], ones[0:TT, 0:NE], r8[:, 0, :], 0.0, ALU.mult, ALU.add))
            c(v.tensor_tensor(r8[:, 2, :], r8[:, 1, :], r8[:, 0, :], ALU.subtract))
            c(v.tensor_scalar(r8[:, 3, :], r8[:, 2, :], float(SLOTS), None, ALU.mult))
            c(v.tensor_tensor(eg(before), eg(before), r8[:, 3, :].unsqueeze(2).to_broadcast([TT, NE, BT]), ALU.add))
            c(v.tensor_tensor(grid(pos), grid(bank[7][0:TT, 0:BT * NE]), flip(before), ALU.add))
            for k, choice in enumerate((first, second)):
                c(v.tensor_tensor(pick, choice, pos, ALU.mult))
                c(v.tensor_reduce(slotf[:, k, :], grid(pick), AX, ALU.add))
            v.tensor_copy(slot[:, :, :], slotf[:, :, :]).then_inc(s_slot, 1)
            shared_hidden(0, 1)
            c(v.tensor_tensor(texp[:, :].rearrange("p (j e) -> p j e", e=NE), tileno,
                              r8[:, 1:2, :].to_broadcast([TT, RT, NE]), ALU.is_ge))
            c(v.tensor_reduce(texpf[:, :], texp[:, :].rearrange("p (j e) -> p j e", e=NE), AX, ALU.add))
            v.tensor_scalar(texpi[:, :], texpf[:, :], float(NE - 1), None, ALU.min).then_inc(s_texp, 1)
            shared_hidden(0, 2)
            dve.wait_ge(s_gw, 1)
            c.add(v.tensor_scalar(gatew[:, 0, :], rs[:, 5, :], 0.5, 0.5, ALU.mult, ALU.add))
            c(v.tensor_scalar(gatew[:, 1, :], rs[:, 5, :], -0.5, 0.5, ALU.mult, ALU.add))

            def shared_add(g):
                for q in range(2):
                    dve.wait_ge(s_sdps, 2 * g + q + 1)
                    hb = h[:, (2 * g + q) * NT * D:(2 * g + q + 1) * NT * D]
                    v.tensor_tensor(hb, hb, bank[6 + q][0:TT, :], ALU.add).then_inc(s_hsh, 1)

            for g in range(1, GR):
                for j in range(FC):
                    shared_hidden(g, j)
                shared_add(g - 1)
            shared_add(GR - 1)

            def x_turned(j, p):
                dve.wait_ge(s_xgTps, j + 1)
                since(dve, s_rups, j - 1)
                v.tensor_copy(xgT[p][:, :, :].rearrange("p c n -> p (c n)"), bank[0][:, 0:D]).then_inc(s_xgT, 1)

            def hidden(j, p):
                dve.wait_ge(s_rg, j + 1)
                since(dve, s_rhTps, j - 1)
                v.tensor_tensor(rh[p][:, :], rg[:, :], bank[2 + 2 * p][:, 0:HALF], ALU.mult).then_inc(s_rh, 1)

            def lowered(j, p):
                dve.wait_ge(s_rdps, j + 1)
                since(dve, s_yst[p], 8 * (j - p))
                v.tensor_copy(ry[p][:, :], bank[6][:, 0:D]).then_inc(s_ry, 1)

            x_turned(0, 0)
            x_turned(1, 1)
            hidden(0, 0)
            x_turned(2, 0)
            hidden(1, 1)

            def tile_step(j, p):
                x_turned(j + 1, 1 - p)
                hidden(j, p)
                lowered(j - 2, p)

            for j in range(2, 5):
                tile_step(j, j % 2)
            with dve.Fori(2, RT // 2 - 1) as i:
                tile_step(2 * i + 1, 1)
                tile_step(2 * i + 2, 0)
            hidden(RT - 1, 1)
            lowered(RT - 3, 1)
            lowered(RT - 2, 0)
            lowered(RT - 1, 1)

            def stats(b, chain, done, st_, mv_, src):
                c = Chain(dve, chain, 4 * b)
                ht = htile(b)
                dve.wait_ge(src, b + 1)
                settle()
                for t in range(NT):
                    c.add(v.bn_stats(st_[:, 6 * t:6 * t + 6], ht[:, t, :]))
                c.wait()
                settle()
                c.add(v.bn_aggr(mv_[:, 0, :], st_[:, 0:6]))
                v.bn_aggr(mv_[:, 1, :], st_[:, 6:12]).then_inc(done, 1)
                c.step(3)

            def normed(b, chain, done, mv_, rstd_, dst):
                c = Chain(dve, chain, 4 * b + 3)
                ht = htile(b)
                c.add(v.tensor_scalar(dst[:, 0, :], ht[:, 0, :], mv_[:, 0, 0:1], rstd_[:, 0:1], ALU.subtract, ALU.mult))
                v.tensor_scalar(dst[:, 1, :], ht[:, 1, :], mv_[:, 1, 0:1], rstd_[:, 1:2], ALU.subtract, ALU.mult).then_inc(done, 1)

            def values1(b, p):
                dve.wait_ge(s_v1ps, b + 1)
                since(dve, s_pv1, 2 * (b - 1))
                for par in range(2):
                    src = bank[3][0:TT, :].rearrange("p (i j d) -> p i j d", j=2, d=HD)
                    dst = vz[p][par][0:TT, :, :, :, :].rearrange("p t i j d -> p (t i) j d")
                    for t in range(NT):
                        ins = v.tensor_tensor(dst[:, 8 * t:8 * t + 8, par, :], src[:, 8 * t:8 * t + 8, par, :],
                                              rows1[:, 0, :].rearrange("p (i j d) -> p i j d", j=2, d=HD)[:, :, par, :], ALU.add)
                        if par == 0 or t == 0:
                            ins.then_inc(v1chx, 1)
                ins.then_inc(s_v1, 1)

            def least(b, u):
                half, t, n, w = UNITS1[u]
                dve.wait_ge(s_sps, NU1 * b + u + 1)
                since(dve, s_ptps, NU1 * b + u - 3)
                settle()
                for i in range(w):
                    col = t * HEADS + half * HH + n + i
                    ins = v.tensor_tensor_reduce(out=ring[u % 4][0:TT, i, :], in0=bank[4 + u % 2][0:TT, i * T:(i + 1) * T],
                                                 in1=fade[t][:, half * HH + n + i, :], scale=1.0, scalar=3e38,
                                                 op0=ALU.add, op1=ALU.min, accum_out=mn[:, col:col + 1])
                ins.then_inc(s_min, 1)

            def probs_turned(b, u):
                if u % 2:
                    return
                half, t, n, w = UNITS1[u]
                dve.wait_ge(s_ptps, NU1 * b + u + 1)
                if u % (NU1 // 2) == 0:
                    since(dve, s_pv1, 2 * b + half - 1)
                v.tensor_copy(pT[half][0:TT, :, n:n + w, t * TT:(t + 1) * TT],
                              bank[6 + u % 2][0:TT, 0:NT * w * TT].rearrange("p (k h q) -> p k h q", k=NT, h=w)).then_inc(s_pt[0], 1)

            def routed4(b):
                dve.wait_ge(s_lg4ps, b + 1)
                v.tensor_scalar(lg[:, bass.ds(b * (NT * NE), NT * NE)], bank[0][0:TT, 0:NT * NE], 1.0, None, ALU.mult).then_inc(s_lg4, 1)

            def sums1(b, p):
                dve.wait_ge(s_p, NU1 * (b + 1))
                v.reciprocal(rinv[:, :, :].rearrange("p t h -> p (t h)"), rsum[p][:, :]).then_inc(s_rinv, 1)
                dve.wait_ge(s_rinv, b + 1)
                since(dve, s_rbps, b)
                v.tensor_copy(rspread[0:TT, :, :].rearrange("p t (h d) -> p (t h) d", d=HD),
                              rinv[:, :, :].rearrange("p t h -> p (t h)").unsqueeze(2).to_broadcast([TT, NT * HEADS, HD])).then_inc(s_rspread, 1)

            def mixed1(b):
                dve.wait_ge(s_rbs, b + 1)
                dve.wait_ge(s_pv1, 2 * b + 2)
                since(dve, s_o1ps, b)
                v.tensor_tensor(yT[:, :, :].rearrange("p c t -> p (c t)"), bank[1][:, 0:KC * T],
                                rbs[:, :, :].rearrange("p c t -> p (c t)"), ALU.mult).then_inc(s_y1, 1)

            def residual1(b):
                dve.wait_ge(s_o1ps, b + 1)
                dve.wait_ge(s_hb, b + 1)
                hb = h[:, bass.ds(b * (NT * D), NT * D)]
                v.tensor_tensor(hb, hb, bank[3][0:TT, :], ALU.add).then_inc(s_h3, 1)
                stats(b, v4ch, s_mv4, st2, mv2, s_h3)

            def normed4(b):
                dve.wait_ge(s_rstd4, b + 1)
                since(dve, s_x4Tps, b)
                normed(b, v4ch, s_x4, mv2, rstd2, x2s)

            def step1(b, p, first=False, second=False, final=False):
                for u in range(NU1):
                    least(b, u)
                    if u >= 3:
                        probs_turned(b, u - 3)
                    elif not first:
                        probs_turned(b - 1, NU1 - 3 + u)
                    if not final:
                        if u == 1:
                            stats(b + 1, v1ch, s_mv1, st, mv, s_comb)
                        elif u == 3:
                            dve.wait_ge(s_rstd1, b + 2)
                            since(dve, s_xT1ps, b + 1)
                            normed(b + 1, v1ch, s_xn1, mv, rstd, xn)
                    if not first:
                        if u == 0:
                            values1(b, p)
                        elif u == 2:
                            sums1(b - 1, 1 - p)
                        elif u == 6:
                            mixed1(b - 1)
                        elif u == 9:
                            residual1(b - 1)
                        elif u == 11:
                            normed4(b - 1)
                    if u == 2 and not (first or second):
                        routed4(b - 2)

            dve.wait_ge(s_fade, 2)
            stats(0, v1ch, s_mv1, st, mv, s_comb)
            dve.wait_ge(s_rstd1, 1)
            normed(0, v1ch, s_xn1, mv, rstd, xn)
            values1(0, 0)
            step1(0, 0, first=True)
            step1(1, 1, second=True)
            step1(2, 0)
            with dve.Fori(1, B // 2 - 1) as i:
                step1(2 * i + 1, 1)
                step1(2 * i + 2, 0)
            step1(B - 1, 1, final=True)
            sums1(B - 1, 1)
            probs_turned(B - 1, NU1 - 2)
            routed4(B - 2)
            mixed1(B - 1)
            residual1(B - 1)
            normed4(B - 1)
            routed4(B - 1)

            dve.wait_ge(s_lg4, B)
            c = Chain(dve, cch2)
            x, e1, pr = rb[:, 0, :], rb[:, 1, :], rb[:, 5, :]
            c(v.tensor_reduce(rs[:, 0, :], grid(lg[:, :]), AX, ALU.max))
            v.tensor_tensor(grid(x), grid(lg[:, :]), over(rs[:, 0, :]), ALU.subtract).then_inc(s_rx, 1)
            dve.wait_ge(s_rexp, 1)
            c(v.tensor_reduce(rs[:, 1, :], grid(e1), AX, ALU.add))
            c(v.reciprocal(rs[:, 2, :], rs[:, 1, :]))
            c(v.tensor_tensor(grid(pr), grid(e1), over(rs[:, 2, :]), ALU.mult))
            top1, top2 = rs[:, 4, :], rs[:, 6, :]
            choose(pr, top1, rs[:, 3, :], rb[:, 2, :])
            c(v.scalar_tensor_tensor(rb[:, 3, :], rb[:, 2, :], -1e30, pr, ALU.mult, ALU.add))
            c(v.tensor_reduce(top2, grid(rb[:, 3, :]), AX, ALU.max))
            c(v.tensor_tensor(rs[:, 1, :], top1, top2, ALU.add))
            c(v.reciprocal(rs[:, 2, :], rs[:, 1, :]))
            c(v.tensor_tensor(rs[:, 0, :], top1, rs[:, 2, :], ALU.mult))
            c(v.tensor_tensor(rs[:, 3, :], top2, rs[:, 2, :], ALU.mult))
            c(v.tensor_tensor(cs[:, :], rs[:, 0, :], rs[:, 3, :], ALU.add))

            for g in range(GR):
                for q in range(2):
                    b = 2 * g + q
                    dve.wait_ge(s_fdps, b + 1)
                    v.tensor_tensor(ftmp[:, :].rearrange("p (t d) -> p t d", t=NT),
                                    bank[6 + q][0:TT, :].rearrange("p (t d) -> p t d", t=NT),
                                    rows1[:, 2:3, :].to_broadcast([TT, NT, D]), ALU.add).then_inc(s_ft, 1)
                    dve.wait_ge(s_ft, b + 1)
                    for t in range(NT):
                        i = NT * b + t
                        hb = h[:, i * D:(i + 1) * D]
                        ins = v.scalar_tensor_tensor(hb, ftmp[:, t * D:(t + 1) * D], cs[:, i:i + 1], hb, ALU.mult, ALU.add)
                        if t == 0:
                            c.add(ins)
                        else:
                            ins.then_inc(s_h4, 1)
                    dve.wait_ge(s_h4, b + 1)
                    c.wait()

        @block.gpsimd
        def _(pool):
            g = nc.gpsimd
            g.memset(EPSC[:, :], EPS).then_inc(gch, 1)
            for i in range(2):
                g.memset(asb[i][:, :, :, :], 0.0).then_inc(gch, 1)
                for par in range(2):
                    g.memset(vz[i][par][:, :, :, :, :], 0.0).then_inc(gch, 1)
            pool.wait_ge(gch, 7)
            pool.sem_inc(s_zero, 1)
            g.memset(zero[:, :], 0.0).then_inc(s_zset, 1)
            pool.wait_ge(s_const, 48)

            def keys(b, p):
                c = Chain(pool, gch, 7 + 6 * b)
                pool.wait_ge(s_G, b + 1)
                since(pool, s_ek, b)
                for r in range(NCH):
                    n = CH * (r + 1)
                    m = CH * r + MIDC
                    ins = g.tensor_tensor(dk[:, :, COFF[r]:COFF[r] + n], G[:, :, m:m + 1].to_broadcast([P, KC, n]),
                                          G[:, :, 0:n], ALU.subtract)
                    if r < NCH - 1:
                        c.add(ins)
                ins.then_inc(s_dk, 1)
                pool.wait_ge(s_ek, b + 1)
                pool.wait_ge(s_ksb, b + 1)
                since(pool, s_aps, 12 * (b - 1))
                for r in range(NCH):
                    n = CH * (r + 1)
                    ins = g.tensor_tensor(kr[p][:, :, COFF[r]:COFF[r] + n], ek[:, :, COFF[r]:COFF[r] + n],
                                          ksb[:, :, 0:n], ALU.mult)
                    if r < NCH - 1:
                        c.add(ins)
                ins.then_inc(s_kr, 1)
                pool.wait_ge(s_qe, b + 1)
                g.tensor_tensor(qb[p][:, 1, :, :], qe[:, 1:2, :].to_broadcast([P, HH, T]),
                                hmask[:, :].unsqueeze(2).to_broadcast([P, HH, T]), ALU.mult).then_inc(s_qb1, 1)
                c.step(6)

            keys(0, 0)
            keys(1, 1)
            with pool.Fori(1, B // 2) as i:
                keys(2 * i, 0)
                keys(2 * i + 1, 1)

            pool.wait_ge(s_zdone, 16 * (RT // 4))
            pool.wait_ge(s_x2all, 16 * B)
            pool.wait_ge(s_slot, 1)
            for i in range(BT):
                for k in range(TOPK):
                    g.indirect_dma_start(xs_dram, bass.IndirectOffsetOnAxis(ap=slot[:, k, i:i + 1], axis=0),
                                         x2[:, i * D:(i + 1) * D], None).then_inc(s_scat, 16)
            pool.wait_ge(s_hsh, 2 * GR)
            pool.wait_ge(s_alpha, 1)
            pool.wait_ge(s_l1c, 16 * 6)
            for t in range(NT):
                g.tensor_tensor(fade[t], dist[:, t:t + 1, :].to_broadcast([TT, HEADS, T]),
                                alpha[:, :].unsqueeze(2).to_broadcast([TT, HEADS, T]), ALU.mult).then_inc(s_fade, 1)

            def gather(b):
                for t in range(NT):
                    for k in range(TOPK):
                        g.indirect_dma_start(yg[b % 2][:, t, k, :], None, ys_dram,
                                             bass.IndirectOffsetOnAxis(ap=slot[:, k, NT * b + t:NT * b + t + 1], axis=0)
                                             ).then_inc(s_yg[b % 2], 16)

            for p in range(2):
                pool.wait_ge(s_yst[p], 16 * (RT // 2))
            gather(0)
            gather(1)
            pool.wait_ge(s_fade, 2)
            for half in range(2):
                g.memset(pT[half][64:P, :, :, :], 0.0).then_inc(g1ch, 1)
            pool.wait_ge(g1ch, 2)
            pool.sem_inc(s_pz, 1)

            def combine(b):
                c = Chain(pool, cch, 5 * b)
                pool.wait_ge(s_yg[b % 2], 16 * NT * TOPK * (b // 2 + 1))
                rows = yg[b % 2]
                for t in range(NT):
                    for k in range(TOPK):
                        i = NT * b + t
                        c.add(g.tensor_scalar(rows[:, t, k, :], rows[:, t, k, :], gatew[:, k, i:i + 1], None, ALU.mult))
                c.wait()
                hb = h[:, b * NT * D:(b + 1) * NT * D].rearrange("p (t d) -> p t d", t=NT)
                c(g.tensor_tensor(hb, hb, rows[:, :, 0, :], ALU.add))
                g.tensor_tensor(hb, hb, rows[:, :, 1, :], ALU.add).then_inc(s_comb, 1)
                c.step(5)

            combine(0)
            for b in range(B):
                p = b % 2
                if b + 1 < B:
                    combine(b + 1)
                pool.wait_ge(s_k1, b + 1)
                since(pool, s_sps, NU1 * (b - 1))
                for half in range(KC):
                    g.tensor_tensor(kb[p][:, half, :, :], ksb1[:, half:half + 1, :].to_broadcast([P, HH, T]),
                                    hmask[:, :].unsqueeze(2).to_broadcast([P, HH, T]), ALU.mult).then_inc(s_kb, 1)
                hb = h[:, b * NT * D:(b + 1) * NT * D].rearrange("p (t d) -> p t d", t=NT)
                pool.wait_ge(s_xn1, b + 1)
                g.tensor_tensor(hb, hb, rows1[:, 1:2, :].to_broadcast([TT, NT, D]), ALU.add).then_inc(s_hb, 1)
                if b + 2 < B:
                    pool.wait_ge(s_comb, b + 1)
                    gather(b + 2)


def laid_out(inputs):
    import numpy as np
    f = {k: np.asarray(v) for k, v in inputs.items()}

    def rows(w):
        return np.ascontiguousarray(w.reshape(-1, P, w.shape[-1]).transpose(1, 0, 2))

    def column(v, rep=1):
        return np.ascontiguousarray(np.repeat(v, rep).reshape(-1, P).T)

    o = {}
    x = f["x"].reshape(B, 3, 6, 16, 6, 16).transpose(0, 1, 3, 5, 2, 4).reshape(B * IMG, PC * P)
    o["patches"] = rows(x.T)
    o["tok_w"] = rows(f["L0_tok_W"])
    o["txt"] = f["txt"]
    o["ident"] = np.eye(P, dtype=np.float32)
    o["hmask"] = (np.arange(P)[:, None] // HD == np.arange(HH)[None]).astype(np.float32)
    k, q = np.arange(TT)[:, None, None], np.arange(CH)[None, None]
    o["cmask"] = (k <= q + CH * np.arange(2)[None, :, None]).astype(np.int32)
    for n, s in (("wq", "q_w"), ("wk", "k_w"), ("wv", "v_w"), ("wo", "o_w"), ("cw1", "cs_w1")):
        o[n] = rows(f["L0_attn_" + s].T)
    o["cb1"] = f["L0_attn_cs_b1"].reshape(64, 1)
    o["cw2"] = np.ascontiguousarray(np.repeat(f["L0_attn_cs_w2"].T, HD, axis=1))
    o["cb2"] = column(f["L0_attn_cs_b2"], HD)
    o["dec"] = column(f["L0_attn_decay_params"].reshape(-1))
    up = f["L0_ffn_w_up"].transpose(2, 0, 1)
    o["eup"] = rows(up.reshape(D, NE * 2 * HALF))
    o["edn"] = rows(f["L0_ffn_w_down"].transpose(2, 0, 1).reshape(HALF, NE * D))
    o["sup"] = rows(np.concatenate([f["L0_ffn_sg_gate"].T, f["L0_ffn_sg_up"].T], axis=1))
    o["sdn"] = rows(f["L0_ffn_sg_down"].T)
    o["gw"] = rows(f["L0_ffn_gate_w"].T)
    o["tri"] = np.triu(np.ones((TT, TT), np.float32), 1)
    o["rc"] = np.ascontiguousarray(np.broadcast_to(np.concatenate([
        np.tile(NE - np.arange(NE), BT), np.tile(np.arange(BT) > 0, NE),
        np.repeat(np.arange(RT), NE), np.arange(NE)]).astype(np.float32), (TT, 2 * BT * NE + RT * NE + NE)))
    qkv = f["L1_attn_qkv_w"].T
    for n, w in (("wq1", qkv[:, 0:D]), ("wk1", qkv[:, D:2 * D]), ("wv1", qkv[:, 2 * D:]), ("wo1", f["L1_attn_out_w"].T),
                 ("rw", f["L1_ffn_router_w"]), ("w1", f["L1_ffn_w1"]), ("w2", f["L1_ffn_w2"])):
        o[n] = rows(w)
    qkv_b = f["L1_attn_qkv_b"]
    o["qkb"] = np.ascontiguousarray(np.stack([column(qkv_b[0:D]), column(qkv_b[D:2 * D])], axis=1))
    o["b1"] = column(f["L1_ffn_b1"])
    o["rows1"] = np.ascontiguousarray(np.broadcast_to(
        np.stack([qkv_b[2 * D:], f["L1_attn_out_b"], f["L1_ffn_b2"]]), (TT, 3, D)))
    o["alpha"] = np.ascontiguousarray(np.broadcast_to(f["L1_attn_decay_alpha"], (TT, HEADS)))
    pos = np.arange(T, dtype=np.float32)
    o["dist"] = np.ascontiguousarray(np.abs(pos.reshape(NT, TT, 1) - pos).transpose(1, 0, 2))
    return o


OUT_SHAPE = (B, T, D)


def kernel(**inputs):
    import numpy as np
    import concourse.bacc as bacc
    from concourse.bass_utils import run_bass_kernel_spmd

    nc = bacc.Bacc("TRN2", target_bir_lowering=False, num_devices=1)
    arrays = laid_out(inputs)
    aps = {n: nc.dram_tensor("in_" + n, x.shape, mybir.dt.from_np(x.dtype), kind="ExternalInput").ap()
           for n, x in arrays.items()}
    out = nc.dram_tensor("out", OUT_SHAPE, mybir.dt.float32, kind="ExternalOutput").ap()
    early_fusion_kernel(nc, aps, out)
    r = run_bass_kernel_spmd(nc, [{"in_" + n: x for n, x in arrays.items()}], core_ids=[0])
    return r.results[0]["out"]
```

```python
import concourse.bass as bass
from concourse import mybir
from contextlib import ExitStack

B, T, D = 8, 164, 256
IMG, TXT = 36, 128
P = 128
KC = D // P
NT = 2
TT = T // NT
HEADS, HD = 16, 16
HH = HEADS // KC
PC = 6
CH = 41
NCH = T // CH
COFF = [CH * r * (r + 1) // 2 for r in range(NCH + 1)]
KW = COFF[NCH]
MIDC = CH // 2
BT = B * NT
LAM_MIN, LAM_MAX = 0.02, 0.9995
NE, TOPK, HALF = 8, 2, 384
FC = HALF // P
FF = 1024
FFC = FF // P
GR = 4
GN = B * T // GR
SLOTS = P
RT = (TOPK * B * T + NE * (SLOTS - 1)) // SLOTS
SCALE = 4.0
EPS = 1e-5


class Chain:

    def __init__(self, eng, sem, base=0):
        self.eng, self.sem, self.base, self.n = eng, sem, base, 0

    def add(self, ins):
        ins.then_inc(self.sem, 1)
        self.n += 1

    def wait(self):
        self.eng.wait_ge(self.sem, self.base + self.n)

    def __call__(self, ins):
        self.add(ins)
        self.wait()

    def step(self, n):
        assert self.n == n, (self.n, n)


def early_fusion_kernel(nc, a, out):
    f32, f16, i32, u32 = mybir.dt.float32, mybir.dt.float16, mybir.dt.int32, mybir.dt.uint32
    ALU = mybir.AluOpType
    ACT = mybir.ActivationFunctionType

    ctx = ExitStack()
    with ctx:
        def sb(name, shape, dt=f32):
            return ctx.enter_context(nc.sbuf_tensor(name, shape, dt))

        def sem(name):
            return ctx.enter_context(nc.semaphore(name))

        bank = [ctx.enter_context(nc.psum_tensor(f"bank{i}", [P, 512], f32)) for i in range(8)]

        h = sb("h", [TT, B * NT * D])
        h4 = h[:, :].rearrange("p (b t d) -> p b t d", b=B, t=NT)
        ident = sb("ident", [P, P])
        hmask = sb("hmask", [P, HH])
        cmask = sb("cmask", [TT, 2, CH], i32)
        ones = sb("ones", [P, T])
        EPSC = sb("eps_column", [P, 1])
        tok = sb("tok", [3 * IMG, 3, D])
        wq = sb("wq", [P, KC, D])
        wk = sb("wk", [P, KC, D])
        wv = sb("wv", [P, KC, D])
        wo = sb("wo", [P, KC, D])
        cw1 = sb("cw1", [P, KC, 64])
        cb1 = sb("cb1", [64, 1])
        cw2 = sb("cw2", [64, D])
        cb2 = sb("cb2", [P, KC])
        dec = sb("dec", [P, KC])
        base = sb("base", [P, KC])
        base02 = sb("base02", [P, KC])
        eup = sb("eup", [P, KC, NE * 2 * HALF])
        flat = eup[:, :, :].rearrange("p c n -> p (c n)")
        used = [0]

        def carve(*shape):
            n = 1
            for x in shape:
                n *= x
            v = flat[:, used[0]:used[0] + n]
            used[0] += n
            assert used[0] <= KC * NE * 2 * HALF
            if len(shape) == 2:
                v = v.rearrange("p (a b) -> p a b", a=shape[0])
            elif len(shape) == 3:
                v = v.rearrange("p (a b c) -> p a b c", a=shape[0], b=shape[1])
            return v

        st = sb("st", [TT, NT * 6])
        mv = sb("mv", [TT, NT, 2])
        lnv = sb("lnv", [TT, NT])
        rstd = sb("rstd", [TT, NT])
        xn = sb("xn", [TT, NT, D])
        xnT = sb("xnT", [P, KC, T])
        th = sb("th", [64, T])
        lc = carve(KC, T)
        lam = carve(KC, T)
        lnlam = carve(KC, T)
        G = carve(KC, T)
        dq = carve(KC * T)
        dk = carve(KC, KW)
        eq = carve(KC * T)
        ek = carve(KC, KW)
        ksb = carve(KC, T)
        qe = carve(KC, T)
        kr = [carve(KC, KW) for i in range(2)]
        qb = [sb(f"qb{i}", [P, KC, HH, T]) for i in range(2)]
        spare = [qb[i][:, :, :, :].rearrange("p c h t -> p (c h t)") for i in range(2)]
        xp = spare[0][:, 0:PC * B * IMG].rearrange("p (c n) -> p c n", c=PC)
        tokw = spare[1][:, 0:PC * D].rearrange("p (c n) -> p c n", c=PC)
        sgate = [spare[0][:, 0:FC * GN].rearrange("p (j n) -> p j n", j=FC)]
        shid = [spare[i][:, FC * GN:2 * FC * GN].rearrange("p (j n) -> p j n", j=FC) for i in range(2)]
        vz = [[sb(f"vz{i}_{par}", [P, NT, HEADS // 2, 2, HD]) for par in range(2)] for i in range(2)]
        asb = [carve(NT, HH, T) for i in range(2)]
        yT = sb("yT", [P, KC, T])

        shared_w = sb("shared_w", [P, KC * 2 * HALF + FC * D])
        sup = shared_w[:, 0:KC * 2 * HALF].rearrange("p (c n) -> p c n", c=KC)
        sdn = shared_w[:, KC * 2 * HALF:].rearrange("p (j n) -> p j n", j=FC)
        edn = sb("edn", [P, FC, NE * D])
        gw = sb("gw", [P, KC, NE])
        st2 = sb("st2", [TT, NT * 6])
        mv2 = sb("mv2", [TT, NT, 2])
        lnv2 = sb("lnv2", [TT, NT])
        rstd2 = sb("rstd2", [TT, NT])
        x2s = sb("x2s", [TT, NT, D])
        x2Ts = sb("x2Ts", [P, KC, T])
        x2w = sb("x2w", [P, BT * D])
        x2 = x2w[0:TT, :]
        w1 = x2w[:, 0:KC * FF].rearrange("p (c n) -> p c n", c=KC)
        w2 = x2w[:, KC * FF:KC * FF + FFC * D].rearrange("p (j n) -> p j n", j=FFC)
        wparts = x2w[:, :].bitcast(f16).rearrange("p (n k) -> p n k", k=2)
        w1p = wparts[:, 0:KC * FF, :].rearrange("p (c n) k -> p c n k", c=KC)
        w2p = wparts[:, KC * FF:KC * FF + FFC * D, :].rearrange("p (j n) k -> p j n k", j=FFC)
        x2T = sb("x2T", [P, KC, B * T])
        tri = sb("tri", [TT, TT])
        rc = sb("rc", [TT, BT * NE + BT * NE + RT * NE])
        desc = rc[:, 0:BT * NE].rearrange("p (i e) -> p i e", e=NE)
        fresh = rc[:, BT * NE:2 * BT * NE]
        tileno = rc[:, 2 * BT * NE:].rearrange("p (j e) -> p j e", e=NE)
        lg = sb("lg", [TT, BT * NE])
        rb = sb("rb", [TT, 12, BT * NE])
        rs = sb("rs", [TT, 8, BT])
        r8 = sb("r8", [TT, 6, NE])
        r8i = sb("r8i", [TT, 2, NE], i32)
        slotf = sb("slotf", [TT, TOPK, BT])
        slot = sb("slot", [TT, TOPK, BT], u32)
        gatew = sb("gatew", [TT, TOPK, BT])
        texp = sb("texp", [TT, RT * NE])
        texpf = sb("texpf", [TT, RT])
        texpi = sb("texpi", [TT, RT], i32)
        WSPLIT = 4
        WN = BT * D // WSPLIT
        wtmp = x2T[:, 1, 0:WN // 2].bitcast(f16)
        zero = x2T[:, :, :].rearrange("p c n -> p (c n)")[:, 0:1024]
        tiles = sb("tiles", [P, 6 * D + 3 * HALF + FC * P])
        xg = [tiles[:, i * D:(i + 1) * D] for i in range(2)]
        ry = [tiles[:, (2 + i) * D:(3 + i) * D] for i in range(2)]
        rg, *rh = [tiles[:, 6 * D + i * HALF:6 * D + (i + 1) * HALF] for i in range(3)]
        eupp = flat.bitcast(f16).rearrange("p (c n k) -> p c n k", c=KC, k=2)
        downflat = edn[:, :, :].rearrange("p j n -> p (j n)")
        ednp = downflat.bitcast(f16).rearrange("p (j n k) -> p j n k", j=FC, k=2)
        EN = NE * 2 * HALF // 4
        PIECES = [(w[:, n:n + EN], w.bitcast(f16).rearrange("p (n k) -> p n k", k=2)[:, n:n + EN, :])
                  for w, total in ((downflat, FC * NE * D), (flat, KC * NE * 2 * HALF)) for n in range(0, total, EN)]
        DOWN = FC * NE * D // EN
        etmp = [tiles[:, 6 * D + i * EN // 2:6 * D + (i + 1) * EN // 2].bitcast(f16) for i in range(2)]
        xgTp = [tiles[:, (4 + i) * D:(5 + i) * D].bitcast(f16).rearrange("p (k c n) -> p k c n", k=2, c=KC) for i in range(2)]
        rhTp = [x.bitcast(f16).rearrange("p (i k n) -> p i k n", i=2, k=FC)
                for x in (tiles[:, 6 * D + 3 * HALF:], x2T[:, 0, 0:FC * P])]
        yg = [tiles[0:TT, i * NT * TOPK * D:(i + 1) * NT * TOPK * D].rearrange("p (t k d) -> p t k d", t=NT, k=TOPK) for i in range(2)]
        used[0] = 0
        pT = [carve(NT, HH, T) for i in range(2)]
        ring = [carve(3, T) for i in range(4)]
        q1 = [carve(KC, T) for i in range(2)]
        ksb1 = carve(KC, T)
        rbs = carve(KC, T)
        rspread = carve(NT, D)
        hid = [carve(FFC, GN)]
        late = hid[0].rearrange("p j n -> p (j n)")
        sgate.append(late[:, 0:FC * GN].rearrange("p (j n) -> p j n", j=FC))
        shid.append(late[:, FC * GN:2 * FC * GN].rearrange("p (j n) -> p j n", j=FC))
        ednf = edn[:, :, :].rearrange("p j n -> p (j n)")
        kb = [ednf[:, i * KC * HH * T:(i + 1) * KC * HH * T].rearrange("p (c h t) -> p c h t", c=KC, h=HH) for i in range(2)]
        hid.append(ednf[:, 0:FFC * GN].rearrange("p (j n) -> p j n", j=FFC))
        fade = [spare[i][0:TT, :].rearrange("p (h t) -> p h t", h=HEADS) for i in range(2)]
        dist = sb("dist", [TT, NT, T])
        arow = sb("arow", [TT, HEADS])
        aabs = sb("aabs", [TT, 2, HEADS])
        alpha = sb("alpha", [TT, HEADS])
        rows1 = sb("rows1", [TT, 2, D])
        qkb = sb("qkb", [P, 2, KC])
        nqb = sb("nqb", [P, KC])
        b1c = sb("b1c", [P, FFC])
        rw = sb("rw", [P, KC, NE])
        mn = sb("mn", [TT, NT * HEADS])
        rsum = [sb(f"rsum{i}", [TT, NT * HEADS]) for i in range(2)]
        rinv = sb("rinv", [TT, NT, HEADS])
        wqp, wkp, wvp = [w[:, :, :].rearrange("p c n -> p (c n)").bitcast(f16).rearrange("p (c n k) -> p c n k", c=KC, k=2) for w in (wq, wk, wv)]
        xnTp = xnT[:, :, :].rearrange("p c t -> p (c t)").bitcast(f16).rearrange("p (k c t) -> p k c t", k=2, c=KC)
        b2c = sb("b2c", [P, KC])
        xpart = [tiles[:, (2 + i) * KC * GN:(3 + i) * KC * GN].bitcast(f16).rearrange("p (k c n) -> p k c n", k=2, c=KC) for i in range(2)]
        hid32 = [ring[i].rearrange("p n t -> p (n t)")[:, 0:GN] for i in range(2)]
        hidp = [x.rearrange("p j n -> p (j n)").bitcast(f16).rearrange("p (k j n) -> p k j n", k=2, j=FFC) for x in hid]
        ffT = [tiles[:, i * KC * GN:(i + 1) * KC * GN].rearrange("p (o n) -> p o n", o=KC) for i in range(2)]
        cs = sb("cs", [TT, BT])

        s_l1c, s_w1in, s_wff = sem("l1_const_in"), sem("l1_weights_in"), sem("ff_weights_in")
        s_al, s_alpha, s_fade, s_nqb, s_pz = sem("alpha_parts"), sem("alpha"), sem("fade"), sem("nqb"), sem("pT_zeroed")
        s_mv1, s_rstd1, s_xn1, s_xT1ps, s_xT1 = [sem(n) for n in ("mv1", "rstd1", "xn1", "xT1_ps", "xT1_sb")]
        s_xTp1 = sem("xT1_parts")
        s_q1ps, s_k1ps, s_v1ps, s_q1, s_k1, s_v1, s_kb, s_hb = [sem(n) for n in ("q1_ps", "k1_ps", "v1_ps", "q1_sb", "k1_sb", "v1_sb", "k1_masked", "h_biased")]
        s_sps, s_min, s_p, s_ptps, s_pv1 = [sem(n) for n in ("logits1_ps", "logits1_sb", "probs", "probsT_ps", "pv1_ps")]
        s_pt = [sem(f"probsT_sb{i}") for i in range(2)]
        s_rspread = sem("rinv_spread")
        s_rinv, s_rbps, s_rbs, s_y1, s_o1ps, s_h3 = [sem(n) for n in ("rinv", "rb_ps", "rb_sb", "y1_sb", "o1_ps", "h_attn1")]
        s_mv4, s_rstd4, s_x4, s_x4Tps, s_x4T, s_lg4ps, s_lg4, s_x4Tall = [sem(n) for n in ("mv4", "rstd4", "x4", "x4T_ps", "x4T_sb", "router_ps", "router_sb", "x4T_all")]
        s_fyps, s_gelu, s_xpart, s_wsplit = [sem(n) for n in ("ff_turned_ps", "ff_gelu", "ff_token_parts", "ff_weight_parts")]
        s_fups, s_hid, s_fdps, s_ft, s_h4, s_rexp, s_rx = [sem(n) for n in ("ff_up_ps", "ff_hidden", "ff_down_ps", "ff_biased", "h_final", "router_exp", "router_shifted")]

        xs_dram = nc.dram_tensor("routed_in", (RT * SLOTS, D), f32, kind="Internal").ap()
        ys_dram = nc.dram_tensor("routed_out", (RT * SLOTS, D), f32, kind="Internal").ap()

        s_rc, s_wf, s_zset, s_zdone = sem("routing_const_in"), sem("wf_in"), sem("zero_set"), sem("slots_zeroed")
        s_mv2, s_rstd2, s_x2 = sem("mv2_ready"), sem("rstd2_ready"), sem("x2_ready")
        s_x2Tps, s_x2T, s_lgps, s_lg = sem("x2T_ps"), sem("x2T_sb"), sem("logits_ps"), sem("logits_sb")
        s_x2all, s_x2Tall = sem("x2_all"), sem("x2T_all")
        vch2, ach2, rch = sem("dve_chain2"), sem("act_chain2"), sem("routing_chain")
        s_gap, s_gw, s_m12, s_rps = sem("logit_gap"), sem("tanh_gap"), sem("choices"), sem("prefix_ps")
        s_slot, s_texp = sem("slots_known"), sem("tile_experts")
        s_eup = [sem(f"eup_in{c}") for c in range(KC)]
        s_eround, s_elow, s_ehigh = sem("expert_rounded"), sem("expert_low"), sem("expert_parts")
        s_xgTp, s_rhTp = sem("xgT_parts"), sem("rhT_parts")
        s_scat, s_xg = sem("scattered"), [sem(f"xg_in{i}") for i in range(2)]
        s_sups, s_sg, s_shid, s_sdps, s_hsh = sem("shared_up_ps"), sem("shared_gate_sb"), sem("shared_hidden"), sem("shared_down_ps"), sem("h_shared")
        s_xgTps, s_xgT, s_rups, s_rg, s_rh = sem("xgT_ps"), sem("xgT_sb"), sem("routed_up_ps"), sem("routed_gate_sb"), sem("routed_hidden")
        s_rhTps, s_rhT, s_rdps, s_ry, s_yst = sem("rhT_ps"), sem("rhT_sb"), sem("routed_down_ps"), sem("routed_y_sb"), [sem(f"routed_stored{i}") for i in range(2)]
        s_yg = [sem(f"gathered{i}") for i in range(2)]
        s_comb, cch = sem("combined"), sem("combine_chain")

        s_const, s_tokin, s_txt, s_w0 = sem("const_in"), sem("tok_in"), sem("txt_in"), sem("w0_in")
        s_tokps, s_toksb, s_tokh0, s_tokh = sem("tok_ps"), sem("tok_sb"), sem("tok0_in_h"), sem("tok_in_h")
        s_base = sem("base_ready")
        nch, vch, ach, gch = sem("dve_norm_chain"), sem("dve_chain"), sem("act_chain"), sem("pool_chain")
        s_mv, s_rstd, s_xn = sem("mv_ready"), sem("rstd_ready"), sem("xn_ready")
        s_xTps, s_xT = sem("xT_ps"), sem("xT_sb")
        s_z1, s_q, s_k, s_v = sem("z1_ps"), sem("q_ps"), sem("k_ps"), sem("v_ps")
        s_th, s_z2, s_lc = sem("tanh_sb"), sem("z2_ps"), sem("lc_sb")
        s_lam, s_lnlam, s_G = sem("lam_sb"), sem("lnlam_sb"), sem("G_sb")
        s_dq, s_dk, s_eq, s_ek = sem("dq_sb"), sem("dk_sb"), sem("eq_sb"), sem("ek_sb")
        s_ksb, s_vsb, s_qe, s_kr = sem("k_sb"), sem("v_sb"), sem("qe_sb"), sem("kr_sb")
        s_qb0, s_qb1 = sem("qb_half0"), sem("qb_half1")
        s_aps, s_adve, s_aact, s_pv = sem("scores_ps"), sem("scores_dve"), sem("scores_act"), sem("pv_ps")
        s_ysb, s_ops, s_h1 = sem("y_sb"), sem("o_ps"), sem("h_attn0")
        s_settled = sem("dve_waits_met")
        s_out = sem("out_done")

        UNITS = [(0, 0), (1, 0), (2, 0), (2, 1), (3, 0), (3, 1)]
        MASKED = [0, 1, 3, 5]
        PLAIN = [2, 4]
        UNITS1 = [(half, t, n, min(3, HH - n)) for half in range(KC) for t in range(NT) for n in range(0, HH, 3)]
        NU1 = len(UNITS1)
        UPBANK = [4, 5, 6, 7] + [(1, 2, 0, 3)[n % 4] for n in range(4, FFC * GR)]

        def since(eng, s, v):
            if not isinstance(v, int) or v > 0:
                eng.wait_ge(s, v)

        def htile(b):
            return h[:, bass.ds(b * (NT * D), NT * D)].rearrange("p (t d) -> p t d", t=NT)

        PRODUCTS = [(0, 0), (0, 1), (1, 0)]

        block = ctx.enter_context(nc.Block())

        @block.sync
        def _(sp):
            sp.dma_start(xp[:, :, :], a["patches"]).then_inc(s_tokin, 16)
            sp.dma_start(tokw[:, :, :], a["tok_w"]).then_inc(s_tokin, 16)
            sp.dma_start(h4[IMG:TT, :, 0, :], a["txt"][:, 0:TT - IMG, :].rearrange("b p d -> p b d")).then_inc(s_txt, 16)
            sp.dma_start(h4[:, :, 1, :], a["txt"][:, TT - IMG:TXT, :].rearrange("b p d -> p b d")).then_inc(s_txt, 16)
            for dst, src in ((ident, "ident"), (hmask, "hmask")):
                sp.dma_start(dst[:, :], a[src]).then_inc(s_const, 16)
            sp.dma_start(cmask[:, :, :], a["cmask"]).then_inc(s_const, 16)
            for dst, src in ((wq, "wq"), (wk, "wk"), (wv, "wv"), (wo, "wo"), (cw1, "cw1"), (gw, "gw")):
                sp.dma_start(dst[:, :, :], a[src]).then_inc(s_w0, 16)
            for dst, src in ((cb1, "cb1"), (cw2, "cw2"), (cb2, "cb2"), (dec, "dec")):
                sp.dma_start(dst[:, :], a[src]).then_inc(s_w0, 16)
            for b in range(B):
                i, j = divmod(b, 3)
                sp.wait_ge(s_toksb, i + 1)
                sp.dma_start(h4[0:IMG, b, 0, :], tok[IMG * j:IMG * j + IMG, i, :]).then_inc(s_tokh0 if i == 0 else s_tokh, 16)
            for dst, src in ((tri, "tri"), (rc, "rc")):
                sp.dma_start(dst[:, :], a[src]).then_inc(s_rc, 16)
            for dst, src in ((sup, "sup"), (sdn, "sdn"), (edn[:, :, :], "edn")):
                sp.dma_start(dst, a[src]).then_inc(s_wf, 16)
            for dst, src in ((arow, "alpha"), (b1c, "b1"), (b2c, "b2")):
                sp.dma_start(dst[:, :], a[src]).then_inc(s_l1c, 16)
            for dst, src in ((dist, "dist"), (rows1, "rows1"), (qkb, "qkb"), (rw, "rw")):
                sp.dma_start(dst[:, :, :], a[src]).then_inc(s_l1c, 16)
            sp.wait_ge(s_zset, 1)
            for n in range(RT // 4):
                sp.dma_start(xs_dram[4 * n * SLOTS:4 * (n + 1) * SLOTS, :].rearrange("(p k) d -> p (k d)", p=P),
                             zero[:, :]).then_inc(s_zdone, 16)
            sp.wait_ge(s_zdone, 16 * (RT // 4))
            with sp.Fori(0, B) as b:
                sp.wait_ge(s_x2, b + 1)
                sp.dma_start(x2[:, bass.ds(b * (NT * D), NT * D)],
                             x2s[:, :, :].rearrange("p t d -> p (t d)")).then_inc(s_x2all, 16)
                sp.wait_ge(s_x2T, b + 1)
                sp.dma_start(x2T[:, :, bass.ds(b * T, T)], x2Ts[:, :, :]).then_inc(s_x2Tall, 16)

            sp.wait_ge(s_h1, B)
            for c in range(KC):
                sp.dma_start(eup[:, c, :], a["eup"][:, c, :]).then_inc(s_eup[c], 16)
            for dst, src in ((wq, "wq1"), (wk, "wk1"), (wv, "wv1"), (wo, "wo1")):
                sp.dma_start(dst[:, :, :], a[src]).then_inc(s_w1in, 16)
            sp.wait_ge(s_scat, 16 * TOPK * BT)

            def load(j, p):
                since(sp, s_xgTps, j - 1)
                sp.dma_start(xg[p][:, :], xs_dram[bass.ds(j * SLOTS, SLOTS), :]).then_inc(s_xg[p], 16)

            def store(j, p):
                sp.wait_ge(s_ry, j + 1)
                sp.dma_start(ys_dram[bass.ds(j * SLOTS, SLOTS), :], ry[p][:, :]).then_inc(s_yst[p], 16)

            for j in range(4):
                load(j, j % 2)
            sp.dma_start(w1, a["w1"]).then_inc(s_wff, 16)
            sp.dma_start(w2, a["w2"]).then_inc(s_wff, 16)
            load(4, 0)
            load(5, 1)
            store(0, 0)
            with sp.Fori(2, RT // 2 - 1) as i:
                load(2 * i + 2, 0)
                store(2 * i - 3, 1)
                load(2 * i + 3, 1)
                store(2 * i - 2, 0)
            for j in range(RT - 5, RT):
                store(j, j % 2)
            with sp.Fori(0, B) as b:
                sp.wait_ge(s_x4T, b + 1)
                sp.dma_start(x2T[:, :, bass.ds(b * T, T)], x2Ts[:, :, :]).then_inc(s_x4Tall, 16)
            for b in range(B):
                sp.wait_ge(s_h4, b + 1)
                sp.dma_start(out[b].rearrange("(t p) d -> p t d", t=NT), h4[:, b, :, :]).then_inc(s_out, 16)
            sp.wait_ge(s_out, 16 * B)

        @block.tensor
        def _(pe):
            mm = nc.tensor.matmul
            pe.wait_ge(s_tokin, 32)
            for i in range(3):
                n = IMG * min(3, B - 3 * i)
                for c in range(PC):
                    last = mm(bank[i][0:n, 0:D], xp[:, c, 3 * IMG * i:3 * IMG * i + n], tokw[:, c, :],
                              start=(c == 0), stop=(c == PC - 1))
                last.then_inc(s_tokps, 1)
            pe.wait_ge(s_w0, 16 * 10)
            pe.wait_ge(s_const, 16 * 3)
            pe.wait_ge(s_toksb, 3)

            def turn(b):
                pe.wait_ge(s_xn, b + 1)
                since(pe, s_lc, 2 * b)
                since(pe, s_x2T, b - 2)
                for t in range(NT):
                    for c in range(KC):
                        last = nc.tensor.transpose(bank[0][:, c * T + t * TT:c * T + (t + 1) * TT],
                                                   xn[:, t, c * P:(c + 1) * P], ident[0:TT, 0:TT])
                last.then_inc(s_xTps, 1)

            def gate_in(b):
                pe.wait_ge(s_xT, b + 1)
                for c in range(KC):
                    last = mm(bank[0][0:64, 0:T], cw1[:, c, :], xnT[:, c, :], start=(c == 0), stop=(c == KC - 1))
                last.then_inc(s_z1, 1)

            def gate_out(b):
                pe.wait_ge(s_th, b + 1)
                for o in range(KC):
                    last = mm(bank[0][:, o * T:(o + 1) * T], cw2[:, o * P:(o + 1) * P], th[:, :], start=True, stop=True)
                last.then_inc(s_z2, 1)

            def keys_queries(b):
                since(pe, s_ksb, b)
                for o in range(KC):
                    for c in range(KC):
                        last = mm(bank[2][:, o * T:(o + 1) * T], wk[:, c, o * P:(o + 1) * P], xnT[:, c, :],
                                  start=(c == 0), stop=(c == KC - 1))
                last.then_inc(s_k, 1)
                since(pe, s_qe, b)
                for o in range(KC):
                    for c in range(KC):
                        last = mm(bank[1][:, o * T:(o + 1) * T], wq[:, c, o * P:(o + 1) * P], xnT[:, c, :],
                                  start=(c == 0), stop=(c == KC - 1))
                last.then_inc(s_q, 1)

            def values(b):
                since(pe, s_vsb, b)
                for t in range(NT):
                    for c in range(KC):
                        last = mm(bank[3][0:TT, t * D:(t + 1) * D], xnT[:, c, t * TT:(t + 1) * TT], wv[:, c, :],
                                  start=(c == 0), stop=(c == KC - 1))
                last.then_inc(s_v, 1)

            def scores(b, p, half, pair):
                if pair == 0:
                    pe.wait_ge(s_kr, b + 1)
                    pe.wait_ge(s_qb0 if half == 0 else s_qb1, b + 1)
                for u in (2 * pair, 2 * pair + 1):
                    r, t = UNITS[u]
                    if u == 0:
                        since(pe, s_aact, 4 * b + 2 * half)
                    elif u == 4:
                        pe.wait_ge(s_aact, 4 * b + 2 * half + 1)
                    else:
                        since(pe, s_adve, 8 * b + 4 * half + [None, 0, 1, 2, None, 3][u])
                    m = min(TT, CH * (r + 1) - TT * t)
                    mm(bank[4 + u % 2][0:m, 0:HH * CH],
                       kr[p][:, half, COFF[r] + TT * t:COFF[r] + TT * t + m],
                       qb[p][:, half, :, CH * r:CH * (r + 1)], start=True, stop=True).then_inc(s_aps, 1)

            def mix(b, p, half):
                pe.wait_ge(s_adve, 8 * b + 4 * half + 4)
                pe.wait_ge(s_aact, 4 * b + 2 * half + 2)
                pe.wait_ge(s_vsb, b + 1)
                since(pe, s_ysb, b)
                for t in range(NT):
                    for par in range(2):
                        for i in range(4):
                            last = mm(bank[6][32 * i:32 * i + 32, half * T + t * TT:(half + 1) * T],
                                      vz[p][par][:, t, 4 * half + i, :, :],
                                      asb[half][:, t, 2 * i + par, t * TT:T],
                                      start=(t == 0 and par == 0), stop=(t == 1 and par == 1),
                                      skip_group_check=True, tile_position=(0, 32 * i))
                last.then_inc(s_pv, 1)

            def project_out(b):
                pe.wait_ge(s_ysb, b + 1)
                since(pe, s_lg, b)
                for t in range(NT):
                    for c in range(KC):
                        last = mm(bank[7][0:TT, t * D:(t + 1) * D], yT[:, c, t * TT:(t + 1) * TT], wo[:, c, :],
                                  start=(c == 0), stop=(c == KC - 1))
                last.then_inc(s_ops, 1)

            def turn2(b, final=False):
                pe.wait_ge(s_x2, b + 1)
                if final:
                    pe.wait_ge(s_x2T, b)
                else:
                    pe.wait_ge(s_lc, 2 * (b + 3))
                for t in range(NT):
                    for c in range(KC):
                        last = nc.tensor.transpose(bank[0][:, c * T + t * TT:c * T + (t + 1) * TT],
                                                   x2s[:, t, c * P:(c + 1) * P], ident[0:TT, 0:TT])
                last.then_inc(s_x2Tps, 1)

            def route(b):
                pe.wait_ge(s_x2T, b + 1)
                pe.wait_ge(s_h1, b + 1)
                for t in range(NT):
                    for c in range(KC):
                        last = mm(bank[7][0:TT, t * NE:(t + 1) * NE], x2Ts[:, c, t * TT:(t + 1) * TT], gw[:, c, :],
                                  start=(c == 0), stop=(c == KC - 1))
                last.then_inc(s_lgps, 1)

            def step(b, p, first=False, final=False):
                if not final:
                    turn(b + 1)
                if first:
                    gate_in(b + 1)
                    gate_out(b + 1)
                scores(b, p, 0, 0)
                if not (first or final):
                    gate_in(b + 1)
                if not first:
                    mix(b - 1, 1 - p, 1)
                if not (first or final):
                    gate_out(b + 1)
                scores(b, p, 0, 1)
                if not final:
                    keys_queries(b + 1)
                if not first:
                    project_out(b - 1)
                scores(b, p, 0, 2)
                scores(b, p, 1, 0)
                if not final:
                    values(b + 1)
                scores(b, p, 1, 1)
                mix(b, p, 0)
                if not first:
                    if final:
                        pe.wait_ge(s_lc, 2 * B)
                    turn2(b - 1, final)
                scores(b, p, 1, 2)
                if not first:
                    route(b - 1)

            turn(0)
            gate_in(0)
            keys_queries(0)
            gate_out(0)
            values(0)
            step(0, 0, first=True)
            step(1, 1)
            with pe.Fori(1, B // 2 - 1) as i:
                step(2 * i, 0)
                step(2 * i + 1, 1)
            step(B - 2, 0)
            step(B - 1, 1, final=True)
            mix(B - 1, 1, 1)
            project_out(B - 1)
            turn2(B - 1, final=True)
            route(B - 1)

            def shared_up(g, j):
                if g == 0:
                    pe.wait_ge(s_lg, B)
                else:
                    pe.wait_ge(s_shid, FC * (g - 1) + j + 1)
                for half in range(2):
                    for c in range(KC):
                        last = mm(bank[2 * j + half][:, 0:GN], sup[:, c, half * HALF + j * P:half * HALF + (j + 1) * P],
                                  x2T[:, c, g * GN:(g + 1) * GN], start=(c == 0), stop=(c == KC - 1))
                last.then_inc(s_sups, 1)

            def shared_down(g):
                pe.wait_ge(s_shid, FC * (g + 1))
                for q in range(2):
                    since(pe, s_hsh, 2 * g + q - 1)
                    for t in range(NT):
                        for j in range(FC):
                            last = mm(bank[6 + q][0:TT, t * D:(t + 1) * D],
                                      shid[g // 3 * 2 + g % 3 % 2][:, j, q * T + t * TT:q * T + (t + 1) * TT], sdn[:, j, :],
                                      start=(j == 0), stop=(j == FC - 1))
                    last.then_inc(s_sdps, 1)

            pe.wait_ge(s_wf, 16 * 3)
            pe.wait_ge(s_x2Tall, 16 * B)
            shared_up(0, 0)
            shared_up(0, 1)
            pe.wait_ge(s_m12, 1)
            pe.wait_ge(s_rc, 32)
            m12 = rb[:, 6, :]
            mm(bank[7][0:TT, 0:BT * NE], tri[:, :], m12, start=True, stop=True)
            mm(bank[7][0:TT, 256:256 + BT * NE], ones[0:TT, 0:TT], m12, start=True, stop=True).then_inc(s_rps, 1)
            shared_up(0, 2)
            for g in range(1, GR - 1):
                for j in range(FC):
                    shared_up(g, j)
                if g == 1:
                    pe.wait_ge(s_slot, 1)
                shared_down(g - 1)
            shared_down(GR - 2)

            pe.wait_ge(s_texp, 1)
            pe.wait_ge(s_shid, FC * (GR - 1))
            pe.wait_ge(s_hsh, 2 * (GR - 1))

            def turn_x(j, p):
                pe.wait_ge(s_xg[p], 8 * j + 16 - 8 * p)
                since(pe, s_xgTp, j)
                for c in range(KC):
                    last = nc.tensor.transpose(bank[0][:, c * P:(c + 1) * P], xg[p][:, c * P:(c + 1) * P], ident[:, :])
                last.then_inc(s_xgTps, 1)

            def expert(j):
                return pe.value_load(texpi[0:1, bass.ds(j, 1)], min_val=0, max_val=NE - 1)

            def up(j, p, e):
                pe.wait_ge(s_xgTp, j + 1)
                since(pe, s_rh, j - 1)
                for half in range(2):
                    for c in range(KC):
                        for i, (kw, kx) in enumerate(PRODUCTS):
                            last = mm(bank[1 + 2 * p + half][:, 0:HALF], xgTp[p][:, kx, c, :],
                                      eupp[:, c, bass.ds(e * (2 * HALF) + half * HALF, HALF), kw],
                                      start=(c == 0 and i == 0), stop=(c == KC - 1 and i == 2))
                last.then_inc(s_rups, 1)

            def turn_hidden(j, p):
                pe.wait_ge(s_rh, j + 1)
                since(pe, s_rhTp, j)
                for k in range(FC):
                    last = nc.tensor.transpose(bank[5][:, k * P:(k + 1) * P], rh[p][:, k * P:(k + 1) * P], ident[:, :])
                last.then_inc(s_rhTps, 1)

            def down(j, p, e):
                pe.wait_ge(s_rhTp, j + 1)
                since(pe, s_ry, j)
                for k in range(FC):
                    for i, (kw, kx) in enumerate(PRODUCTS):
                        last = mm(bank[6][:, 0:D], rhTp[p][:, kx, k, :], ednp[:, k, bass.ds(e * D, D), kw],
                                  start=(k == 0 and i == 0), stop=(k == FC - 1 and i == 2))
                last.then_inc(s_rdps, 1)

            def tile_step(j, p, e, before=None, more=True):
                turn_x(j + 1, 1 - p)
                up(j, p, e)
                if before is None:
                    before = expert(j - 2)
                after = expert(j + 1) if more else None
                turn_hidden(j - 1, 1 - p)
                down(j - 2, p, before)
                return after

            turn_x(0, 0)
            turn_x(1, 1)
            pe.wait_ge(s_ehigh, len(PIECES))
            up(0, 0, expert(0))
            turn_x(2, 0)
            up(1, 1, expert(1))
            turn_hidden(0, 0)
            tile_step(2, 0, expert(2), more=False)
            with pe.Fori(0, RT // 4 - 1) as i:
                e = [None, None, expert(4 * i + 3)]
                for n in range(4):
                    e.append(tile_step(4 * i + 3 + n, (3 + n) % 2, e[n + 2], e[n], more=n < 3))
            up(RT - 1, 1, expert(RT - 1))
            turn_hidden(RT - 2, 0)
            down(RT - 3, 1, expert(RT - 3))
            turn_hidden(RT - 1, 1)
            down(RT - 2, 0, expert(RT - 2))
            down(RT - 1, 1, expert(RT - 1))
            pe.wait_ge(s_rh, RT)
            pe.wait_ge(s_rhTp, RT)
            for j in range(FC):
                shared_up(GR - 1, j)
            pe.wait_ge(s_ry, RT)
            shared_down(GR - 1)

            pe.wait_ge(s_w1in, 64)
            pe.wait_ge(s_l1c, 16 * 7)

            def turn1(b):
                pe.wait_ge(s_xn1, b + 1)
                since(pe, s_lg4, b - 2)
                for t in range(NT):
                    for c in range(KC):
                        last = nc.tensor.transpose(bank[0][:, c * T + t * TT:c * T + (t + 1) * TT],
                                                   xn[:, t, c * P:(c + 1) * P], ident[0:TT, 0:TT])
                last.then_inc(s_xT1ps, 1)

            def keys1(b):
                pe.wait_ge(s_xTp1, b + 1)
                for o in range(KC):
                    for c in range(KC):
                        for i, (kw, kx) in enumerate(PRODUCTS):
                            last = mm(bank[0][:, o * T:(o + 1) * T], wkp[:, c, o * P:(o + 1) * P, kw], xnTp[:, kx, c, :],
                                      start=(c == 0 and i == 0), stop=(c == KC - 1 and i == 2))
                last.then_inc(s_k1ps, 1)

            def queries1(b):
                since(pe, s_rbs, b - 1)
                for o in range(KC):
                    for c in range(KC):
                        for i, (kw, kx) in enumerate(PRODUCTS):
                            last = mm(bank[2][:, o * T:(o + 1) * T], wqp[:, c, o * P:(o + 1) * P, kw], xnTp[:, kx, c, :],
                                      start=(c == 0 and i == 0), stop=(c == KC - 1 and i == 2))
                last.then_inc(s_q1ps, 1)

            def values1(b, t):
                if t == 0:
                    since(pe, s_h3, b - 1)
                for c in range(KC):
                    for i, (kw, kx) in enumerate(PRODUCTS):
                        last = mm(bank[3][0:TT, t * D:(t + 1) * D], xnTp[:, kx, c, t * TT:(t + 1) * TT], wvp[:, c, :, kw],
                                  start=(c == 0 and i == 0), stop=(c == KC - 1 and i == 2))
                if t == 1:
                    last.then_inc(s_v1ps, 1)

            def logits1(b, p, u):
                half, t, n, w = UNITS1[u]
                if u == 0:
                    pe.wait_ge(s_q1, 2 * b + 2)
                if u % (NU1 // 2) == 0:
                    pe.wait_ge(s_kb, 2 * b + half + 1)
                since(pe, s_min, NU1 * b + u - 1)
                mm(bank[4 + u % 2][0:TT, 0:w * T], q1[p][:, half, t * TT:(t + 1) * TT], kb[p][:, half, n:n + w, :],
                   start=True, stop=True).then_inc(s_sps, 1)

            def turn_probs(b, u):
                half, t, n, w = UNITS1[u]
                pe.wait_ge(s_p, NU1 * b + u + 1)
                since(pe, s_pt[u % 2], NU1 // 2 * b + u // 2)
                for kt in range(NT):
                    for i in range(w):
                        last = nc.tensor.transpose(bank[6 + u % 2][0:TT, (kt * w + i) * TT:(kt * w + i + 1) * TT],
                                                   ring[u % 4][0:TT, i, kt * TT:(kt + 1) * TT], ident[0:TT, 0:TT])
                last.then_inc(s_ptps, 1)

            def turn4(b):
                pe.wait_ge(s_x4, b + 1)
                since(pe, s_lg4, b)
                for t in range(NT):
                    for c in range(KC):
                        last = nc.tensor.transpose(bank[0][:, c * T + t * TT:c * T + (t + 1) * TT],
                                                   x2s[:, t, c * P:(c + 1) * P], ident[0:TT, 0:TT])
                last.then_inc(s_x4Tps, 1)

            def router(b):
                pe.wait_ge(s_x4T, b + 1)
                for t in range(NT):
                    for c in range(KC):
                        last = mm(bank[0][0:TT, t * NE:(t + 1) * NE], x2Ts[:, c, t * TT:(t + 1) * TT], rw[:, c, :],
                                  start=(c == 0), stop=(c == KC - 1))
                last.then_inc(s_lg4ps, 1)

            def mix1(b, p, half):
                for par in range(2):
                    pe.wait_ge(s_pt[par], NU1 // 2 * b + (half + 1) * NU1 // 4)
                pe.wait_ge(s_v1, b + 1)
                since(pe, s_y1, b)
                for t in range(NT):
                    for par in range(2):
                        for i in range(4):
                            last = mm(bank[1][32 * i:32 * i + 32, half * T:(half + 1) * T],
                                      vz[p][par][:, t, 4 * half + i, :, :], pT[half][:, t, 2 * i + par, :],
                                      start=(t == 0 and par == 0), stop=(t == 1 and par == 1),
                                      skip_group_check=True, tile_position=(0, 32 * i))
                last.then_inc(s_pv1, 1)

            def sums1(b):
                pe.wait_ge(s_rspread, b + 1)
                for half in range(KC):
                    for t in range(NT):
                        last = mm(bank[2][:, half * T + t * TT:half * T + (t + 1) * TT],
                                  rspread[0:TT, t, half * P:(half + 1) * P],
                                  ident[0:TT, 0:TT], start=True, stop=True)
                last.then_inc(s_rbps, 1)

            def project_out1(b, t, final=False):
                if t == 0:
                    pe.wait_ge(s_y1, b + 1)
                    pe.wait_ge(s_v1, b + 1 if final else b + 2)
                for c in range(KC):
                    last = mm(bank[3][0:TT, t * D:(t + 1) * D], yT[:, c, t * TT:(t + 1) * TT], wo[:, c, :],
                              start=(c == 0), stop=(c == KC - 1))
                if t == 1:
                    last.then_inc(s_o1ps, 1)

            def step1(b, p, first=False, second=False, final=False):
                for u in range(NU1):
                    logits1(b, p, u)
                    if u >= 2:
                        turn_probs(b, u - 2)
                    elif not first:
                        turn_probs(b - 1, NU1 - 2 + u)
                    if not (first or second):
                        if u == 0:
                            turn4(b - 2)
                        elif u == 2:
                            router(b - 2)
                    if not first:
                        if u == 3:
                            mix1(b - 1, 1 - p, 1)
                        elif u == 5:
                            sums1(b - 1)
                        elif u == 7:
                            project_out1(b - 1, 0)
                        elif u == 8:
                            project_out1(b - 1, 1)
                    if not final:
                        if u == 4:
                            turn1(b + 1)
                        elif u == 6:
                            keys1(b + 1)
                        elif u == 9:
                            queries1(b + 1)
                        elif u == 11:
                            values1(b + 1, 0)
                            values1(b + 1, 1)
                    if u == 10:
                        if first:
                            pe.wait_ge(s_pz, 2)
                        mix1(b, p, 0)

            turn1(0)
            pe.wait_ge(s_wsplit, 1)
            keys1(0)
            queries1(0)
            values1(0, 0)
            values1(0, 1)
            pe.wait_ge(s_hsh, 2 * GR)
            step1(0, 0, first=True)
            step1(1, 1, second=True)
            step1(2, 0)
            with pe.Fori(1, B // 2 - 1) as i:
                step1(2 * i + 1, 1)
                step1(2 * i + 2, 0)
            step1(B - 1, 1, final=True)
            def ff_up(n):
                g, j = divmod(n, FFC)
                before = [m for m in range(n) if UPBANK[m] == UPBANK[n]]
                if before:
                    pe.wait_ge(s_gelu, before[-1] + 1)
                if j == 0:
                    pe.wait_ge(s_xpart, g + 1)
                for c in range(KC):
                    for i, (kw, kx) in enumerate(PRODUCTS):
                        last = mm(bank[UPBANK[n]][:, 0:GN], w1p[:, c, j * P:(j + 1) * P, kw], xpart[g % 2][:, kx, c, :],
                                  start=(c == 0 and i == 0), stop=(c == KC - 1 and i == 2))
                last.then_inc(s_fups, 1)

            turn_probs(B - 1, NU1 - 2)
            pe.wait_ge(s_min, NU1 * B - 1)
            ff_up(0)
            turn_probs(B - 1, NU1 - 1)
            turn4(B - 2)
            mix1(B - 1, 1, 1)
            sums1(B - 1)
            router(B - 2)
            pe.wait_ge(s_min, NU1 * B)
            ff_up(1)
            project_out1(B - 1, 0, final=True)
            project_out1(B - 1, 1)
            pe.wait_ge(s_pt[0], NU1 // 2 * B)
            ff_up(2)
            pe.wait_ge(s_pt[1], NU1 // 2 * B)
            ff_up(3)
            ff_up(4)
            ff_up(5)
            turn4(B - 1)
            router(B - 1)

            def ff_down(g, o):
                if o == 0:
                    pe.wait_ge(s_hid, FFC * (g + 1))
                since(pe, s_ft, KC * (g - 1) + o + 1)
                for j in range(FFC):
                    for i, (kw, kx) in enumerate(PRODUCTS):
                        last = mm(bank[4 + o][:, 0:GN], w2p[:, j, o * P:(o + 1) * P, kw], hidp[g % 2][:, kx, j, :],
                                  start=(j == 0 and i == 0), stop=(j == FFC - 1 and i == 2))
                last.then_inc(s_fdps, 1)

            def ff_turn(g):
                pe.wait_ge(s_ft, KC * (g + 1))
                for q in range(2):
                    since(pe, s_h4, 2 * (g - 1) + q + 1)
                    for t in range(NT):
                        for o in range(KC):
                            last = nc.tensor.transpose(bank[6 + q][0:TT, t * D + o * P:t * D + (o + 1) * P],
                                                       ffT[g % 2][:, o, q * T + t * TT:q * T + (t + 1) * TT], ident[:, :])
                    last.then_inc(s_fyps, 1)

            pe.wait_ge(s_lg4, B)
            for n in range(6, 2 * FFC):
                ff_up(n)
            ff_down(0, 0)
            ff_down(0, 1)
            for g in range(1, GR):
                for n in range(FFC * (g + 1), min(FFC * (g + 2), FFC * GR)):
                    ff_up(n)
                ff_down(g, 0)
                ff_turn(g - 1)
                ff_down(g, 1)
            ff_turn(GR - 1)

        @block.scalar
        def _(act):
            acte = nc.scalar.activation
            for i in range(3):
                n = IMG * min(3, B - 3 * i)
                act.wait_ge(s_tokps, i + 1)
                nc.scalar.copy(tok[0:n, i, :], bank[i][0:n, 0:D]).then_inc(s_toksb, 1)
            act.wait_ge(s_w0, 16 * 10)
            nc.scalar.preload_act_table_set("sigmoid_and_others")
            acte(base[:, :], dec[:, :], ACT.Sigmoid).then_inc(s_base, 1)
            act.wait_ge(gch, 7)
            nc.scalar.preload_act_table_set("natural_log_exp_and_others")

            def norm_scale(b):
                act.wait_ge(s_mv, b + 1)
                acte(lnv[:, :], mv[:, :, 1], ACT.Ln, bias=EPSC[0:TT, 0:1]).then_inc(ach, 1)
                act.wait_ge(ach, b + 1)
                acte(rstd[:, :], lnv[:, :], ACT.Exp, scale=-0.5).then_inc(s_rstd, 1)

            def turned(b):
                act.wait_ge(s_xTps, b + 1)
                since(act, s_v, b)
                nc.scalar.copy(xnT[:, :, :].rearrange("p c t -> p (c t)"), bank[0][:, 0:KC * T]).then_inc(s_xT, 1)
                nc.scalar.preload_act_table_set("sigmoid_and_others")

            def gate_in(b):
                act.wait_ge(s_z1, b + 1)
                since(act, s_z2, b)
                acte(th[:, :], bank[0][0:64, 0:T], ACT.Tanh, bias=cb1[:, 0:1]).then_inc(s_th, 1)

            def gate_out(b):
                act.wait_ge(s_z2, b + 1)
                since(act, s_lam, b)
                for o in range(KC):
                    acte(lc[:, o, :], bank[0][:, o * T:(o + 1) * T], ACT.Sigmoid, bias=cb2[:, o:o + 1]).then_inc(s_lc, 1)
                nc.scalar.preload_act_table_set("natural_log_exp_and_others")

            def logs(b):
                act.wait_ge(s_lam, b + 1)
                since(act, s_G, b)
                acte(lnlam[:, :, :], lam[:, :, :], ACT.Ln).then_inc(s_lnlam, 1)

            def keys_in(b):
                act.wait_ge(s_k, b + 1)
                since(act, s_kr, b)
                nc.scalar.copy(ksb[:, :, :].rearrange("p c t -> p (c t)"), bank[2][:, 0:KC * T]).then_inc(s_ksb, 1)

            def query_decay(b):
                act.wait_ge(s_dq, b + 1)
                since(act, s_qe, b)
                acte(eq[:, :], dq[:, :], ACT.Exp).then_inc(s_eq, 1)

            def key_decay(b):
                act.wait_ge(s_dk, b + 1)
                since(act, s_kr, b)
                acte(ek[:, :, :], dk[:, :, :], ACT.Exp).then_inc(s_ek, 1)

            def values(b, p):
                act.wait_ge(s_v, b + 1)
                since(act, s_pv, 2 * b - 2)
                for par in range(2):
                    src = bank[3][0:TT, :].rearrange("p (t i j d) -> p (t i) j d", t=NT, i=HEADS // 2, j=2)
                    dst = vz[p][par][0:TT, :, :, :, :].rearrange("p t i j d -> p (t i) j d")
                    ins = nc.scalar.copy(dst[:, :, par, :], src[:, :, par, :])
                ins.then_inc(s_vsb, 1)

            def plain(b, half, n):
                u = PLAIN[n]
                r, t = UNITS[u]
                act.wait_ge(s_aps, 12 * b + 6 * half + u + 1)
                if n == 0:
                    since(act, s_pv, 2 * b + half - 1)
                nc.scalar.copy(asb[half][0:TT, t, :, CH * r:CH * (r + 1)],
                               bank[4 + u % 2][0:TT, 0:HH * CH].rearrange("p (h c) -> p h c", c=CH)).then_inc(s_aact, 1)

            def mixed(b):
                act.wait_ge(s_pv, 2 * b + 2)
                since(act, s_ops, b)
                nc.scalar.copy(yT[:, :, :].rearrange("p c t -> p (c t)"), bank[6][:, 0:KC * T]).then_inc(s_ysb, 1)

            def norm2(b):
                act.wait_ge(s_mv2, b + 1)
                acte(lnv2[:, :], mv2[:, :, 1], ACT.Ln, bias=EPSC[0:TT, 0:1]).then_inc(ach2, 1)
                act.wait_ge(ach2, b + 1)
                acte(rstd2[:, :], lnv2[:, :], ACT.Exp, scale=-0.5).then_inc(s_rstd2, 1)

            def turned2(b):
                act.wait_ge(s_x2Tps, b + 1)
                since(act, s_x2Tall, 16 * b)
                since(act, s_lgps, b)
                nc.scalar.copy(x2Ts[:, :, :].rearrange("p c t -> p (c t)"), bank[0][:, 0:KC * T]).then_inc(s_x2T, 1)

            def step(b, p, first=False, last=False, final=False):
                if not final:
                    turned(b + 1)
                    gate_in(b + 1)
                if not first:
                    mixed(b - 1)
                if not final:
                    gate_out(b + 1)
                if first:
                    logs(b + 1)
                plain(b, 0, 0)
                if not (first or final):
                    logs(b + 1)
                if not final:
                    keys_in(b + 1)
                    query_decay(b + 1)
                if not (last or final):
                    norm_scale(b + 2)
                plain(b, 0, 1)
                if not final:
                    key_decay(b + 1)
                if not first:
                    norm2(b - 1)
                if not final:
                    values(b + 1, 1 - p)
                plain(b, 1, 0)
                if not first:
                    turned2(b - 1)
                plain(b, 1, 1)

            norm_scale(0)
            norm_scale(1)
            turned(0)
            gate_in(0)
            keys_in(0)
            gate_out(0)
            logs(0)
            query_decay(0)
            key_decay(0)
            values(0, 0)
            step(0, 0, first=True)
            step(1, 1)
            with act.Fori(1, B // 2 - 1) as i:
                step(2 * i, 0)
                step(2 * i + 1, 1)
            step(B - 2, 0, last=True)
            step(B - 1, 1, final=True)
            mixed(B - 1)
            norm2(B - 1)
            turned2(B - 1)

            act.wait_ge(s_al, 1)
            acte(aabs[:, 1, :], aabs[:, 0, :], ACT.Exp, scale=-1.0).then_inc(ach, 1)
            act.wait_ge(ach, B + 1)
            acte(aabs[:, 0, :], aabs[:, 1, :], ACT.Ln, bias=1.0).then_inc(s_al, 1)

            nc.scalar.preload_act_table_set("silu_and_others")
            act.wait_ge(s_gap, 1)
            acte(rs[:, 5, :], rs[:, 4, :], ACT.Tanh, scale=0.5).then_inc(s_gw, 1)

            def shared_gate(g):
                for j in range(FC):
                    act.wait_ge(s_sups, FC * g + j + 1)
                    since(act, s_shid, FC * (g - 1) + j + 1)
                    acte(sgate[g // 3][:, j, :], bank[2 * j][:, 0:GN], ACT.Silu).then_inc(s_sg, 1)

            def expert_round(n):
                if n >= DOWN:
                    act.wait_ge(s_eup[(n - DOWN) // 4], 16)
                else:
                    act.wait_ge(s_wf, 16 * 3)
                since(act, s_ehigh, n - 1)
                nc.scalar.copy(etmp[n % 2], PIECES[n][0]).then_inc(s_eround, 1)

            def expert_high(n):
                act.wait_ge(s_elow, n + 1)
                nc.scalar.copy(PIECES[n][1][:, :, 0], etmp[n % 2]).then_inc(s_ehigh, 1)

            for g in range(GR - 1):
                shared_gate(g)
                for n in range(4 * g, 4 * g + 4):
                    expert_round(n)
                    if n > 0:
                        expert_high(n - 1)
            expert_high(len(PIECES) - 1)

            def x_high(j, p):
                act.wait_ge(s_xgTps, j + 1)
                since(act, s_rups, j - 1)
                nc.scalar.copy(xgTp[p][:, 0, :, :].rearrange("p c n -> p (c n)"), bank[0][:, 0:D]).then_inc(s_xgT, 1)

            def silu(j, p):
                act.wait_ge(s_rups, j + 1)
                since(act, s_rh, j)
                acte(rg[:, :], bank[1 + 2 * p][:, 0:HALF], ACT.Silu).then_inc(s_rg, 1)

            def hidden_turned(j, p):
                act.wait_ge(s_rhTps, j + 1)
                since(act, s_rdps, j - 1)
                nc.scalar.copy(rhTp[p][:, 0, :, :].rearrange("p k n -> p (k n)"), bank[5][:, 0:FC * P]).then_inc(s_rhT, 1)

            x_high(0, 0)
            x_high(1, 1)
            silu(0, 0)
            x_high(2, 0)
            silu(1, 1)
            hidden_turned(0, 0)
            x_high(3, 1)
            silu(2, 0)
            hidden_turned(1, 1)
            with act.Fori(0, RT // 4 - 1) as i:
                for n in range(4):
                    x_high(4 * i + 4 + n, n % 2)
                    silu(4 * i + 3 + n, (3 + n) % 2)
                    hidden_turned(4 * i + 2 + n, n % 2)
            silu(RT - 1, 1)
            hidden_turned(RT - 2, 0)
            hidden_turned(RT - 1, 1)
            shared_gate(GR - 1)

            nc.scalar.preload_act_table_set("natural_log_exp_and_others")

            def norm1(b):
                act.wait_ge(s_mv1, b + 1)
                acte(lnv[:, :], mv[:, :, 1], ACT.Ln, bias=EPSC[0:TT, 0:1]).then_inc(ach, 1)
                act.wait_ge(ach, B + b + 2)
                acte(rstd[:, :], lnv[:, :], ACT.Exp, scale=-0.5).then_inc(s_rstd1, 1)

            def norm4(b):
                act.wait_ge(s_mv4, b + 1)
                acte(lnv2[:, :], mv2[:, :, 1], ACT.Ln, bias=EPSC[0:TT, 0:1]).then_inc(ach2, 1)
                act.wait_ge(ach2, B + b + 1)
                acte(rstd2[:, :], lnv2[:, :], ACT.Exp, scale=-0.5).then_inc(s_rstd4, 1)

            def turned1(b):
                act.wait_ge(s_xT1ps, b + 1)
                since(act, s_v1ps, b)
                nc.scalar.copy(xnTp[:, 0, :, :].rearrange("p c t -> p (c t)"), bank[0][:, 0:KC * T]).then_inc(s_xT1, 1)

            def keys1(b):
                act.wait_ge(s_k1ps, b + 1)
                since(act, s_kb, 2 * b)
                for o in range(KC):
                    ins = acte(ksb1[:, o, :], bank[0][:, o * T:(o + 1) * T], ACT.Identity, bias=qkb[:, 1, o:o + 1])
                ins.then_inc(s_k1, 1)

            def queries1(b, p):
                act.wait_ge(s_q1ps, b + 1)
                since(act, s_sps, NU1 * (b - 1))
                for o in range(KC):
                    acte(q1[p][:, o, :], bank[2][:, o * T:(o + 1) * T], ACT.Identity, bias=nqb[:, o:o + 1],
                         scale=-1.0 / SCALE).then_inc(s_q1, 1)

            def probs(b, p, u):
                half, t, n, w = UNITS1[u]
                if u == 0:
                    since(act, s_rinv, b - 1)
                act.wait_ge(s_min, NU1 * b + u + 1)
                for i in range(w):
                    col = t * HEADS + half * HH + n + i
                    ins = acte(ring[u % 4][0:TT, i, :], ring[u % 4][0:TT, i, :], ACT.Exp, scale=-1.0,
                               bias=mn[:, col:col + 1], accum_out=rsum[p][:, col:col + 1])
                ins.then_inc(s_p, 1)

            def probs_turned(b, u):
                if u % 2 == 0:
                    return
                half, t, n, w = UNITS1[u]
                act.wait_ge(s_ptps, NU1 * b + u + 1)
                if u in (1, 7):
                    since(act, s_pv1, 2 * b + half - 1)
                nc.scalar.copy(pT[half][0:TT, :, n:n + w, t * TT:(t + 1) * TT],
                               bank[6 + u % 2][0:TT, 0:NT * w * TT].rearrange("p (k h q) -> p k h q", k=NT, h=w)).then_inc(s_pt[1], 1)

            def sums1(b):
                act.wait_ge(s_rbps, b + 1)
                since(act, s_y1, b)
                nc.scalar.copy(rbs[:, :, :].rearrange("p c t -> p (c t)"), bank[2][:, 0:KC * T]).then_inc(s_rbs, 1)

            def step1(b, p, first=False, second=False, final=False):
                for u in range(NU1):
                    if u >= 3:
                        probs_turned(b, u - 3)
                    elif not first:
                        probs_turned(b - 1, NU1 - 3 + u)
                    probs(b, p, u)
                    if not first:
                        if u == 5:
                            sums1(b - 1)
                        elif u == 10:
                            norm4(b - 1)
                    if u == 0 and not (first or second):
                        turned4(b - 2)
                    if not final:
                        if u == 2:
                            norm1(b + 1)
                        elif u == 4:
                            turned1(b + 1)
                        elif u == 6:
                            keys1(b + 1)
                        elif u == 9:
                            queries1(b + 1, 1 - p)

            def turned4(b):
                act.wait_ge(s_x4Tps, b + 1)
                since(act, s_x4Tall, 16 * b)
                since(act, s_lg4ps, b)
                nc.scalar.copy(x2Ts[:, :, :].rearrange("p c t -> p (c t)"), bank[0][:, 0:KC * T]).then_inc(s_x4T, 1)

            act.wait_ge(s_nqb, 1)
            act.wait_ge(s_l1c, 16 * 7)
            norm1(0)
            turned1(0)
            keys1(0)
            queries1(0, 0)
            step1(0, 0, first=True)
            step1(1, 1, second=True)
            step1(2, 0)
            with act.Fori(1, B // 2 - 1) as i:
                step1(2 * i + 1, 1)
                step1(2 * i + 2, 0)
            step1(B - 1, 1, final=True)
            probs_turned(B - 1, NU1 - 3)
            probs_turned(B - 1, NU1 - 1)
            turned4(B - 2)
            sums1(B - 1)
            norm4(B - 1)
            nc.scalar.preload_act_table_set("gelu_apprx_tanh_and_others")
            turned4(B - 1)
            for g in range(GR):
                if g == GR // 2:
                    act.wait_ge(s_rx, 1)
                    nc.scalar.preload_act_table_set("natural_log_exp_and_others")
                    acte(rb[:, 1, :], rb[:, 0, :], ACT.Exp).then_inc(s_rexp, 1)
                    nc.scalar.preload_act_table_set("gelu_apprx_tanh_and_others")
                for j in range(FFC):
                    n = FFC * g + j
                    act.wait_ge(s_fups, n + 1)
                    if j == 0:
                        since(act, s_fdps, KC * (g - 1))
                    since(act, s_hid, n - 1)
                    ins = acte(hid32[n % 2], bank[UPBANK[n]][:, 0:GN], ACT.Gelu_apprx_tanh, bias=b1c[:, j:j + 1])
                    if j % 2:
                        ins.then_inc(s_gelu, 1)
                    else:
                        acte(hidp[g % 2][:, 0, j, :], bank[UPBANK[n]][:, 0:GN], ACT.Gelu_apprx_tanh, bias=b1c[:, j:j + 1]).then_inc(s_gelu, 1)

        @block.vector
        def _(dve):
            v = nc.vector

            def settle():
                dve.sem_inc(s_settled, 1)

            v.memset(ones[:, :], 1.0).then_inc(vch, 1)
            dve.wait_ge(s_base, 1)
            v.tensor_scalar(base02[:, :], base[:, :], 0.2, None, ALU.mult).then_inc(vch, 1)
            dve.wait_ge(s_txt, 32)
            dve.wait_ge(s_tokh0, 16 * 3)
            dve.wait_ge(s_const, 48)
            dve.wait_ge(vch, 2)

            def stats0(b):
                c = Chain(dve, nch, 4 * b)
                ht = htile(b)
                for t in range(NT):
                    c.add(v.bn_stats(st[:, 6 * t:6 * t + 6], ht[:, t, :]))
                c.wait()
                since(dve, s_rstd, b)
                settle()
                c.add(v.bn_aggr(mv[:, 0, :], st[:, 0:6]))
                v.bn_aggr(mv[:, 1, :], st[:, 6:12]).then_inc(s_mv, 1)
                c.step(3)

            def normed0(b):
                c = Chain(dve, nch, 4 * b + 3)
                ht = htile(b)
                dve.wait_ge(s_rstd, b + 1)
                since(dve, s_xTps, b)
                c.add(v.tensor_scalar(xn[:, 0, :], ht[:, 0, :], mv[:, 0, 0:1], rstd[:, 0:1], ALU.subtract, ALU.mult))
                v.tensor_scalar(xn[:, 1, :], ht[:, 1, :], mv[:, 1, 0:1], rstd[:, 1:2], ALU.subtract, ALU.mult).then_inc(s_xn, 1)
                c.step(1)

            def decay(b):
                c = Chain(dve, vch, 2 + 3 * b)
                dve.wait_ge(s_lc, 2 * b + 2)
                since(dve, s_lnlam, b)
                for o in range(KC):
                    c.add(v.tensor_scalar(lam[:, o, :], lc[:, o, :], base02[:, o:o + 1], base[:, o:o + 1], ALU.mult, ALU.add))
                c.wait()
                v.tensor_scalar(lam[:, :, :], lam[:, :, :], LAM_MAX, LAM_MIN, ALU.min, ALU.max).then_inc(s_lam, 1)
                c.step(2)

            def summed(b):
                c = Chain(dve, vch, 2 + 3 * b + 2)
                dve.wait_ge(s_lnlam, b + 1)
                since(dve, s_dk, b)
                c.add(v.tensor_tensor_scan(G[:, 0, :], ones[:, :], lnlam[:, 0, :], 0.0, ALU.mult, ALU.add))
                v.tensor_tensor_scan(G[:, 1, :], ones[:, :], lnlam[:, 1, :], 0.0, ALU.mult, ALU.add).then_inc(s_G, 1)
                c.wait()
                dve.wait_ge(s_G, b + 1)
                since(dve, s_eq, b)
                Gc = G[:, :, :].rearrange("p c (n t) -> p (c n) t", t=CH)
                v.tensor_tensor(dq[:, :].rearrange("p (n t) -> p n t", t=CH), Gc,
                                Gc[:, :, MIDC:MIDC + 1].to_broadcast([P, KC * NCH, CH]), ALU.subtract).then_inc(s_dq, 1)
                c.step(1)

            def queries(b):
                dve.wait_ge(s_eq, b + 1)
                dve.wait_ge(s_q, b + 1)
                since(dve, s_qb1, b)
                v.tensor_tensor(qe[:, :, :].rearrange("p c t -> p (c t)"), bank[1][:, 0:KC * T], eq[:, :], ALU.mult).then_inc(s_qe, 1)

            def queries_masked(b, p):
                dve.wait_ge(s_qe, b + 1)
                since(dve, s_aps, 12 * (b - 1))
                v.tensor_tensor(qb[p][:, 0, :, :], qe[:, 0:1, :].to_broadcast([P, HH, T]),
                                hmask[:, :].unsqueeze(2).to_broadcast([P, HH, T]), ALU.mult).then_inc(s_qb0, 1)

            def masked(b, half, n):
                u = MASKED[n]
                r, t = UNITS[u]
                m = min(TT, CH * (r + 1) - TT * t)
                dve.wait_ge(s_aps, 12 * b + 6 * half + u + 1)
                if n == 0:
                    since(dve, s_pv, 2 * b + half - 1)
                settle()
                v.copy_predicated(asb[half][0:m, t, :, CH * r:CH * (r + 1)],
                                  cmask[0:m, r % 2, :].unsqueeze(1).to_broadcast([m, HH, CH]),
                                  bank[4 + u % 2][0:m, 0:HH * CH].rearrange("p (h c) -> p h c", c=CH)).then_inc(s_adve, 1)

            def residual(b):
                dve.wait_ge(s_ops, b + 1)
                hb = h[:, bass.ds(b * (NT * D), NT * D)]
                v.tensor_tensor(hb, hb, bank[7][0:TT, :], ALU.add).then_inc(s_h1, 1)

            def stats2(b):
                c = Chain(dve, vch2, 4 * b)
                ht = htile(b)
                dve.wait_ge(s_h1, b + 1)
                settle()
                for t in range(NT):
                    c.add(v.bn_stats(st2[:, 6 * t:6 * t + 6], ht[:, t, :]))
                c.wait()
                settle()
                c.add(v.bn_aggr(mv2[:, 0, :], st2[:, 0:6]))
                v.bn_aggr(mv2[:, 1, :], st2[:, 6:12]).then_inc(s_mv2, 1)
                c.step(3)

            def normed2(b):
                c = Chain(dve, vch2, 4 * b + 3)
                ht = htile(b)
                dve.wait_ge(s_rstd2, b + 1)
                since(dve, s_x2Tps, b)
                since(dve, s_x2all, 16 * b)
                c.add(v.tensor_scalar(x2s[:, 0, :], ht[:, 0, :], mv2[:, 0, 0:1], rstd2[:, 0:1], ALU.subtract, ALU.mult))
                v.tensor_scalar(x2s[:, 1, :], ht[:, 1, :], mv2[:, 1, 0:1], rstd2[:, 1:2], ALU.subtract, ALU.mult).then_inc(s_x2, 1)
                c.step(1)

            def logits(b):
                dve.wait_ge(s_lgps, b + 1)
                v.tensor_scalar(lg[:, bass.ds(b * (NT * NE), NT * NE)], bank[7][0:TT, 0:NT * NE], 1.0, None, ALU.mult).then_inc(s_lg, 1)

            def step(b, p, first=False, last=False, final=False):
                if first:
                    decay(b + 1)
                masked(b, 0, 0)
                masked(b, 0, 1)
                if not (last or final):
                    stats0(b + 2)
                if not (first or final):
                    decay(b + 1)
                masked(b, 0, 2)
                if not final:
                    summed(b + 1)
                if not first:
                    residual(b - 1)
                masked(b, 0, 3)
                if not final:
                    queries(b + 1)
                if not first:
                    stats2(b - 1)
                masked(b, 1, 0)
                masked(b, 1, 1)
                if not final:
                    queries_masked(b + 1, 1 - p)
                if not first:
                    normed2(b - 1)
                masked(b, 1, 2)
                if not (last or final):
                    normed0(b + 2)
                masked(b, 1, 3)
                if not first:
                    logits(b - 1)

            stats0(0)
            normed0(0)
            stats0(1)
            normed0(1)
            decay(0)
            summed(0)
            queries(0)
            queries_masked(0, 0)
            step(0, 0, first=True)
            dve.wait_ge(s_tokh, 16 * (B - 3))
            step(1, 1)
            with dve.Fori(1, B // 2 - 1) as i:
                step(2 * i, 0)
                step(2 * i + 1, 1)
            step(B - 2, 0, last=True)
            step(B - 1, 1, final=True)
            residual(B - 1)
            stats2(B - 1)
            normed2(B - 1)
            logits(B - 1)

            dve.wait_ge(s_l1c, 16 * 7)
            v.tensor_scalar(nqb[:, :], qkb[:, 0, :], -1.0 / SCALE, None, ALU.mult).then_inc(s_nqb, 1)
            v.scalar_tensor_tensor(aabs[:, 0, :], arow[:, :], -1.0, arow[:, :], ALU.mult, ALU.max).then_inc(s_al, 1)
            dve.wait_ge(s_al, 2)
            v.scalar_tensor_tensor(alpha[:, :], arow[:, :], 0.0, aabs[:, 0, :], ALU.max, ALU.add).then_inc(s_alpha, 1)

            dve.wait_ge(s_lg, B)
            dve.wait_ge(s_rc, 32)
            c = Chain(dve, rch)
            AX = mybir.AxisListType.X

            def grid(x):
                return x.rearrange("p (i e) -> p i e", e=NE)

            def over(x):
                return x.unsqueeze(2).to_broadcast([TT, BT, NE])

            logit, same, rank, first, rest, second = lg[:, :], rb[:, 0, :], rb[:, 1, :], rb[:, 2, :], rb[:, 3, :], rb[:, 4, :]
            best, bestrank, next_, nextrank = rs[:, 0, :], rs[:, 1, :], rs[:, 2, :], rs[:, 3, :]

            def choose(x, top, toprank, pick):
                c(v.tensor_reduce(top, grid(x), AX, ALU.max))
                c(v.tensor_tensor(grid(same), grid(x), over(top), ALU.is_equal))
                c(v.tensor_tensor(grid(rank), grid(same), desc, ALU.mult))
                c(v.tensor_reduce(toprank, grid(rank), AX, ALU.max))
                c(v.tensor_tensor(grid(pick), desc, over(toprank), ALU.is_equal))

            choose(logit, best, bestrank, first)
            c(v.scalar_tensor_tensor(rest, first, -1e30, logit, ALU.mult, ALU.add))
            choose(rest, next_, nextrank, second)
            v.tensor_tensor(rs[:, 4, :], best, next_, ALU.subtract).then_inc(s_gap, 1)
            v.tensor_tensor(rb[:, 6, :], first, second, ALU.add).then_inc(s_m12, 1)

            def shared_hidden(g, j):
                dve.wait_ge(s_sg, FC * g + j + 1)
                since(dve, s_sdps, 2 * (g - 1))
                v.tensor_tensor(shid[g // 3 * 2 + g % 3 % 2][:, j, :], sgate[g // 3][:, j, :], bank[2 * j + 1][:, 0:GN], ALU.mult).then_inc(s_shid, 1)

            shared_hidden(0, 0)
            dve.wait_ge(s_rps, 1)
            tot, cum, before, pos, pick = rb[:, 7, :], rb[:, 8, :], rb[:, 9, :], rb[:, 10, :], rb[:, 11, :]
            eg = lambda x: x.rearrange("p (e i) -> p e i", e=NE)
            flip = lambda x: x.rearrange("p (e i) -> p i e", e=NE)
            c(v.tensor_copy(eg(tot), bank[7][0:TT, 256:256 + BT * NE].rearrange("p (i e) -> p e i", e=NE)))
            c(v.tensor_tensor_scan(cum, fresh, tot, 0.0, ALU.mult, ALU.add))
            c(v.tensor_tensor(before, cum, tot, ALU.subtract))
            c(v.tensor_scalar(r8i[:, 0, :], eg(cum)[:, :, BT - 1], float(SLOTS - 1), None, ALU.add))
            c(v.tensor_scalar(r8i[:, 1, :], r8i[:, 0, :], 7, None, ALU.arith_shift_right))
            c(v.tensor_copy(r8[:, 0, :], r8i[:, 1, :]))
            c(v.tensor_tensor_scan(r8[:, 1, :], ones[0:TT, 0:NE], r8[:, 0, :], 0.0, ALU.mult, ALU.add))
            c(v.tensor_tensor(r8[:, 2, :], r8[:, 1, :], r8[:, 0, :], ALU.subtract))
            c(v.tensor_scalar(r8[:, 3, :], r8[:, 2, :], float(SLOTS), None, ALU.mult))
            c(v.tensor_tensor(eg(before), eg(before), r8[:, 3, :].unsqueeze(2).to_broadcast([TT, NE, BT]), ALU.add))
            c(v.tensor_tensor(grid(pos), grid(bank[7][0:TT, 0:BT * NE]), flip(before), ALU.add))
            for k, choice in enumerate((first, second)):
                c(v.tensor_tensor(pick, choice, pos, ALU.mult))
                c(v.tensor_reduce(slotf[:, k, :], grid(pick), AX, ALU.add))
            v.tensor_copy(slot[:, :, :], slotf[:, :, :]).then_inc(s_slot, 1)
            shared_hidden(0, 1)
            c(v.tensor_tensor(texp[:, :].rearrange("p (j e) -> p j e", e=NE), tileno,
                              r8[:, 1:2, :].to_broadcast([TT, RT, NE]), ALU.is_ge))
            c(v.tensor_reduce(texpf[:, :], texp[:, :].rearrange("p (j e) -> p j e", e=NE), AX, ALU.add))
            v.tensor_scalar(texpi[:, :], texpf[:, :], float(NE - 1), None, ALU.min).then_inc(s_texp, 1)
            shared_hidden(0, 2)
            dve.wait_ge(s_gw, 1)
            c.add(v.tensor_scalar(gatew[:, 0, :], rs[:, 5, :], 0.5, 0.5, ALU.mult, ALU.add))
            c(v.tensor_scalar(gatew[:, 1, :], rs[:, 5, :], -0.5, 0.5, ALU.mult, ALU.add))

            def shared_add(g):
                for q in range(2):
                    dve.wait_ge(s_sdps, 2 * g + q + 1)
                    hb = h[:, (2 * g + q) * NT * D:(2 * g + q + 1) * NT * D]
                    v.tensor_tensor(hb, hb, bank[6 + q][0:TT, :], ALU.add).then_inc(s_hsh, 1)

            def expert_low(n):
                dve.wait_ge(s_eround, n + 1)
                v.tensor_tensor(PIECES[n][1][:, :, 1], PIECES[n][0], etmp[n % 2], ALU.subtract).then_inc(s_elow, 1)

            for n in range(4):
                expert_low(n)
            for g in range(1, GR - 1):
                for j in range(FC):
                    shared_hidden(g, j)
                for n in range(4 * g, 4 * g + 4):
                    expert_low(n)
                    if n % 4 == 0:
                        shared_add(g - 1)
            shared_add(GR - 2)

            def x_turned(j, p):
                dve.wait_ge(s_xgT, j + 1)
                v.tensor_tensor(xgTp[p][:, 1, :, :].rearrange("p c n -> p (c n)"), bank[0][:, 0:D],
                                xgTp[p][:, 0, :, :].rearrange("p c n -> p (c n)"), ALU.subtract).then_inc(s_xgTp, 1)

            def hidden(j, p):
                dve.wait_ge(s_rg, j + 1)
                since(dve, s_rhTps, j - 1)
                v.tensor_tensor(rh[p][:, :], rg[:, :], bank[2 + 2 * p][:, 0:HALF], ALU.mult).then_inc(s_rh, 1)

            def hidden_turned(j, p):
                dve.wait_ge(s_rhT, j + 1)
                v.tensor_tensor(rhTp[p][:, 1, :, :].rearrange("p k n -> p (k n)"), bank[5][:, 0:FC * P],
                                rhTp[p][:, 0, :, :].rearrange("p k n -> p (k n)"), ALU.subtract).then_inc(s_rhTp, 1)

            def lowered(j, p):
                dve.wait_ge(s_rdps, j + 1)
                since(dve, s_yst[p], 8 * (j - p))
                v.tensor_copy(ry[p][:, :], bank[6][:, 0:D]).then_inc(s_ry, 1)

            x_turned(0, 0)
            x_turned(1, 1)
            hidden(0, 0)
            x_turned(2, 0)
            hidden(1, 1)
            hidden_turned(0, 0)

            def tile_step(j, p):
                x_turned(j + 1, 1 - p)
                hidden(j, p)
                hidden_turned(j - 1, 1 - p)
                lowered(j - 2, p)

            for j in range(2, 7):
                tile_step(j, j % 2)
            with dve.Fori(1, RT // 4 - 1) as i:
                for n in range(4):
                    tile_step(4 * i + 3 + n, (3 + n) % 2)
            hidden(RT - 1, 1)
            hidden_turned(RT - 2, 0)
            lowered(RT - 3, 1)
            hidden_turned(RT - 1, 1)
            lowered(RT - 2, 0)
            lowered(RT - 1, 1)
            for j in range(FC):
                shared_hidden(GR - 1, j)

            def stats(b, chain, done, st_, mv_, src):
                c = Chain(dve, chain, 4 * (B + b))
                ht = htile(b)
                dve.wait_ge(src, b + 1)
                settle()
                for t in range(NT):
                    c.add(v.bn_stats(st_[:, 6 * t:6 * t + 6], ht[:, t, :]))
                c.wait()
                settle()
                c.add(v.bn_aggr(mv_[:, 0, :], st_[:, 0:6]))
                v.bn_aggr(mv_[:, 1, :], st_[:, 6:12]).then_inc(done, 1)
                c.step(3)

            def normed(b, chain, done, mv_, rstd_, dst):
                c = Chain(dve, chain, 4 * (B + b) + 3)
                ht = htile(b)
                c.add(v.tensor_scalar(dst[:, 0, :], ht[:, 0, :], mv_[:, 0, 0:1], rstd_[:, 0:1], ALU.subtract, ALU.mult))
                v.tensor_scalar(dst[:, 1, :], ht[:, 1, :], mv_[:, 1, 0:1], rstd_[:, 1:2], ALU.subtract, ALU.mult).then_inc(done, 1)

            def values1(b, p):
                dve.wait_ge(s_v1ps, b + 1)
                since(dve, s_pv1, 2 * (b - 1))
                for par in range(2):
                    src = bank[3][0:TT, :].rearrange("p (i j d) -> p i j d", j=2, d=HD)
                    dst = vz[p][par][0:TT, :, :, :, :].rearrange("p t i j d -> p (t i) j d")
                    for t in range(NT):
                        ins = v.tensor_tensor(dst[:, 8 * t:8 * t + 8, par, :], src[:, 8 * t:8 * t + 8, par, :],
                                              rows1[:, 0, :].rearrange("p (i j d) -> p i j d", j=2, d=HD)[:, :, par, :], ALU.add)
                ins.then_inc(s_v1, 1)

            def least(b, u):
                half, t, n, w = UNITS1[u]
                dve.wait_ge(s_sps, NU1 * b + u + 1)
                since(dve, s_ptps, NU1 * b + u - 3)
                settle()
                for i in range(w):
                    col = t * HEADS + half * HH + n + i
                    ins = v.tensor_tensor_reduce(out=ring[u % 4][0:TT, i, :], in0=bank[4 + u % 2][0:TT, i * T:(i + 1) * T],
                                                 in1=fade[t][:, half * HH + n + i, :], scale=1.0, scalar=3e38,
                                                 op0=ALU.add, op1=ALU.min, accum_out=mn[:, col:col + 1])
                ins.then_inc(s_min, 1)

            def probs_turned(b, u):
                if u % 2:
                    return
                half, t, n, w = UNITS1[u]
                dve.wait_ge(s_ptps, NU1 * b + u + 1)
                if u % (NU1 // 2) == 0:
                    since(dve, s_pv1, 2 * b + half - 1)
                v.tensor_copy(pT[half][0:TT, :, n:n + w, t * TT:(t + 1) * TT],
                              bank[6 + u % 2][0:TT, 0:NT * w * TT].rearrange("p (k h q) -> p k h q", k=NT, h=w)).then_inc(s_pt[0], 1)

            def routed4(b):
                dve.wait_ge(s_lg4ps, b + 1)
                v.tensor_scalar(lg[:, bass.ds(b * (NT * NE), NT * NE)], bank[0][0:TT, 0:NT * NE], 1.0, None, ALU.mult).then_inc(s_lg4, 1)

            def turned1(b):
                dve.wait_ge(s_xT1, b + 1)
                v.tensor_tensor(xnTp[:, 1, :, :].rearrange("p c t -> p (c t)"), bank[0][:, 0:KC * T],
                                xnTp[:, 0, :, :].rearrange("p c t -> p (c t)"), ALU.subtract).then_inc(s_xTp1, 1)

            def sums1(b, p):
                dve.wait_ge(s_p, NU1 * (b + 1))
                v.reciprocal(rinv[:, :, :].rearrange("p t h -> p (t h)"), rsum[p][:, :]).then_inc(s_rinv, 1)
                dve.wait_ge(s_rinv, b + 1)
                since(dve, s_rbps, b)
                v.tensor_copy(rspread[0:TT, :, :].rearrange("p t (h d) -> p (t h) d", d=HD),
                              rinv[:, :, :].rearrange("p t h -> p (t h)").unsqueeze(2).to_broadcast([TT, NT * HEADS, HD])).then_inc(s_rspread, 1)

            def mixed1(b):
                dve.wait_ge(s_rbs, b + 1)
                dve.wait_ge(s_pv1, 2 * b + 2)
                since(dve, s_o1ps, b)
                v.tensor_tensor(yT[:, :, :].rearrange("p c t -> p (c t)"), bank[1][:, 0:KC * T],
                                rbs[:, :, :].rearrange("p c t -> p (c t)"), ALU.mult).then_inc(s_y1, 1)

            def residual1(b):
                dve.wait_ge(s_o1ps, b + 1)
                dve.wait_ge(s_hb, b + 1)
                hb = h[:, bass.ds(b * (NT * D), NT * D)]
                v.tensor_tensor(hb, hb, bank[3][0:TT, :], ALU.add).then_inc(s_h3, 1)
                stats(b, vch2, s_mv4, st2, mv2, s_h3)

            def normed4(b):
                dve.wait_ge(s_rstd4, b + 1)
                since(dve, s_x4Tps, b)
                normed(b, vch2, s_x4, mv2, rstd2, x2s)

            def step1(b, p, first=False, second=False, final=False):
                for u in range(NU1):
                    if u >= 3:
                        probs_turned(b, u - 3)
                    elif not first:
                        probs_turned(b - 1, NU1 - 3 + u)
                    least(b, u)
                    if not final:
                        if u == 2:
                            stats(b + 1, nch, s_mv1, st, mv, s_comb)
                        elif u == 3:
                            dve.wait_ge(s_rstd1, b + 2)
                            since(dve, s_xT1ps, b + 1)
                            normed(b + 1, nch, s_xn1, mv, rstd, xn)
                        elif u == 5:
                            turned1(b + 1)
                    if not first:
                        if u == 2:
                            sums1(b - 1, 1 - p)
                        elif u == 3:
                            values1(b, p)
                        elif u == 6:
                            mixed1(b - 1)
                        elif u == 9:
                            residual1(b - 1)
                        elif u == 11:
                            normed4(b - 1)
                    if u == 2 and not (first or second):
                        routed4(b - 2)

            dve.wait_ge(s_fade, 2)
            dve.wait_ge(s_yg[0], 16 * NT * TOPK)
            for k in range(TOPK):
                for t in range(NT):
                    hb = h[:, t * D:(t + 1) * D]
                    ins = v.scalar_tensor_tensor(hb, yg[0][:, t, k, :], gatew[:, k, t:t + 1], hb, ALU.mult, ALU.add)
                    if k == 0 or t == 0:
                        c.add(ins)
                    else:
                        ins.then_inc(s_comb, 1)
                if k == 0:
                    c.wait()
            stats(0, nch, s_mv1, st, mv, s_comb)
            dve.wait_ge(s_rstd1, 1)
            normed(0, nch, s_xn1, mv, rstd, xn)
            shared_add(GR - 1)
            turned1(0)
            dve.wait_ge(s_k1, 1)
            for half in range(KC):
                v.tensor_tensor(kb[0][:, half, :, :], ksb1[:, half:half + 1, :].to_broadcast([P, HH, T]),
                                hmask[:, :].unsqueeze(2).to_broadcast([P, HH, T]), ALU.mult).then_inc(s_kb, 1)
            values1(0, 0)
            step1(0, 0, first=True)
            step1(1, 1, second=True)
            step1(2, 0)
            with dve.Fori(1, B // 2 - 1) as i:
                step1(2 * i + 1, 1)
                step1(2 * i + 2, 0)
            step1(B - 1, 1, final=True)
            sums1(B - 1, 1)
            probs_turned(B - 1, NU1 - 2)
            routed4(B - 2)
            mixed1(B - 1)
            residual1(B - 1)
            normed4(B - 1)
            routed4(B - 1)

            dve.wait_ge(s_lg4, B)
            x, e1, pr = rb[:, 0, :], rb[:, 1, :], rb[:, 5, :]
            c(v.tensor_reduce(rs[:, 0, :], grid(lg[:, :]), AX, ALU.max))
            v.tensor_tensor(grid(x), grid(lg[:, :]), over(rs[:, 0, :]), ALU.subtract).then_inc(s_rx, 1)
            dve.wait_ge(s_comb, B)

            def rests(g):
                for j in range(FFC):
                    n = FFC * g + j
                    dve.wait_ge(s_gelu, n + 1)
                    if j % 2:
                        c(v.tensor_copy(hidp[g % 2][:, 0, j, :], hid32[n % 2]))
                    v.tensor_tensor(hidp[g % 2][:, 1, j, :], hid32[n % 2], hidp[g % 2][:, 0, j, :], ALU.subtract).then_inc(s_hid, 1)

            rests(0)
            rests(1)
            dve.wait_ge(s_rexp, 1)
            c(v.tensor_reduce(rs[:, 1, :], grid(e1), AX, ALU.add))
            c(v.reciprocal(rs[:, 2, :], rs[:, 1, :]))
            c(v.tensor_tensor(grid(pr), grid(e1), over(rs[:, 2, :]), ALU.mult))
            top1, top2 = rs[:, 4, :], rs[:, 6, :]
            choose(pr, top1, rs[:, 3, :], rb[:, 2, :])
            c(v.scalar_tensor_tensor(rb[:, 3, :], rb[:, 2, :], -1e30, pr, ALU.mult, ALU.add))
            c(v.tensor_reduce(top2, grid(rb[:, 3, :]), AX, ALU.max))
            c(v.tensor_tensor(rs[:, 1, :], top1, top2, ALU.add))
            c(v.reciprocal(rs[:, 2, :], rs[:, 1, :]))
            c(v.tensor_tensor(rs[:, 0, :], top1, rs[:, 2, :], ALU.mult))
            c(v.tensor_tensor(rs[:, 3, :], top2, rs[:, 2, :], ALU.mult))
            c(v.tensor_tensor(cs[:, :], rs[:, 0, :], rs[:, 3, :], ALU.add))

            for g in range(GR):
                for o in range(KC):
                    dve.wait_ge(s_fdps, KC * g + o + 1)
                    since(dve, s_fyps, 2 * (g - 1))
                    v.tensor_scalar(ffT[g % 2][:, o, :], bank[4 + o][:, 0:GN], b2c[:, o:o + 1], None, ALU.add).then_inc(s_ft, 1)
                if g + 2 < GR:
                    rests(g + 2)
                for q in range(2):
                    b = 2 * g + q
                    dve.wait_ge(s_fyps, b + 1)
                    for t in range(NT):
                        i = NT * b + t
                        hb = h[:, i * D:(i + 1) * D]
                        ins = v.scalar_tensor_tensor(hb, bank[6 + q][0:TT, t * D:(t + 1) * D], cs[:, i:i + 1], hb, ALU.mult, ALU.add)
                        if t == 0:
                            c.add(ins)
                        else:
                            c.wait()
                            ins.then_inc(s_h4, 1)

        @block.gpsimd
        def _(pool):
            g = nc.gpsimd
            g.memset(EPSC[:, :], EPS).then_inc(gch, 1)
            for i in range(2):
                g.memset(asb[i][:, :, :, :], 0.0).then_inc(gch, 1)
                for par in range(2):
                    g.memset(vz[i][par][:, :, :, :, :], 0.0).then_inc(gch, 1)
            g.memset(zero[:, :], 0.0).then_inc(s_zset, 1)
            pool.wait_ge(s_const, 48)

            def keys(b, p):
                c = Chain(pool, gch, 7 + 6 * b)
                pool.wait_ge(s_G, b + 1)
                since(pool, s_ek, b)
                for r in range(NCH):
                    n = CH * (r + 1)
                    m = CH * r + MIDC
                    ins = g.tensor_tensor(dk[:, :, COFF[r]:COFF[r] + n], G[:, :, m:m + 1].to_broadcast([P, KC, n]),
                                          G[:, :, 0:n], ALU.subtract)
                    if r < NCH - 1:
                        c.add(ins)
                ins.then_inc(s_dk, 1)
                pool.wait_ge(s_ek, b + 1)
                pool.wait_ge(s_ksb, b + 1)
                since(pool, s_aps, 12 * (b - 1))
                for r in range(NCH):
                    n = CH * (r + 1)
                    ins = g.tensor_tensor(kr[p][:, :, COFF[r]:COFF[r] + n], ek[:, :, COFF[r]:COFF[r] + n],
                                          ksb[:, :, 0:n], ALU.mult)
                    if r < NCH - 1:
                        c.add(ins)
                ins.then_inc(s_kr, 1)
                pool.wait_ge(s_qe, b + 1)
                g.tensor_tensor(qb[p][:, 1, :, :], qe[:, 1:2, :].to_broadcast([P, HH, T]),
                                hmask[:, :].unsqueeze(2).to_broadcast([P, HH, T]), ALU.mult).then_inc(s_qb1, 1)
                c.step(6)

            keys(0, 0)
            keys(1, 1)
            with pool.Fori(1, B // 2) as i:
                keys(2 * i, 0)
                keys(2 * i + 1, 1)

            pool.wait_ge(s_zdone, 16 * (RT // 4))
            pool.wait_ge(s_x2all, 16 * B)
            pool.wait_ge(s_slot, 1)
            for i in range(BT):
                for k in range(TOPK):
                    g.indirect_dma_start(xs_dram, bass.IndirectOffsetOnAxis(ap=slot[:, k, i:i + 1], axis=0),
                                         x2[:, i * D:(i + 1) * D], None).then_inc(s_scat, 16)
            pool.wait_ge(s_hsh, 2 * (GR - 1))
            pool.wait_ge(s_alpha, 1)
            pool.wait_ge(s_l1c, 16 * 7)
            for t in range(NT):
                g.tensor_tensor(fade[t], dist[:, t:t + 1, :].to_broadcast([TT, HEADS, T]),
                                alpha[:, :].unsqueeze(2).to_broadcast([TT, HEADS, T]), ALU.mult).then_inc(s_fade, 1)

            def gather(b):
                for t in range(NT):
                    for k in range(TOPK):
                        g.indirect_dma_start(yg[b % 2][:, t, k, :], None, ys_dram,
                                             bass.IndirectOffsetOnAxis(ap=slot[:, k, NT * b + t:NT * b + t + 1], axis=0)
                                             ).then_inc(s_yg[b % 2], 16)

            def combine(b):
                c = Chain(pool, cch, 5 * (b - 1))
                if b == 2 * (GR - 1):
                    pool.wait_ge(s_hsh, 2 * GR)
                pool.wait_ge(s_yg[b % 2], 16 * NT * TOPK * (b // 2 + 1))
                rows = yg[b % 2]
                for t in range(NT):
                    for k in range(TOPK):
                        i = NT * b + t
                        c.add(g.tensor_scalar(rows[:, t, k, :], rows[:, t, k, :], gatew[:, k, i:i + 1], None, ALU.mult))
                c.wait()
                hb = h[:, b * NT * D:(b + 1) * NT * D].rearrange("p (t d) -> p t d", t=NT)
                c(g.tensor_tensor(hb, hb, rows[:, :, 0, :], ALU.add))
                g.tensor_tensor(hb, hb, rows[:, :, 1, :], ALU.add).then_inc(s_comb, 1)
                c.step(5)

            pool.wait_ge(s_wff, 32)
            pool.wait_ge(s_w1in, 64)
            pool.wait_ge(s_fade, 2)
            c = Chain(pool, gch, 7 + 6 * B)
            for i in range(WSPLIT):
                part = slice(i * WN, (i + 1) * WN)
                c(g.tensor_copy(wtmp, x2w[:, part]))
                c(g.tensor_tensor(wparts[:, part, 1], x2w[:, part], wtmp, ALU.subtract))
                c(g.tensor_copy(wparts[:, part, 0], wtmp))
            tmp = wtmp[:, 0:KC * D].rearrange("p (c n) -> p c n", c=KC)
            for w, parts in ((wq, wqp), (wk, wkp), (wv, wvp)):
                c(g.tensor_copy(tmp, w[:, :, :]))
                c(g.tensor_tensor(parts[:, :, :, 1], w[:, :, :], tmp, ALU.subtract))
                c(g.tensor_copy(parts[:, :, :, 0], tmp))
            pool.sem_inc(s_wsplit, 1)
            for p in range(2):
                pool.wait_ge(s_yst[p], 16 * (RT // 2))
            gather(0)
            gather(1)
            pool.wait_ge(s_comb, 1)
            for half in range(2):
                g.memset(pT[half][64:P, :, :, :], 0.0).then_inc(s_pz, 1)
            pool.wait_ge(s_pz, 2)
            for b in range(B):
                p = b % 2
                if b + 1 < B:
                    combine(b + 1)
                pool.wait_ge(s_k1, b + 1)
                since(pool, s_sps, NU1 * (b - 1))
                for half in range(KC if b else 0):
                    g.tensor_tensor(kb[p][:, half, :, :], ksb1[:, half:half + 1, :].to_broadcast([P, HH, T]),
                                    hmask[:, :].unsqueeze(2).to_broadcast([P, HH, T]), ALU.mult).then_inc(s_kb, 1)
                hb = h[:, b * NT * D:(b + 1) * NT * D].rearrange("p (t d) -> p t d", t=NT)
                pool.wait_ge(s_xn1, b + 1)
                g.tensor_tensor(hb, hb, rows1[:, 1:2, :].to_broadcast([TT, NT, D]), ALU.add).then_inc(s_hb, 1)
                if b + 2 < B:
                    pool.wait_ge(s_comb, b + 1)
                    gather(b + 2)
            pool.wait_ge(s_comb, B)
            c = Chain(pool, gch, 7 + 6 * B + 3 * (WSPLIT + 3))
            for grp in range(GR):
                pool.wait_ge(s_x4Tall, 16 * GN // T * (grp + 1))
                since(pool, s_fups, FFC * (grp - 1))
                x = x2T[:, :, grp * GN:(grp + 1) * GN]
                c(g.tensor_copy(xpart[grp % 2][:, 0, :, :], x))
                g.tensor_tensor(xpart[grp % 2][:, 1, :, :], x, xpart[grp % 2][:, 0, :, :], ALU.subtract).then_inc(s_xpart, 1)


def laid_out(inputs):
    import numpy as np
    f = {k: np.asarray(v) for k, v in inputs.items()}

    def rows(w):
        return np.ascontiguousarray(w.reshape(-1, P, w.shape[-1]).transpose(1, 0, 2))

    def column(v, rep=1):
        return np.ascontiguousarray(np.repeat(v, rep).reshape(-1, P).T)

    o = {}
    x = f["x"].reshape(B, 3, 6, 16, 6, 16).transpose(0, 1, 3, 5, 2, 4).reshape(B * IMG, PC * P)
    o["patches"] = rows(x.T)
    o["tok_w"] = rows(f["L0_tok_W"])
    o["txt"] = f["txt"]
    o["ident"] = np.eye(P, dtype=np.float32)
    o["hmask"] = (np.arange(P)[:, None] // HD == np.arange(HH)[None]).astype(np.float32)
    k, q = np.arange(TT)[:, None, None], np.arange(CH)[None, None]
    o["cmask"] = (k <= q + CH * np.arange(2)[None, :, None]).astype(np.int32)
    for n, s in (("wq", "q_w"), ("wk", "k_w"), ("wv", "v_w"), ("wo", "o_w"), ("cw1", "cs_w1")):
        o[n] = rows(f["L0_attn_" + s].T)
    o["cb1"] = f["L0_attn_cs_b1"].reshape(64, 1)
    o["cw2"] = np.ascontiguousarray(np.repeat(f["L0_attn_cs_w2"].T, HD, axis=1))
    o["cb2"] = column(f["L0_attn_cs_b2"], HD)
    o["dec"] = column(f["L0_attn_decay_params"].reshape(-1))
    up = f["L0_ffn_w_up"].transpose(2, 0, 1)
    o["eup"] = rows(up.reshape(D, NE * 2 * HALF))
    o["edn"] = rows(f["L0_ffn_w_down"].transpose(2, 0, 1).reshape(HALF, NE * D))
    o["sup"] = rows(np.concatenate([f["L0_ffn_sg_gate"].T, f["L0_ffn_sg_up"].T], axis=1))
    o["sdn"] = rows(f["L0_ffn_sg_down"].T)
    o["gw"] = rows(f["L0_ffn_gate_w"].T)
    o["tri"] = np.triu(np.ones((TT, TT), np.float32), 1)
    o["rc"] = np.ascontiguousarray(np.broadcast_to(np.concatenate([
        np.tile(NE - np.arange(NE), BT), np.tile(np.arange(BT) > 0, NE),
        np.repeat(np.arange(RT), NE)]).astype(np.float32), (TT, 2 * BT * NE + RT * NE)))
    qkv = f["L1_attn_qkv_w"].T
    for n, w in (("wq1", qkv[:, 0:D]), ("wk1", qkv[:, D:2 * D]), ("wv1", qkv[:, 2 * D:]), ("wo1", f["L1_attn_out_w"].T),
                 ("rw", f["L1_ffn_router_w"]), ("w1", f["L1_ffn_w1"]), ("w2", f["L1_ffn_w2"])):
        o[n] = rows(w)
    qkv_b = f["L1_attn_qkv_b"]
    o["qkb"] = np.ascontiguousarray(np.stack([column(qkv_b[0:D]), column(qkv_b[D:2 * D])], axis=1))
    o["b1"] = column(f["L1_ffn_b1"])
    o["rows1"] = np.ascontiguousarray(np.broadcast_to(
        np.stack([qkv_b[2 * D:], f["L1_attn_out_b"]]), (TT, 2, D)))
    o["b2"] = column(f["L1_ffn_b2"])
    o["alpha"] = np.ascontiguousarray(np.broadcast_to(f["L1_attn_decay_alpha"], (TT, HEADS)))
    pos = np.arange(T, dtype=np.float32)
    o["dist"] = np.ascontiguousarray(np.abs(pos.reshape(NT, TT, 1) - pos).transpose(1, 0, 2))
    return o


OUT_SHAPE = (B, T, D)


def kernel(**inputs):
    import numpy as np
    import concourse.bacc as bacc
    from concourse.bass_utils import run_bass_kernel_spmd

    nc = bacc.Bacc("TRN2", target_bir_lowering=False, num_devices=1)
    arrays = laid_out(inputs)
    aps = {n: nc.dram_tensor("in_" + n, x.shape, mybir.dt.from_np(x.dtype), kind="ExternalInput").ap()
           for n, x in arrays.items()}
    out = nc.dram_tensor("out", OUT_SHAPE, mybir.dt.float32, kind="ExternalOutput").ap()
    early_fusion_kernel(nc, aps, out)
    r = run_bass_kernel_spmd(nc, [{"in_" + n: x for n, x in arrays.items()}], core_ids=[0])
    return r.results[0]["out"]
```
